# Optimizing a Trainium2 kernel written in Bass

```python
import numpy as np
import jax
import jax.numpy as jnp

def _softmax(x, axis=-1):
    return jax.nn.softmax(x, axis=axis)

def _gelu(x):
    return jax.nn.gelu(x, approximate=True)

def _silu(x):
    return jax.nn.silu(x)

def _sigmoid(x):
    return jax.nn.sigmoid(x)

def _layernorm(x, axis=-1, eps=1e-05):
    m = jnp.mean(x, axis=axis, keepdims=True)
    v = jnp.var(x, axis=axis, keepdims=True)
    return (x - m) / jnp.sqrt(v + eps)

def _scatter_add(tgt, idx, src, axis=0):
    return tgt.at[idx].add(src)

def _segment_sum(src, seg, n):
    return jax.ops.segment_sum(src, seg, n)
kernel_name = 'mk_gnn_resnorm_d2_gnn_r8_6a9ec3'

def setup_inputs(seed: int=0):
    np.random.seed(seed)
    _w = jnp.asarray

    def _rec_inputs():
        import jax
        import jax.numpy as jnp
        _gk = jax.random.key(seed)
        x = -0.000202 + 1 * jax.random.normal(jax.random.fold_in(_gk, 1), (6250, 128), jnp.float32)
        src = jax.random.randint(jax.random.fold_in(_gk, 2), (100000,), 0, 6250, jnp.int32)
        dst = jnp.minimum((6250 * jax.random.uniform(jax.random.fold_in(_gk, 3), (100000,)) ** 2.0).astype(jnp.int32), 49999)
        _o = jnp.argsort(dst, stable=True)
        src = src[_o]
        dst = dst[_o]
        edge_attr_2 = 0.000279007 + 1.00013 * jax.random.normal(jax.random.fold_in(_gk, 11), (100000, 2), jnp.float32)
        edge_attr_8 = 0.000398945 + 1.00003 * jax.random.normal(jax.random.fold_in(_gk, 12), (100000, 8), jnp.float32)
        return (x, src, dst, edge_attr_2, edge_attr_8)
    x, src, dst, edge_attr_2, edge_attr_8 = _rec_inputs()

    def _L0_gnn_setup():
        import jax, jax.numpy as jnp
        import numpy as np
        N = 6250
        E = 100000
        F = 128
        H = 8
        D = F // H
        key = jax.random.key(seed)
        ks = jax.random.split(key, 12)
        s = 0.02
        return {'node_features': jax.random.normal(ks[0], (N, F), dtype=jnp.float32), 'edge_index': jax.random.randint(ks[1], (2, E), 0, N, dtype=jnp.int32), 'attention_mask': jax.random.normal(ks[2], (E, H), dtype=jnp.float32), 'Wq': jax.random.normal(ks[3], (F, F), dtype=jnp.float32) * s, 'bq': jnp.zeros((F,), dtype=jnp.float32), 'Wk': jax.random.normal(ks[4], (F, F), dtype=jnp.float32) * s, 'bk': jnp.zeros((F,), dtype=jnp.float32), 'Wv': jax.random.normal(ks[5], (F, F), dtype=jnp.float32) * s, 'bv': jnp.zeros((F,), dtype=jnp.float32), 'Wo': jax.random.normal(ks[6], (F, F), dtype=jnp.float32) * s, 'bo': jnp.zeros((F,), dtype=jnp.float32)}
    _L0_gnn_all = _L0_gnn_setup()
    _L0_gnn_in = {k: v for k, v in _L0_gnn_all.items() if k in ('Wq', 'bq', 'Wk', 'bk', 'Wv', 'bv', 'Wo', 'bo')}
    del _L0_gnn_all

    def _L1_gnn_setup():
        import jax, jax.numpy as jnp
        import numpy as np
        N_NODES = 6250
        N_EDGES = 75000
        IN_NF = 128
        OUT_NF = 128
        HID = 128
        IN_EF = 2

        def _linear_params(key, fan_in, fan_out):
            kw, kb = jax.random.split(key)
            bound = 1.0 / np.sqrt(fan_in)
            W = jax.random.uniform(kw, (fan_in, fan_out), minval=-bound, maxval=bound, dtype=jnp.float32)
            b = jax.random.uniform(kb, (fan_out,), minval=-bound, maxval=bound, dtype=jnp.float32)
            return (W, b)
        key = jax.random.key(seed)
        ks = jax.random.split(key, 8)
        x = jax.random.normal(ks[0], (N_NODES, IN_NF), dtype=jnp.float32)
        edge_features = jax.random.normal(ks[1], (N_EDGES, IN_EF), dtype=jnp.float32)
        edge_idx = jax.random.randint(ks[2], (2, N_EDGES), 0, N_NODES, dtype=jnp.int64 if jax.config.jax_enable_x64 else jnp.int32)
        eW1, eb1 = _linear_params(ks[3], IN_NF * 2 + IN_EF, HID)
        eW2, eb2 = _linear_params(ks[4], HID, HID)
        nW1, nb1 = _linear_params(ks[5], HID + IN_NF, HID)
        nW2, nb2 = _linear_params(ks[6], HID, OUT_NF)
        return {'x': x, 'edge_features': edge_features, 'edge_idx': edge_idx, 'eW1': eW1, 'eb1': eb1, 'eW2': eW2, 'eb2': eb2, 'nW1': nW1, 'nb1': nb1, 'nW2': nW2, 'nb2': nb2}
    _L1_gnn_all = _L1_gnn_setup()
    _L1_gnn_in = {k: v for k, v in _L1_gnn_all.items() if k in ('eW1', 'eb1', 'eW2', 'eb2', 'nW1', 'nb1', 'nW2', 'nb2')}
    del _L1_gnn_all
    return {'x': x, 'src': src, 'dst': dst, 'edge_attr_2': edge_attr_2, 'edge_attr_8': edge_attr_8, 'L0_gnn_Wq': _L0_gnn_in['Wq'], 'L0_gnn_bq': _L0_gnn_in['bq'], 'L0_gnn_Wk': _L0_gnn_in['Wk'], 'L0_gnn_bk': _L0_gnn_in['bk'], 'L0_gnn_Wv': _L0_gnn_in['Wv'], 'L0_gnn_bv': _L0_gnn_in['bv'], 'L0_gnn_Wo': _L0_gnn_in['Wo'], 'L0_gnn_bo': _L0_gnn_in['bo'], 'L1_gnn_eW1': _L1_gnn_in['eW1'], 'L1_gnn_eb1': _L1_gnn_in['eb1'], 'L1_gnn_eW2': _L1_gnn_in['eW2'], 'L1_gnn_eb2': _L1_gnn_in['eb2'], 'L1_gnn_nW1': _L1_gnn_in['nW1'], 'L1_gnn_nb1': _L1_gnn_in['nb1'], 'L1_gnn_nW2': _L1_gnn_in['nW2'], 'L1_gnn_nb2': _L1_gnn_in['nb2']}

def reference(x, src, dst, edge_attr_2, edge_attr_8, L0_gnn_Wq, L0_gnn_bq, L0_gnn_Wk, L0_gnn_bk, L0_gnn_Wv, L0_gnn_bv, L0_gnn_Wo, L0_gnn_bo, L1_gnn_eW1, L1_gnn_eb1, L1_gnn_eW2, L1_gnn_eb2, L1_gnn_nW1, L1_gnn_nb1, L1_gnn_nW2, L1_gnn_nb2):
    import jax
    import jax.numpy as jnp

    def _L0_gnn_ref(node_features, edge_index, attention_mask, Wq, bq, Wk, bk, Wv, bv, Wo, bo):
        import jax, jax.numpy as jnp
        import numpy as np
        N = 6250
        E = 100000
        F = 128
        H = 8
        D = F // H
        src, dest = (edge_index[0], edge_index[1])
        q = (node_features @ Wq.T + bq).reshape(N, H, D)
        k = (node_features @ Wk.T + bk).reshape(N, H, D)
        v = (node_features @ Wv.T + bv).reshape(N, H, D)
        scores = jnp.sum(q[src] * k[dest], axis=-1) / jnp.sqrt(jnp.float32(D))
        scores = scores + attention_mask
        seg_max = jax.ops.segment_max(scores, src, num_segments=N)
        ex = jnp.exp(scores - seg_max[src])
        seg_sum = jax.ops.segment_sum(ex, src, num_segments=N)
        weights = ex / seg_sum[src]
        weighted = v[src] * weights[:, :, None]
        out = jax.ops.segment_sum(weighted, dest, num_segments=N)
        out = out.reshape(N, F)
        return out @ Wo.T + bo

    def _L1_gnn_ref(x, edge_features, edge_idx, eW1, eb1, eW2, eb2, nW1, nb1, nW2, nb2):
        import jax, jax.numpy as jnp
        import numpy as np
        N_NODES = 6250
        N_EDGES = 75000
        IN_NF = 128
        OUT_NF = 128
        HID = 128
        IN_EF = 2

        def _linear_params(key, fan_in, fan_out):
            kw, kb = jax.random.split(key)
            bound = 1.0 / np.sqrt(fan_in)
            W = jax.random.uniform(kw, (fan_in, fan_out), minval=-bound, maxval=bound, dtype=jnp.float32)
            b = jax.random.uniform(kb, (fan_out,), minval=-bound, maxval=bound, dtype=jnp.float32)
            return (W, b)
        row, col = (edge_idx[0], edge_idx[1])
        edge_in = jnp.concatenate([x[row], x[col], edge_features], axis=-1)
        h = jax.nn.silu(edge_in @ eW1 + eb1)
        edge_feat = jax.nn.silu(h @ eW2 + eb2)
        agg = jax.ops.segment_sum(edge_feat, row, num_segments=x.shape[0])
        node_in = jnp.concatenate([x, agg], axis=-1)
        out = jax.nn.silu(node_in @ nW1 + nb1) @ nW2 + nb2
        return out
    edge_index = jnp.stack([src, dst])
    x = _layernorm(x + _L0_gnn_ref(x, edge_index, edge_attr_8, L0_gnn_Wq, L0_gnn_bq, L0_gnn_Wk, L0_gnn_bk, L0_gnn_Wv, L0_gnn_bv, L0_gnn_Wo, L0_gnn_bo), axis=-1)
    x = _layernorm(x + _L1_gnn_ref(x, edge_attr_2, edge_index, L1_gnn_eW1, L1_gnn_eb1, L1_gnn_eW2, L1_gnn_eb2, L1_gnn_nW1, L1_gnn_nb1, L1_gnn_nW2, L1_gnn_nb2), axis=-1)
    return x

_drawn_inputs = setup_inputs


def setup_inputs(seed=0):
    import zlib

    import numpy as np

    out = dict(_drawn_inputs(seed))
    spreads = {'L0_gnn_bq': (0.0, 0.8),
     'L0_gnn_bk': (0.0, 0.8),
     'L0_gnn_bv': (0.0, 0.1),
     'L0_gnn_bo': (0.0, 0.1)}
    factors = {'edge_attr_2': 8.0,
     'edge_attr_8': 3.83,
     'L0_gnn_Wq': 8.0,
     'L0_gnn_Wk': 8.0,
     'L0_gnn_Wv': 3.018,
     'L1_gnn_eb1': 4.234,
     'L1_gnn_nb1': 4.889}
    for name, (base, spread) in spreads.items():
        noise = np.random.default_rng([zlib.crc32(name.encode()), seed]).standard_normal(out[name].shape)
        drawn = base * np.exp(spread * noise) if base else spread * noise
        out[name] = jnp.asarray(drawn.astype(out[name].dtype))
    for name, factor in factors.items():
        out[name] = (out[name] * factor).astype(out[name].dtype)
    return out
```

```python
from contextlib import ExitStack

import concourse.bass as bass
from concourse import mybir

ALU = mybir.AluOpType
ACT = mybir.ActivationFunctionType
AX_X = mybir.AxisListType.X
F32 = mybir.dt.float32
BF16 = mybir.dt.bfloat16
I32 = mybir.dt.int32

P = 128
N = 6250
E = 100000
F = 128
H = 8
D = F // H
NW = -(-N // P)
NP = NW * P
LAST = N - (NW - 1) * P
EL = 125
ET = E // EL
G = 4
NT = -(-(E // P + NW) // (2 * G)) * 2 * G
SLOTS = NT * P
PAIRS = NT // (2 * G)
R = 16
C_ATTR, C_DST, C_SL, C_DL, C_ROW = 8, 10, 11, 12, 13
CW = 132
NOROW = float(1 << 20)
BIG = float(2 ** 100)
EPS = 1e-5
PG = 8
PB = ET // PG
EC = 10
RF = NT // 16
CF = 8


class Ctx:
    pass


def semaphores(nc, stack, names):
    return [stack.enter_context(nc.semaphore(n)) for n in names.split()]


class Epoch(ExitStack):

    def enter_context(self, context):
        got = super().enter_context(context)
        self.taken = [*self.taken, got] if hasattr(self, "taken") else [got]
        return got


def wait_count(eng, sem, count):
    if not isinstance(count, int) or count > 0:
        eng.wait_ge(sem, count)


def constants(c):
    nc, k = c.nc, c.stack
    sb = lambda n, s, d: k.enter_context(nc.sbuf_tensor(n, s, d))
    c.iota = sb("iota", [P, P], F32)
    c.ident = sb("ident", [P, P], F32)
    c.identb = sb("identb", [P, P], BF16)
    c.bigid = sb("bigid", [P, P], BF16)
    c.tri = sb("tri", [P, P], BF16)
    c.ones = sb("ones", [P, P], BF16)
    c.mtab = sb("mtab", [P, NW * H], F32)
    c.dtab = sb("dtab", [P, NW * H], F32)
    c.win = {s: sb("win_" + s, [1, NT], I32) for s in ("src", "dst")}
    (s_set,) = semaphores(nc, c.sems, "const_set")
    with ExitStack() as t:
        ii = t.enter_context(nc.sbuf_tensor("iota_int", [P, P], I32))
        with nc.Block() as block:
            @block.gpsimd
            def _(pool):
                pool.iota(ii[:, :], pattern=[[1, P]], base=0, channel_multiplier=0).then_inc(s_set, 1)
                pool.memset(c.ident[:, :], 0.0).then_inc(s_set, 1)
                pool.memset(c.identb[:, :], 0.0).then_inc(s_set, 1)
                pool.memset(c.bigid[:, :], 0.0).then_inc(s_set, 1)
                pool.memset(c.tri[:, :], 1.0).then_inc(s_set, 1)
                pool.memset(c.ones[:, :], 1.0).then_inc(s_set, 1)
                pool.wait_ge(s_set, 6)
                pool.tensor_copy(c.iota[:, :], ii[:, :])
                for m, v in ((c.ident, 1.0), (c.identb, 1.0), (c.bigid, BIG)):
                    pool.affine_select(out=m[:, :], in_=m[:, :], compare_op=ALU.not_equal, fill=v, base=0,
                                       pattern=[[-1, P]], channel_multiplier=1)
                pool.affine_select(out=c.tri[:, :], in_=c.tri[:, :], compare_op=ALU.is_gt, fill=0.0, base=0,
                                   pattern=[[1, P]], channel_multiplier=-1)


def project(c, a):
    nc = c.nc
    s_w, s_bias, s_x0, s_x1, s_mm0, s_mm1, s_q0, s_q1, s_k0, s_k1 = semaphores(
        nc, c.sems, "w_in bias_in x_in0 x_in1 qkv_ready0 qkv_ready1 qkv_read0 qkv_read1 k_out0 k_out1")
    s_x, s_mm, s_q, s_k = (s_x0, s_x1), (s_mm0, s_mm1), (s_q0, s_q1), (s_k0, s_k1)
    with ExitStack() as t:
        w = t.enter_context(nc.sbuf_tensor("w_qkv", [P, 3 * F], F32))
        bias = t.enter_context(nc.sbuf_tensor("b_qkv", [P, 3 * F], F32))
        xt = t.enter_context(nc.sbuf_tensor("xt", [P, 2, P], F32))
        kt = t.enter_context(nc.sbuf_tensor("k_rows", [P, 2, F], F32))
        ps = [t.enter_context(nc.psum_tensor(f"ps_qkv{b}", [P, 512], F32)) for b in range(2)]
        with nc.Block() as block:
            @block.sync
            def _(sp):
                for j, (m, v) in enumerate((("WqT", "bq"), ("WkT", "bk"), ("WvT", "bv"))):
                    sp.dma_start(w[:, j * F:(j + 1) * F], a[m]).then_inc(s_w, 16)
                    sp.dma_start(bias[:, j * F:(j + 1) * F],
                                 a[v].rearrange("(o n) -> o n", o=1).to_broadcast([P, F])).then_inc(s_bias, 16)

                def load(win, n, cols):
                    sp.dma_start(xt[:, n, 0:cols], a["xT"][:, bass.ds(win * P, cols)]).then_inc(s_x[n], 16)

                def store(win, n, use):
                    sp.wait_ge(s_q[n], 3 * use)
                    sp.dma_start(c.k_dram[bass.ds(win * P, P), :], kt[:, n, :]).then_inc(s_k[n], 16)
                load(0, 0, P)
                load(1, 1, P)
                with sp.Fori(0, NW // 2 - 1) as i:
                    for n in range(2):
                        store(2 * i + n, n, i + 1)
                        load(2 * i + 2 + n, n, P)
                store(NW - 3, 0, NW // 2)
                load(NW - 1, 0, LAST)
                store(NW - 2, 1, NW // 2)
                store(NW - 1, 0, NW // 2 + 1)
                sp.wait_ge(s_k[0], 16 * (NW // 2 + 1))
                sp.wait_ge(s_k[1], 16 * (NW // 2))

            @block.tensor
            def _(pe):
                pe.wait_ge(s_w, 48)

                def mm(n, use, first):
                    pe.wait_ge(s_x[n], 16 * use)
                    if not first:
                        pe.wait_ge(s_q[n], 3 * (use - 1))
                    pe.matmul(ps[n][:, 0:3 * F], xt[:, n, :], w[:, :], start=True, stop=True).then_inc(s_mm[n], 1)
                for n in range(2):
                    mm(n, 1, True)
                with pe.Fori(2, NW // 2 + 1) as i:
                    for n in range(2):
                        mm(n, i, False)
                mm(0, NW // 2 + 1, False)

            @block.vector
            def _(dve):
                dve.wait_ge(s_bias, 48)

                def out(win, n, use, first):
                    dve.wait_ge(s_mm[n], use)
                    if not first:
                        dve.wait_ge(s_k[n], 16 * (use - 1))
                    cols = bass.ds(win * F, F)
                    dve.tensor_tensor(kt[:, n, :], ps[n][:, F:2 * F], bias[:, F:2 * F], ALU.add).then_inc(s_q[n], 1)
                    dve.tensor_tensor(c.work[:, cols], ps[n][:, 0:F], bias[:, 0:F], ALU.add).then_inc(s_q[n], 1)
                    dve.tensor_tensor(c.vals[:, cols], ps[n][:, 2 * F:3 * F], bias[:, 2 * F:3 * F],
                                      ALU.add).then_inc(s_q[n], 1)
                for n in range(2):
                    out(n, n, 1, True)
                with dve.Fori(1, NW // 2) as i:
                    for n in range(2):
                        out(2 * i + n, n, i + 1, False)
                out(NW - 1, 0, NW // 2 + 1, False)


def split_table(c, scale=None):
    nc = c.nc
    c.splits = c.splits + 1 if hasattr(c, "splits") else 0
    s_part, s_rest = semaphores(nc, c.sems, f"part{c.splits} rest{c.splits}")
    with nc.Block() as block:
        @block.vector
        def _(dve):
            n = 0
            if scale is not None:
                dve.tensor_scalar(c.work[:, :], c.work[:, :], scale, None, ALU.mult).then_inc(s_rest, 1)
                dve.wait_ge(s_rest, 1)
                n = 1
            for j in range(3):
                dve.tensor_copy(c.tab[:, j, :], c.work[:, :]).then_inc(s_part, 1)
                if j < 2:
                    dve.wait_ge(s_part, j + 1)
                    dve.tensor_tensor(c.work[:, :], c.work[:, :], c.tab[:, j, :], ALU.subtract).then_inc(s_rest, 1)
                    dve.wait_ge(s_rest, n + j + 1)


SIDES = ("src", "dst")


def load_edges(c, a, e):
    nc = c.nc
    s_def, s_in, s_win, s_lane = semaphores(nc, c.sems, "defaults_set edges_in window_of lane_of")
    (s_fill,) = semaphores(nc, c.stack, "fill_out")
    s_zero, s_rcopy = semaphores(nc, c.sems, "fill_zeroed record_parts")
    c.s_fill = s_fill
    with nc.Block() as block:
        @block.gpsimd
        def _(pool):
            for s in SIDES:
                pool.memset(e.ids[s][:, :], NW * P).then_inc(s_def, 1)
            pool.memset(e.attr[:, :], 0.0).then_inc(s_def, 1)
            pool.memset(e.mask[:, :], 0.0).then_inc(s_def, 1)
            pool.memset(e.rec[:, :, C_ROW:R], 0.0).then_inc(s_def, 1)
            pool.memset(c.rfill[:, :, :], 0.0).then_inc(s_zero, 1)
            pool.memset(c.fill[:, :, :], 0.0).then_inc(s_zero, 1)
            pool.wait_ge(s_zero, 2)
            pool.memset(c.rfill[:, :, C_SL:C_SL + 1], -1.0).then_inc(s_def, 1)
            pool.memset(c.rfill[:, :, C_ROW:C_ROW + 1], NOROW).then_inc(s_def, 1)
            pool.memset(c.fill[:, :, F:F + 1], -1.0).then_inc(s_def, 1)

        @block.sync
        def _(sp):
            sp.wait_ge(s_def, 8)
            for s in SIDES:
                sp.dma_start(e.ids[s][0:EL, :], a[s].rearrange("(p t) -> p t", p=EL)).then_inc(s_in, 16)
            sp.dma_start(e.attr[0:EL, :], a["edge_attr_2"].rearrange("(p t) c -> p (t c)", p=EL)).then_inc(s_in, 16)
            sp.dma_start(e.mask[0:EL, :], a["edge_attr_8"].rearrange("(p t) c -> p (t c)", p=EL)).then_inc(s_in, 16)
            for j in range(NT // RF):
                sp.dma_start(c.rec_dram[:, j * RF * R:(j + 1) * RF * R],
                             c.rfill[:, :, :].rearrange("p t r -> p (t r)")).then_inc(s_fill, 16)
            for j in range(NT // CF):
                sp.dma_start(c.row_dram[:, j * CF * CW:(j + 1) * CF * CW],
                             c.fill[:, :, :].rearrange("p t r -> p (t r)")).then_inc(s_fill, 16)

        @block.vector
        def _(dve):
            dve.wait_ge(s_in, 64)
            for n, s in enumerate(SIDES):
                dve.tensor_scalar(e.tmpi[:, n, :], e.ids[s][:, :], 7, None, ALU.arith_shift_right).then_inc(s_win, 1)
                dve.wait_ge(s_win, 2 * n + 1)
                dve.tensor_copy(e.hi[s][:, :], e.tmpi[:, n, :]).then_inc(s_win, 1)
                dve.wait_ge(s_win, 2 * n + 2)
                dve.tensor_scalar(e.tmpi[:, n, :], e.ids[s][:, :], P - 1, None, ALU.bitwise_and).then_inc(s_lane, 1)
                dve.wait_ge(s_lane, 2 * n + 1)
                col = C_SL if s == "src" else C_DL
                dve.tensor_copy(e.rec[:, :, col], e.tmpi[:, n, :]).then_inc(s_lane, 1)
            dve.tensor_copy(e.rec[:, :, C_DST], e.ids["dst"][:, :]).then_inc(s_rcopy, 1)

        @block.scalar
        def _(act):
            act.wait_ge(s_in, 64)
            act.activation(e.rec[:, :, 0:H], e.mask[:, :].rearrange("p (t h) -> p t h", h=H), ACT.Copy).then_inc(s_rcopy, 1)
            act.activation(e.rec[:, :, C_ATTR:C_ATTR + 2], e.attr[:, :].rearrange("p (t h) -> p t h", h=2),
                           ACT.Copy).then_inc(s_rcopy, 1)


def windows_onehot(dve, c, e, s, t0, n, out):
    return dve.tensor_tensor(out, e.hi[s][:, bass.ds(t0, n)].unsqueeze(2).to_broadcast([P, n, NW]),
                             c.iota[:, 0:NW].unsqueeze(1).to_broadcast([P, n, NW]), ALU.is_equal)


def count_windows(c, e):
    nc = c.nc
    s_oh0, s_oh1, s_mm0, s_mm1, s_sum, s_step, s_turn, s_past, s_row = semaphores(
        nc, c.sems, "count_onehot0 count_onehot1 counted0 counted1 window_sums base_step ends_turned tile_past tile_windows")
    s_oh, s_mm = (s_oh0, s_oh1), (s_mm0, s_mm1)
    (s_z, s_io) = semaphores(nc, c.sems, "zero_set tile_iota")
    with ExitStack() as t:
        sb = lambda n, s, d: t.enter_context(nc.sbuf_tensor(n, s, d))
        oh = sb("count_oh", [P, 2, EC, NW], BF16)
        zero = sb("count_zero", [P, 512], BF16)
        cnt = sb("cnt", [P, 2, NW], F32)
        cnti = sb("cnti", [P, 2, NW], I32)
        cnti2 = sb("cnti2", [P, 2, NW], I32)
        til = sb("tiles", [P, 2, NW], F32)
        ends = sb("ends", [P, 2, NW], F32)
        endc = sb("end_col", [P, 2], F32)
        one = sb("one_f", [P, NW], F32)
        past = sb("past", [P, 2, NT], BF16)
        tio = sb("tile_io", [P, NT], F32)
        tii = sb("tile_ii", [P, NT], I32)
        ps_c = [t.enter_context(nc.psum_tensor(f"ps_count{n}", [P, 512], F32)) for n in range(2)]
        ps_e = t.enter_context(nc.psum_tensor("ps_ends", [P, 512], F32))
        ps_w = [t.enter_context(nc.psum_tensor(f"ps_win{n}", [P, 512], F32)) for n in range(4)]
        IT = ET // EC
        HT = NT // 2
        with nc.Block() as block:
            @block.gpsimd
            def _(pool):
                pool.memset(zero[:, :], 0.0).then_inc(s_z, 1)
                pool.memset(one[:, :], 1.0).then_inc(s_z, 1)
                pool.memset(endc[:, :], 1e9).then_inc(s_z, 1)
                pool.iota(tii[:, :], pattern=[[1, NT]], base=0, channel_multiplier=0).then_inc(s_io, 1)
                pool.wait_ge(s_io, 1)
                pool.tensor_copy(tio[:, :], tii[:, :]).then_inc(s_io, 1)

            @block.vector
            def _(dve):
                def one_hot(i, n, first):
                    if not first:
                        dve.wait_ge(s_mm[n], i)
                    windows_onehot(dve, c, e, SIDES[n], i * EC, EC, oh[:, n]).then_inc(s_oh[n], 1)
                for n in range(2):
                    one_hot(0, n, True)
                with dve.Fori(1, IT) as i:
                    for n in range(2):
                        one_hot(i, n, False)
                for n in range(2):
                    dve.wait_ge(s_mm[n], IT + 1)
                    dve.tensor_reduce(cnt[:, n, :], ps_c[n][:, 0:EC * NW].rearrange("p (j w) -> p w j", w=NW),
                                      AX_X, ALU.add).then_inc(s_sum, 1)
                dve.wait_ge(s_sum, 2)
                dve.wait_ge(s_z, 3)
                steps = [0]

                def step(ins):
                    steps[0] += 1
                    ins.then_inc(s_step, 1)
                    dve.wait_ge(s_step, steps[0])
                step(dve.tensor_scalar(cnti[:, :, :], cnt[:, :, :], float(P - 1), None, ALU.add))
                step(dve.tensor_scalar(cnti2[:, :, :], cnti[:, :, :], 7, None, ALU.arith_shift_right))
                step(dve.tensor_copy(til[:, :, :], cnti2[:, :, :]))
                for n in range(2):
                    step(dve.tensor_tensor_scan(ends[:, n, :], one[:, :], til[:, n, :], 0.0, ALU.mult, ALU.add))
                step(dve.tensor_tensor(til[:, :, :], ends[:, :, :], til[:, :, :], ALU.subtract))
                for n in range(2):
                    step(dve.tensor_scalar(e.run[SIDES[n]][:, 0, :], til[:, n, :], float(P), None, ALU.mult))
                dve.wait_ge(s_turn, 2)
                for n in range(2):
                    step(dve.tensor_copy(endc[0:NW, n:n + 1], ps_e[0:NW, n * P:n * P + 1]))
                dve.wait_ge(s_io, 2)
                for n in range(2):
                    dve.tensor_scalar(past[:, n, :], tio[:, :], endc[:, n:n + 1], None, ALU.is_ge).then_inc(s_past, 1)
                for n in range(2):
                    for h in range(2):
                        dve.wait_ge(s_row, 2 * n + h + 1)
                        dve.tensor_scalar(c.win[SIDES[n]][0:1, h * HT:(h + 1) * HT], ps_w[2 * n + h][0:1, 0:HT],
                                          float(NW - 1), None, ALU.min)

            @block.tensor
            def _(pe):
                pe.wait_ge(s_z, 3)
                for n in range(2):
                    pe.matmul(ps_c[n][:, 0:EC * NW], c.ones[:, :], zero[:, 0:EC * NW], start=True, stop=False)
                with pe.Fori(0, IT) as i:
                    for n in range(2):
                        pe.wait_ge(s_oh[n], i + 1)
                        pe.matmul(ps_c[n][:, 0:EC * NW], c.ones[:, :], oh[:, n].rearrange("p j w -> p (j w)"),
                                  start=False, stop=False, skip_group_check=True).then_inc(s_mm[n], 1)
                for n in range(2):
                    pe.matmul(ps_c[n][:, 0:EC * NW], c.ones[:, :], zero[:, 0:EC * NW], start=False,
                              stop=True).then_inc(s_mm[n], 1)
                pe.wait_ge(s_step, 5)
                for n in range(2):
                    pe.transpose(ps_e[0:NW, n * P:(n + 1) * P], ends[:, n, :], c.ident[:, :]).then_inc(s_turn, 1)
                for n in range(2):
                    pe.wait_ge(s_past, n + 1)
                    for h in range(2):
                        pe.matmul(ps_w[2 * n + h][:, 0:HT], c.ones[:, :], past[:, n, h * HT:(h + 1) * HT],
                                  start=True, stop=True).then_inc(s_row, 1)


def place_edges(c, e):
    nc = c.nc
    names = ("place_onehot before after_start masked slot running slot_int slot_lane slot_tile lane_part tile_part "
             "row_of rec_slot row_index")
    (s_oh, s_cum, s_add, s_msk, s_slot, s_run, s_int, s_lane, s_tile, s_lp, s_tp, s_row, s_rec, s_idx) = semaphores(
        nc, c.sems, names)
    s_sent = semaphores(nc, c.stack, "records_sent0 records_sent1")
    (s_turn, s_init) = semaphores(nc, c.sems, "scatter_turn place_init")
    IT = ET // PG
    with ExitStack() as t:
        sb = lambda n, s, d: t.enter_context(nc.sbuf_tensor(n, s, d))
        oh = {s: sb("place_oh_" + s, [P, PG + 1, NW], BF16) for s in SIDES}
        cum = {s: sb("cum_" + s, [P, PG, NW], F32) for s in SIDES}
        slot = sb("slot", [P, 2, PG], F32)
        sloti = sb("sloti", [P, 2, PG], I32)
        lane = sb("slot_lane_i", [P, 2, PG], I32)
        tile = sb("slot_tile_i", [P, 2, PG], I32)
        lanef = sb("slot_lane_f", [P, 2, PG], F32)
        row = sb("row_f", [P, 2, PG], F32)
        idx = sb("row_idx", [P, 2, PG], I32)
        out = sb("rec_out", [P, 2, PG, R], F32)
        norow = sb("norow", [P, 1], F32)
        lanes = sb("lanes_i", [P, 1], I32)
        ps = {s: t.enter_context(nc.psum_tensor("ps_before_" + s, [P, 512], F32)) for s in SIDES}
        with nc.Block() as block:
            @block.vector
            def _(dve):
                dve.wait_ge(s_init, 4)

                def place(g, half):
                    for n, s in enumerate(SIDES):
                        wait_count(dve, s_cum, 2 * g)
                        windows_onehot(dve, c, e, s, g * PG, PG, oh[s][:, 0:PG]).then_inc(s_oh, 1)
                    for n, s in enumerate(SIDES):
                        dve.wait_ge(s_cum, 2 * g + n + 1)
                        start = e.run[s][:, half:half + 1, :]
                        dve.tensor_tensor(cum[s][:, :, :], ps[s][:, 0:PG * NW].rearrange("p (j w) -> p j w", w=NW),
                                          start.to_broadcast([P, PG, NW]), ALU.add).then_inc(s_add, 1)
                        dve.tensor_tensor(e.run[s][:, 1 - half, :], ps[s][:, PG * NW:(PG + 1) * NW],
                                          e.run[s][:, half, :], ALU.add).then_inc(s_run, 1)
                        dve.wait_ge(s_add, 2 * g + n + 1)
                        dve.tensor_tensor(cum[s][:, :, :], cum[s][:, :, :], oh[s][:, 0:PG], ALU.mult).then_inc(s_msk, 1)
                        dve.wait_ge(s_msk, 2 * g + n + 1)
                        dve.tensor_reduce(slot[:, n, :], cum[s][:, :, :], AX_X, ALU.add).then_inc(s_slot, 1)
                    dve.wait_ge(s_slot, 2 * g + 2)
                    dve.wait_ge(s_run, 2 * g + 2)
                    dve.tensor_copy(sloti[:, :, :], slot[:, :, :]).then_inc(s_int, 1)
                    dve.wait_ge(s_int, g + 1)
                    dve.tensor_scalar(lane[:, :, :], sloti[:, :, :], P - 1, None, ALU.bitwise_and).then_inc(s_lane, 1)
                    dve.tensor_scalar(tile[:, :, :], sloti[:, :, :], 7, None, ALU.arith_shift_right).then_inc(s_tile, 1)
                    dve.wait_ge(s_lane, g + 1)
                    dve.tensor_scalar(lanef[:, :, :], lane[:, :, :], float(NT), norow[:, 0:1], ALU.mult,
                                      ALU.add).then_inc(s_lp, 1)
                    dve.wait_ge(s_lp, g + 1)
                    dve.wait_ge(s_tile, g + 1)
                    wait_count(dve, s_sent[half], 8 * PG * (g - half))
                    dve.tensor_tensor(idx[:, half, :], lanef[:, 0, :], tile[:, 0, :], ALU.add).then_inc(s_idx, 1)
                    dve.tensor_copy(out[:, half, :, :], e.rec[:, bass.ds(g * PG, PG), :]).then_inc(s_rec, 1)
                    dve.wait_ge(s_rec, g + 1)
                    dve.tensor_tensor(out[:, half, :, C_ROW], lanef[:, 1, :], tile[:, 1, :], ALU.add).then_inc(s_row, 1)
                    dve.wait_ge(s_row, g + 1)
                place(0, 0)
                place(1, 1)
                with dve.Fori(1, IT // 2) as i:
                    place(2 * i, 0)
                    place(2 * i + 1, 1)

            @block.tensor
            def _(pe):
                pe.wait_ge(s_init, 4)

                def before(g):
                    for n, s in enumerate(SIDES):
                        pe.wait_ge(s_oh, 2 * g + n + 1)
                        wait_count(pe, s_run, 2 * g)
                        wait_count(pe, s_add, 2 * g)
                        flat = oh[s][:, :, :].rearrange("p j w -> p (j w)")
                        pe.matmul(ps[s][:, 0:(PG + 1) * NW], c.tri[:, :], flat, start=True, stop=False)
                        for j in range(PG):
                            m = PG - j
                            ins = pe.matmul(ps[s][:, (j + 1) * NW:(PG + 1) * NW].rearrange("p (j w) -> p j w", w=NW),
                                            c.ones[:, :], oh[s][:, j:j + 1, :].to_broadcast([P, m, NW]),
                                            start=False, stop=(j == PG - 1))
                        ins.then_inc(s_cum, 1)
                before(0)
                with pe.Fori(1, IT) as g:
                    before(g)

            @block.gpsimd
            def _(pool):
                for s in SIDES:
                    pool.memset(oh[s][:, PG:PG + 1, :], 0.0).then_inc(s_init, 1)
                pool.iota(lanes[:, :], pattern=[[0, 1]], base=0, channel_multiplier=1).then_inc(s_init, 1)
                pool.wait_ge(s_init, 3)
                pool.tensor_scalar(norow[:, :], lanes[:, :], float(EL), NOROW, ALU.is_ge, ALU.mult).then_inc(s_init, 1)
                pool.wait_ge(c.s_fill, 16 * (NT // RF + NT // CF))

                def send(g, half):
                    pool.wait_ge(s_row, g + 1)
                    pool.wait_ge(s_idx, g + 1)
                    pool.sem_inc(s_turn, 1)
                    for j in range(PG):
                        pool.indirect_dma_start(
                            c.rec_rows, bass.IndirectOffsetOnAxis(ap=idx[:, half, j:j + 1], axis=0),
                            out[:, half, j, :], None, bounds_check=SLOTS - 1, oob_is_err=False).then_inc(s_sent[half], 16)
                with pool.Fori(0, IT // 2) as i:
                    for half in range(2):
                        send(2 * i + half, half)
                for half in range(2):
                    pool.wait_ge(s_sent[half], 16 * PG * (IT // 2))


NG = NT // G
RING = 4


def each_group(eng, step, lead=0, lag=0, groups=NG):
    for g in range(-lead, RING):
        step(g, g % RING)
    with eng.Fori(1, groups // RING - 1) as i:
        for r in range(RING):
            step(RING * i + r, r)
    for g in range(groups - RING, groups + lag):
        step(g, g % RING)


def group_at(g, r, by, groups=NG):
    there = not isinstance(g, int) or 0 <= g + by < groups
    return g + by, (r + by) % RING, there


def ring_count(g, r, each):
    return (g - r + RING) * (each // RING)


def load_windows(eng, c, regs, side, g, n=1):
    eng.reg_load(regs[:n * G], c.win[side][0:1, bass.ds(g * G, n * G)])
    return [eng.snap(r, min_val=0, max_val=NW - 1) for r in regs[:n * G]]


def lane_onehot(dve, c, lanes, out):
    return dve.tensor_tensor(out, c.iota[:, :].unsqueeze(1).to_broadcast([P, G, P]),
                             lanes.unsqueeze(2).to_broadcast([P, G, P]), ALU.is_equal)


def load_records(c):
    nc = c.nc
    (s_r,) = semaphores(nc, c.sems, "records_in")
    with nc.Block() as block:
        @block.sync
        def _(sp):
            sp.dma_start(c.rec[:, :, :].rearrange("p t r -> p (t r)"), c.rec_dram[:, :]).then_inc(s_r, 16)
            sp.wait_ge(s_r, 16)

        @block.vector
        def _(dve):
            dve.memset(c.mtab[:, :], -1e30)


def score(c):
    nc = c.nc
    names = ("sc_onehot sc_turned sc_onehot_t sc_onehot_m sc_q sc_index sc_prod sc_dot sc_score sc_hi sc_rest sc_parts "
             "sc_parts_turned sc_parts_t sc_spread sc_tilemax sc_max")
    (s_oh, s_tr, s_oht, s_ohm, s_q, s_idx, s_prod, s_dot, s_sc, s_hi, s_rest, s_parts, s_ptr, s_pt, s_mx, s_red,
     s_max) = semaphores(nc, c.sems, names)
    s_k = semaphores(nc, c.stack, "sc_k_in0 sc_k_in1")
    s_turn, s_init, s_isel = semaphores(nc, c.sems, "sc_gather_turn sc_init sc_sel_zeroed")
    with ExitStack() as t:
        sb = lambda n, s, d: t.enter_context(nc.sbuf_tensor(n, s, d))
        oh = sb("sc_oh", [P, 2, G, P], BF16)
        oht = sb("sc_oht", [P, 2, G, P], BF16)
        ohm = sb("sc_ohm", [P, 2, G, P], BF16)
        idx = sb("sc_idx", [P, 2, G], I32)
        kg = sb("sc_k", [P, 2, G, F], F32)
        prod = sb("sc_prods", [P, G * F], F32)
        dot = sb("sc_dots", [P, G, H], F32)
        rest = sb("sc_rests", [P, G * H], F32)
        parts = sb("sc_split", [P, 2, P], BF16)
        pt = sb("sc_split_t", [P, 2, P], BF16)
        red = sb("sc_red", [P, G, H], F32)
        sel = sb("sc_sel", [P, G * H, P], BF16)
        psq = [t.enter_context(nc.psum_tensor(f"ps_q{b}", [P, 512], F32)) for b in range(2)]
        pst = t.enter_context(nc.psum_tensor("ps_oht", [P, 1024], BF16))
        psp = t.enter_context(nc.psum_tensor("ps_pt", [P, 1024], BF16))
        psm = [t.enter_context(nc.psum_tensor(f"ps_spread{b}", [P, 1024], F32)) for b in range(2)]
        with nc.Block() as block:
            @block.gpsimd
            def _(pool):
                pool.memset(sel[:, :, :], 0.0).then_inc(s_isel, 1)
                pool.memset(parts[:, :, :], 0.0).then_inc(s_init, 1)
                pool.wait_ge(s_isel, 1)
                pool.affine_select(out=sel[:, :, :], in_=sel[:, :, :], compare_op=ALU.not_equal, fill=1.0, base=0,
                                   pattern=[[-1, G * H], [0, P]], channel_multiplier=1).then_inc(s_isel, 1)
                pool.wait_ge(s_isel, 2)
                pool.affine_select(out=sel[:, :, :], in_=sel[:, :, :], compare_op=ALU.not_equal, fill=1.0,
                                   base=-G * H, pattern=[[-1, G * H], [0, P]], channel_multiplier=1).then_inc(s_init, 1)

                def gather(g, b):
                    pool.wait_ge(s_idx, g + 1)
                    wait_count(pool, s_prod, g - 1)
                    pool.sem_inc(s_turn, 1)
                    for k in range(G):
                        pool.indirect_dma_start(kg[:, b, k, :], None, c.k_dram[:, :],
                                                bass.IndirectOffsetOnAxis(ap=idx[:, b, k:k + 1], axis=0)
                                                ).then_inc(s_k[b], 16)
                gather(0, 0)
                gather(1, 1)
                with pool.Fori(1, PAIRS) as i:
                    for b in range(2):
                        gather(2 * i + b, b)

            @block.vector
            def _(dve):
                dve.wait_ge(s_init, 2)

                def front(g, b):
                    wait_count(dve, s_tr, g - 1)
                    rec = c.rec[:, bass.ds(g * G, G), :]
                    dve.tensor_copy(idx[:, b, :], rec[:, :, C_DST]).then_inc(s_idx, 1)
                    lane_onehot(dve, c, rec[:, :, C_SL], oh[:, b]).then_inc(s_oh, 1)

                def middle(g, b, use):
                    dve.wait_ge(s_q, g + 1)
                    dve.wait_ge(s_k[b], 16 * G * use)
                    dve.tensor_tensor(prod[:, :], psq[b][:, :], kg[:, b].rearrange("p k f -> p (k f)"),
                                      ALU.mult).then_inc(s_prod, 1)
                    dve.wait_ge(s_prod, g + 1)
                    dve.tensor_reduce(dot[:, :, :].rearrange("p k h -> p (k h)"),
                                      prod[:, :].rearrange("p (j d) -> p j d", d=D), AX_X, ALU.add).then_inc(s_dot, 1)
                    dve.wait_ge(s_dot, g + 1)
                    dve.tensor_tensor(dot[:, :, :], dot[:, :, :], c.rec[:, bass.ds(g * G, G), 0:H],
                                      ALU.add).then_inc(s_sc, 1)
                    dve.wait_ge(s_sc, g + 1)
                    wait_count(dve, s_ptr, g - 1)
                    flat = dot[:, :, :].rearrange("p k h -> p (k h)")
                    dve.tensor_copy(parts[:, b, 0:G * H], flat).then_inc(s_hi, 1)
                    dve.tensor_copy(c.sc[:, bass.ds(g * G * H, G * H)], flat)
                    dve.wait_ge(s_hi, g + 1)
                    dve.tensor_tensor(rest[:, :], flat, parts[:, b, 0:G * H], ALU.subtract).then_inc(s_rest, 1)
                    dve.wait_ge(s_rest, g + 1)
                    dve.tensor_copy(parts[:, b, G * H:2 * G * H], rest[:, :]).then_inc(s_parts, 1)

                def back(g):
                    win = load_windows(dve, c, c.dve_regs, "src", g)
                    for k in range(G):
                        dve.wait_ge(s_mx, G * g + k + 1)
                        dve.tensor_reduce(red[:, k, :], psm[k % 2][:, :].rearrange("p (h e) -> p h e", h=H),
                                          AX_X, ALU.max).then_inc(s_red, 1)
                    for k in range(G):
                        dve.wait_ge(s_red, G * g + k + 1)
                        wait_count(dve, s_max, G * g + k)
                        m = c.mtab[:, bass.ds(win[k] * H, H)]
                        dve.tensor_tensor(m, m, red[:, k, :], ALU.max).then_inc(s_max, 1)

                def pair(i, last):
                    for b in range(2):
                        middle(2 * i + b, b, i + 1)
                    if not last:
                        for b in range(2):
                            front(2 * i + 2 + b, b)
                    for b in range(2):
                        back(2 * i + b)
                for b in range(2):
                    front(b, b)
                pair(0, False)
                with dve.Fori(1, PAIRS - 1) as i:
                    pair(i, False)
                pair(PAIRS - 1, True)

            @block.scalar
            def _(act):
                def one_hots(g, b):
                    act.wait_ge(s_tr, g + 1)
                    wait_count(act, s_mx, G * (g - 1))
                    act.activation(oht[:, b].rearrange("p k n -> p (k n)"), pst[:, 0:G * P], ACT.Copy).then_inc(s_oht, 1)
                    act.activation(ohm[:, b].rearrange("p k n -> p (k n)"), pst[:, 0:G * P], ACT.Copy,
                                   bias=-1.0).then_inc(s_ohm, 1)

                def split(g, b):
                    act.wait_ge(s_ptr, g + 1)
                    act.activation(pt[:, b, :], psp[:, 0:P], ACT.Copy).then_inc(s_pt, 1)

                def pair(i):
                    for b in range(2):
                        one_hots(2 * i + b, b)
                    for b in range(2):
                        split(2 * i + b, b)
                pair(0)
                with act.Fori(1, PAIRS) as i:
                    pair(i)

            @block.tensor
            def _(pe):
                pe.wait_ge(s_init, 2)

                def queries(g, b):
                    pe.wait_ge(s_oh, g + 1)
                    wait_count(pe, s_ohm, g)
                    for k in range(G):
                        ins = pe.transpose(pst[:, k * P:(k + 1) * P], oh[:, b, k, :], c.identb[:, :])
                    ins.then_inc(s_tr, 1)
                    win = load_windows(pe, c, c.pe_regs, "src", g)
                    pe.wait_ge(s_oht, g + 1)
                    wait_count(pe, s_prod, g - 1)
                    for k in range(G):
                        for j in range(3):
                            ins = pe.matmul(psq[b][:, k * F:(k + 1) * F], oht[:, b, k, :],
                                            c.tab[:, j, bass.ds(win[k] * F, F)], start=(j == 0), stop=(j == 2))
                    ins.then_inc(s_q, 1)

                def spread(g, b):
                    pe.wait_ge(s_parts, g + 1)
                    wait_count(pe, s_pt, g)
                    pe.transpose(psp[:, 0:P], parts[:, b, :], c.identb[:, :]).then_inc(s_ptr, 1)
                    pe.wait_ge(s_pt, g + 1)
                    pe.wait_ge(s_ohm, g + 1)
                    for k in range(G):
                        wait_count(pe, s_red, G * g + k - 1)
                        for q in range(2):
                            pe.matmul(psm[k % 2][:, q * 512:(q + 1) * 512].rearrange("p (h e) -> p h e", h=4),
                                      c.bigid[:, :], ohm[:, b, k, :].unsqueeze(1).to_broadcast([P, 4, P]),
                                      start=True, stop=False)
                            for h in range(4):
                                kh = k * H + q * 4 + h
                                ins = pe.matmul(psm[k % 2][:, (q * 4 + h) * P:(q * 4 + h + 1) * P], sel[:, kh, :],
                                                pt[:, b, :], start=False, stop=(h == 3))
                        ins.then_inc(s_mx, 1)

                def pair(i):
                    for b in range(2):
                        queries(2 * i + b, b)
                    for b in range(2):
                        spread(2 * i + b, b)
                pair(0)
                with pe.Fori(1, PAIRS) as i:
                    pair(i)


def split_maximum(c, mt):
    nc = c.nc
    s_hi, s_rest = semaphores(nc, c.sems, "max_hi max_rest")
    with ExitStack() as t:
        rest = t.enter_context(nc.sbuf_tensor("max_rests", [P, NW * H], F32))
        with nc.Block() as block:
            @block.vector
            def _(dve):
                dve.tensor_copy(mt[:, 0, :], c.mtab[:, :]).then_inc(s_hi, 1)
                dve.wait_ge(s_hi, 1)
                dve.tensor_tensor(rest[:, :], c.mtab[:, :], mt[:, 0, :], ALU.subtract).then_inc(s_rest, 1)
                dve.wait_ge(s_rest, 1)
                dve.tensor_copy(mt[:, 1, :], rest[:, :])


def exps(c):
    nc = c.nc
    names = ("ex_onehot ex_turned ex_onehot_t ex_m ex_less ex_exp ex_part0 ex_rest0 ex_part1 ex_rest1 ex_parts ex_sums "
             "ex_zero ex_end")
    (s_oh, s_tr, s_oht, s_m, s_d, s_ex, s_p0, s_r0, s_p1, s_r1, s_parts, s_sum, s_z, s_end) = semaphores(
        nc, c.sems, names)
    with ExitStack() as t:
        sb = lambda n, s, d: t.enter_context(nc.sbuf_tensor(n, s, d))
        mt = sb("max_parts", [P, 2, NW * H], BF16)
        split_maximum(c, mt)
        oh = sb("ex_oh", [P, 2, G, P], BF16)
        oht = sb("ex_oht", [P, 2, G, P], BF16)
        less = sb("ex_lesses", [P, 2, G * H], F32)
        ex = sb("ex_exps", [P, 2, G * H], F32)
        rest = sb("ex_rests", [P, G * H], F32)
        parts = sb("ex_split", [P, 2, 3, G * H], BF16)
        zero = sb("ex_zeros", [P, 512], BF16)
        pst = t.enter_context(nc.psum_tensor("ps_ex_oht", [P, 1024], BF16))
        psm = [t.enter_context(nc.psum_tensor(f"ps_ex_m{b}", [P, 512], F32)) for b in range(2)]
        psd = t.enter_context(nc.psum_tensor("ps_sums", [P, 512], F32))
        with nc.Block() as block:
            @block.gpsimd
            def _(pool):
                pool.memset(zero[:, :], 0.0).then_inc(s_z, 1)

            @block.vector
            def _(dve):
                def front(g, b):
                    wait_count(dve, s_sum, g - 1)
                    lane_onehot(dve, c, c.rec[:, bass.ds(g * G, G), C_SL], oh[:, b]).then_inc(s_oh, 1)

                def middle(g, b):
                    cols = bass.ds(g * G * H, G * H)
                    dve.wait_ge(s_m, g + 1)
                    wait_count(dve, s_ex, g - 1)
                    dve.tensor_tensor(less[:, b, :], c.sc[:, cols], psm[b][:, 0:G * H], ALU.subtract).then_inc(s_d, 1)

                def split(g, b):
                    cols = bass.ds(g * G * H, G * H)
                    dve.wait_ge(s_ex, g + 1)
                    wait_count(dve, s_sum, g - 1)
                    dve.tensor_copy(parts[:, b, 0, :], ex[:, b, :]).then_inc(s_p0, 1)
                    dve.tensor_copy(c.sc[:, cols], ex[:, b, :])
                    dve.wait_ge(s_p0, g + 1)
                    dve.tensor_tensor(rest[:, :], ex[:, b, :], parts[:, b, 0, :], ALU.subtract).then_inc(s_r0, 1)
                    dve.wait_ge(s_r0, g + 1)
                    dve.tensor_copy(parts[:, b, 1, :], rest[:, :]).then_inc(s_p1, 1)
                    dve.wait_ge(s_p1, g + 1)
                    dve.tensor_tensor(rest[:, :], rest[:, :], parts[:, b, 1, :], ALU.subtract).then_inc(s_r1, 1)
                    dve.wait_ge(s_r1, g + 1)
                    dve.tensor_copy(parts[:, b, 2, :], rest[:, :]).then_inc(s_parts, 1)

                def pair(i, last):
                    for b in range(2):
                        middle(2 * i + b, b)
                    for b in range(2):
                        split(2 * i + b, b)
                    if not last:
                        for b in range(2):
                            front(2 * i + 2 + b, b)
                for b in range(2):
                    front(b, b)
                pair(0, False)
                with dve.Fori(1, PAIRS - 1) as i:
                    pair(i, False)
                pair(PAIRS - 1, True)
                dve.wait_ge(s_end, 1)
                dve.tensor_scalar(c.dtab[:, :], psd[:, 0:NW * H], 1e-20, None, ALU.max)

            @block.scalar
            def _(act):
                def turned(g, b):
                    act.wait_ge(s_tr, g + 1)
                    wait_count(act, s_m, g - 1)
                    act.activation(oht[:, b].rearrange("p k n -> p (k n)"), pst[:, 0:G * P], ACT.Copy).then_inc(s_oht, 1)

                def exp(g, b):
                    act.wait_ge(s_d, g + 1)
                    wait_count(act, s_parts, g - 1)
                    act.activation(ex[:, b, :], less[:, b, :], ACT.Exp).then_inc(s_ex, 1)

                def pair(i):
                    for b in range(2):
                        turned(2 * i + b, b)
                    for b in range(2):
                        exp(2 * i + b, b)
                pair(0)
                with act.Fori(1, PAIRS) as i:
                    pair(i)

            @block.tensor
            def _(pe):
                pe.wait_ge(s_z, 1)
                pe.matmul(psd[:, 0:NW * H], c.ones[:, :], zero[:, 0:NW * H], start=True, stop=False)

                def maxima(g, b, win):
                    pe.wait_ge(s_oh, g + 1)
                    wait_count(pe, s_oht, g)
                    for k in range(G):
                        ins = pe.transpose(pst[:, k * P:(k + 1) * P], oh[:, b, k, :], c.identb[:, :])
                    ins.then_inc(s_tr, 1)
                    pe.wait_ge(s_oht, g + 1)
                    wait_count(pe, s_d, g - 1)
                    for k in range(G):
                        for j in range(2):
                            ins = pe.matmul(psm[b][:, k * H:(k + 1) * H], oht[:, b, k, :],
                                            mt[:, j, bass.ds(win[k] * H, H)], start=(j == 0), stop=(j == 1))
                    ins.then_inc(s_m, 1)

                def sums(g, b, win):
                    pe.wait_ge(s_parts, g + 1)
                    for k in range(G):
                        for j in range(3):
                            ins = pe.matmul(psd[:, bass.ds(win[k] * H, H)], oh[:, b, k, :],
                                            parts[:, b, j, k * H:(k + 1) * H], start=False, stop=False,
                                            skip_group_check=True)
                    ins.then_inc(s_sum, 1)

                def pair(i):
                    win = load_windows(pe, c, c.pe_regs, "src", 2 * i, 2)
                    for b in range(2):
                        maxima(2 * i + b, b, win[b * G:(b + 1) * G])
                    for b in range(2):
                        sums(2 * i + b, b, win[b * G:(b + 1) * G])
                pair(0)
                with pe.Fori(1, PAIRS) as i:
                    pair(i)
                pe.matmul(psd[:, 0:NW * H], c.ones[:, :], zero[:, 0:NW * H], start=False, stop=True).then_inc(s_end, 1)


def normalise_values(c):
    nc = c.nc
    (s_rec,) = semaphores(nc, c.sems, "sums_inverted")
    with nc.Block() as block:
        @block.vector
        def _(dve):
            dve.reciprocal(c.mtab[:, :], c.dtab[:, :]).then_inc(s_rec, 1)
            dve.wait_ge(s_rec, 1)
            dve.tensor_tensor(c.work[:, :].rearrange("p (j d) -> p j d", d=D),
                              c.vals[:, :].rearrange("p (j d) -> p j d", d=D),
                              c.mtab[:, :].unsqueeze(2).to_broadcast([P, NW * H, D]), ALU.mult)


def weigh(c):
    nc = c.nc
    names = "we_onehot we_turned we_onehot_t we_v we_index we_contrib we_lane"
    (s_oh, s_tr, s_oht, s_v, s_idx, s_con, s_lane) = semaphores(nc, c.sems, names)
    s_sent = semaphores(nc, c.stack, "we_sent0 we_sent1")
    s_turn, s_pad = semaphores(nc, c.sems, "we_scatter_turn we_padded")
    with ExitStack() as t:
        sb = lambda n, s, d: t.enter_context(nc.sbuf_tensor(n, s, d))
        oh = sb("we_oh", [P, 2, G, P], BF16)
        oht = sb("we_oht", [P, 2, G, P], BF16)
        idx = sb("we_idx", [P, 2, G], I32)
        con = sb("we_rows", [P, 2, G, CW], F32)
        pst = t.enter_context(nc.psum_tensor("ps_we_oht", [P, 1024], BF16))
        psv = [t.enter_context(nc.psum_tensor(f"ps_v{b}", [P, 512], F32)) for b in range(2)]
        with nc.Block() as block:
            @block.gpsimd
            def _(pool):
                def scatter(g, b):
                    pool.wait_ge(s_con, g + 1)
                    pool.wait_ge(s_lane, g + 1)
                    pool.wait_ge(s_idx, g + 1)
                    pool.sem_inc(s_turn, 1)
                    for k in range(G):
                        pool.indirect_dma_start(c.row_rows, bass.IndirectOffsetOnAxis(ap=idx[:, b, k:k + 1], axis=0),
                                                con[:, b, k, :], None, bounds_check=SLOTS - 1, oob_is_err=False
                                                ).then_inc(s_sent[b], 16)
                pool.wait_ge(s_pad, 1)
                with pool.Fori(0, PAIRS) as i:
                    for b in range(2):
                        scatter(2 * i + b, b)
                for b in range(2):
                    pool.wait_ge(s_sent[b], 16 * G * PAIRS)

            @block.vector
            def _(dve):
                dve.memset(con[:, :, :, F + 1:CW], 0.0).then_inc(s_pad, 1)

                def front(g, b):
                    wait_count(dve, s_tr, g - 1)
                    lane_onehot(dve, c, c.rec[:, bass.ds(g * G, G), C_SL], oh[:, b]).then_inc(s_oh, 1)

                def middle(g, b):
                    wait_count(dve, s_sent[b], 8 * G * (g - b))
                    rec = c.rec[:, bass.ds(g * G, G), :]
                    dve.tensor_copy(idx[:, b, :], rec[:, :, C_ROW]).then_inc(s_idx, 1)
                    dve.tensor_copy(con[:, b, :, F], rec[:, :, C_DL]).then_inc(s_lane, 1)
                    dve.wait_ge(s_v, g + 1)
                    ex = c.sc[:, bass.ds(g * G * H, G * H)].rearrange("p (k h) -> p k h", h=H)
                    dve.tensor_tensor(con[:, b, :, 0:F].rearrange("p k (h d) -> p k h d", d=D),
                                      psv[b][:, :].rearrange("p (k h d) -> p k h d", h=H, d=D),
                                      ex.unsqueeze(3).to_broadcast([P, G, H, D]), ALU.mult).then_inc(s_con, 1)

                def pair(i, last):
                    for b in range(2):
                        middle(2 * i + b, b)
                        if not last:
                            front(2 * i + 2 + b, b)
                for b in range(2):
                    front(b, b)
                pair(0, False)
                with dve.Fori(1, PAIRS - 1) as i:
                    pair(i, False)
                pair(PAIRS - 1, True)

            @block.scalar
            def _(act):
                def turned(g, b):
                    act.wait_ge(s_tr, g + 1)
                    wait_count(act, s_v, g - 1)
                    act.activation(oht[:, b].rearrange("p k n -> p (k n)"), pst[:, 0:G * P], ACT.Copy).then_inc(s_oht, 1)
                for b in range(2):
                    turned(b, b)
                with act.Fori(1, PAIRS) as i:
                    for b in range(2):
                        turned(2 * i + b, b)

            @block.tensor
            def _(pe):
                def values(g, b):
                    win = load_windows(pe, c, c.pe_regs, "src", g)
                    pe.wait_ge(s_oh, g + 1)
                    wait_count(pe, s_oht, g)
                    for k in range(G):
                        ins = pe.transpose(pst[:, k * P:(k + 1) * P], oh[:, b, k, :], c.identb[:, :])
                    ins.then_inc(s_tr, 1)
                    pe.wait_ge(s_oht, g + 1)
                    wait_count(pe, s_con, g - 1)
                    for k in range(G):
                        for j in range(3):
                            ins = pe.matmul(psv[b][:, k * F:(k + 1) * F], oht[:, b, k, :],
                                            c.tab[:, j, bass.ds(win[k] * F, F)], start=(j == 0), stop=(j == 2))
                    ins.then_inc(s_v, 1)
                for b in range(2):
                    values(b, b)
                with pe.Fori(1, PAIRS) as i:
                    for b in range(2):
                        values(2 * i + b, b)


CB = 4


def collect(c):
    nc = c.nc
    s_oh, s_mm, s_add, s_z = semaphores(nc, c.sems, "co_onehot co_sums co_added co_zeroed")
    s_in = semaphores(nc, c.sems, "co_in0 co_in1 co_in2 co_in3")
    with ExitStack() as t:
        sb = lambda n, s, d: t.enter_context(nc.sbuf_tensor(n, s, d))
        cin = sb("co_rows", [P, CB, G, CW], F32)
        oh = sb("co_oh", [P, 2, G, P], F32)
        ps = [t.enter_context(nc.psum_tensor(f"ps_co{b}", [P, 512], F32)) for b in range(2)]
        IT = NT // (G * CB)
        with nc.Block() as block:
            @block.sync
            def _(sp):
                def load(g, r):
                    wait_count(sp, s_mm, g - CB + 1)
                    sp.dma_start(cin[:, r].rearrange("p k c -> p (k c)"),
                                 c.row_dram[:, bass.ds(g * G * CW, G * CW)]).then_inc(s_in[r], 16)
                for r in range(CB):
                    load(r, r)
                with sp.Fori(1, IT) as i:
                    for r in range(CB):
                        load(CB * i + r, r)

            @block.vector
            def _(dve):
                dve.memset(c.vals[:, :], 0.0).then_inc(s_add, 1)

                def front(g, r, use):
                    dve.wait_ge(s_in[r], 16 * use)
                    wait_count(dve, s_mm, g - 1)
                    lane_onehot(dve, c, cin[:, r, :, F], oh[:, r % 2]).then_inc(s_oh, 1)

                def back(g, r):
                    win = load_windows(dve, c, c.dve_regs, "dst", g)
                    dve.wait_ge(s_mm, g + 1)
                    for k in range(G):
                        dve.wait_ge(s_add, G * g + k + 1)
                        acc = c.vals[:, bass.ds(win[k] * P, P)]
                        dve.tensor_tensor(acc, acc, ps[r % 2][:, k * P:(k + 1) * P], ALU.add).then_inc(s_add, 1)

                def lot(i, last):
                    for r in range(CB):
                        if not (last and r == CB - 1):
                            front(CB * i + r + 1, (r + 1) % CB, i + 1 + (r + 1) // CB)
                        back(CB * i + r, r)
                front(0, 0, 1)
                lot(0, False)
                with dve.Fori(1, IT - 1) as i:
                    lot(i, False)
                lot(IT - 1, True)

            @block.tensor
            def _(pe):
                def sums(g, r):
                    pe.wait_ge(s_oh, g + 1)
                    wait_count(pe, s_add, G * (g - 1) + 1)
                    for k in range(G):
                        ins = pe.matmul(ps[r % 2][:, k * P:(k + 1) * P], cin[:, r, k, 0:F], oh[:, r % 2, k, :],
                                        start=True, stop=True)
                    ins.then_inc(s_mm, 1)
                for r in range(CB):
                    sums(r, r)
                with pe.Fori(1, IT) as i:
                    for r in range(CB):
                        sums(CB * i + r, r)


def each_window(eng, body):
    for b in range(2):
        body(b, b, 1)
    with eng.Fori(1, NW // 2) as i:
        for b in range(2):
            body(2 * i + b, b, i + 1)
    body(NW - 1, 0, NW // 2 + 1)


def row_vector(v, n):
    return v.rearrange("(o n) -> o n", o=1).to_broadcast([P, n])


def nodes1(c, a):
    nc = c.nc
    names = ("n1_weights n1_acc n1_o n1_res n1_sum n1_stats n1_moments n1_std n1_rstd n1_shift n1_x1 n1_turn n1_x1t "
             "n1_ab n1_a n1_b n1_act_turn n1_x1tab n1_dve_turn n1_set")
    (s_w, s_acc, s_o, s_res, s_sum, s_st, s_mv, s_std, s_rstd, s_shift, s_x1, s_tr, s_x1t, s_ab, s_a, s_b, s_turn,
     s_x1tab, s_dturn, s_set) = semaphores(nc, c.sems, names)
    s_x = semaphores(nc, c.sems, "n1_x0 n1_x1in")
    s_bo = semaphores(nc, c.sems, "n1_b_out0 n1_b_out1")
    s_xo = semaphores(nc, c.sems, "n1_x1_out0 n1_x1_out1")
    with ExitStack() as t:
        sb = lambda n, s, d: t.enter_context(nc.sbuf_tensor(n, s, d))
        wo = sb("w_o", [P, F], F32)
        bo = sb("b_o", [P, F], F32)
        w1 = sb("w_1", [P, 2 * F], F32)
        b1 = sb("b_1", [P, F], F32)
        accs = sb("n1_accs", [P, 2, P], F32)
        xr = sb("n1_xr", [P, 2, F], F32)
        res = sb("n1_ress", [P, F], F32)
        stats = sb("n1_statss", [P, nc.vector.BN_STATS_DIM], F32)
        mv = sb("n1_mvs", [P, nc.vector.BN_AGGR_DIM], F32)
        std = sb("n1_stds", [P, 1], F32)
        rstd = sb("n1_rstds", [P, 1], F32)
        eps = sb("n1_eps", [P, 1], F32)
        x1 = sb("n1_x1s", [P, 2, F], F32)
        x1t = sb("n1_x1ts", [P, 2, P], F32)
        bt = sb("n1_bts", [P, 2, F], F32)
        pso = [t.enter_context(nc.psum_tensor(f"ps_o{b}", [P, 512], F32)) for b in range(2)]
        psx = [t.enter_context(nc.psum_tensor(f"ps_x{b}", [P, 512], F32)) for b in range(2)]
        psab = [t.enter_context(nc.psum_tensor(f"ps_ab{b}", [P, 512], F32)) for b in range(2)]
        with nc.Block() as block:
            @block.gpsimd
            def _(pool):
                pool.memset(eps[:, :], EPS).then_inc(s_set, 1)
                pool.memset(xr[:, :, :], 0.0).then_inc(s_set, 1)

            @block.sync
            def _(sp):
                sp.dma_start(wo[:, :], a["WoT"]).then_inc(s_w, 16)
                sp.dma_start(bo[:, :], row_vector(a["bo"], F)).then_inc(s_w, 16)
                sp.dma_start(w1[:, 0:F], a["eW1"][0:F, :]).then_inc(s_w, 16)
                sp.dma_start(w1[:, F:2 * F], a["eW1"][F:2 * F, :]).then_inc(s_w, 16)
                sp.dma_start(b1[:, :], row_vector(a["eb1"], F)).then_inc(s_w, 16)

                def load(w, b, use):
                    wait_count(sp, s_res, w - 1)
                    rows = LAST if isinstance(w, int) and w == NW - 1 else P
                    sp.dma_start(xr[0:rows, b, :], a["x"][bass.ds(w * P, rows), :]).then_inc(s_x[b], 16)

                def store(w, b, use):
                    sp.wait_ge(s_x1, w + 1)
                    sp.dma_start(c.x1_dram[bass.ds(w * P, P), :], x1[:, b, :]).then_inc(s_xo[b], 16)
                    sp.wait_ge(s_b, w + 1)
                    sp.dma_start(c.b_dram[bass.ds(w * P, P), :], bt[:, b, :]).then_inc(s_bo[b], 16)
                sp.wait_ge(s_set, 2)
                load(0, 0, 1)
                load(1, 1, 1)
                with sp.Fori(0, NW // 2 - 1) as i:
                    for b in range(2):
                        store(2 * i + b, b, 0)
                        load(2 * i + 2 + b, b, 0)
                store(NW - 3, 0, 0)
                load(NW - 1, 0, 0)
                store(NW - 2, 1, 0)
                store(NW - 1, 0, 0)
                for b in range(2):
                    sp.wait_ge(s_xo[b], 16 * (NW // 2 + 1 - b))
                    sp.wait_ge(s_bo[b], 16 * (NW // 2 + 1 - b))

            @block.scalar
            def _(act):
                act.wait_ge(s_set, 2)

                def window(w, b, use):
                    wait_count(act, s_o, w - 1)
                    act.sem_inc(s_turn, 1)
                    act.activation(accs[:, b, :], c.vals[:, bass.ds(w * P, P)], ACT.Copy).then_inc(s_acc, 1)
                    act.wait_ge(s_mv, w + 1)
                    wait_count(act, s_rstd, w)
                    act.activation(std[:, :], mv[:, 1:2], ACT.Sqrt, bias=eps[:, 0:1]).then_inc(s_std, 1)
                    act.wait_ge(s_tr, w + 1)
                    wait_count(act, s_ab, w - 1)
                    act.activation(x1t[:, b, :], psx[b][:, 0:P], ACT.Copy).then_inc(s_x1t, 1)
                    act.wait_ge(s_x1t, w + 1)
                    act.sem_inc(s_turn, 1)
                    act.activation(c.x1t[:, bass.ds(w * P, P)], x1t[:, b, :], ACT.Copy).then_inc(s_x1tab, 1)
                each_window(act, window)

            @block.tensor
            def _(pe):
                pe.wait_ge(s_w, 80)

                def window(w, b, use):
                    pe.wait_ge(s_acc, w + 1)
                    wait_count(pe, s_res, w - 1)
                    pe.matmul(pso[b][:, 0:F], accs[:, b, :], wo[:, :], start=True, stop=True).then_inc(s_o, 1)
                    pe.wait_ge(s_x1, w + 1)
                    wait_count(pe, s_x1t, w - 1)
                    pe.transpose(psx[b][:, 0:P], x1[:, b, :], c.ident[:, :]).then_inc(s_tr, 1)
                    pe.wait_ge(s_x1t, w + 1)
                    wait_count(pe, s_b, w - 1)
                    pe.matmul(psab[b][:, 0:2 * F], x1t[:, b, :], w1[:, :], start=True, stop=True).then_inc(s_ab, 1)
                each_window(pe, window)

            @block.vector
            def _(dve):
                dve.wait_ge(s_w, 80)

                def window(w, b, use):
                    dve.wait_ge(s_x[b], 16 * use)
                    dve.wait_ge(s_o, w + 1)
                    dve.tensor_tensor(res[:, :], pso[b][:, 0:F], xr[:, b, :], ALU.add).then_inc(s_res, 1)
                    dve.wait_ge(s_res, w + 1)
                    dve.tensor_tensor(res[:, :], res[:, :], bo[:, :], ALU.add).then_inc(s_sum, 1)
                    dve.wait_ge(s_sum, w + 1)
                    normalise(dve, c, w, res, stats, mv, std, rstd, (s_st, s_mv, s_std, s_rstd, s_dturn))
                    wait_count(dve, s_xo[b], 16 * (use - 1))
                    wait_count(dve, s_tr, w - 1)
                    dve.tensor_scalar(x1[:, b, :], res[:, :], mv[:, 0:1], rstd[:, 0:1], ALU.subtract,
                                      ALU.mult).then_inc(s_x1, 1)
                    dve.wait_ge(s_ab, w + 1)
                    dve.tensor_tensor(c.work[:, bass.ds(w * F, F)], psab[b][:, 0:F], b1[:, :], ALU.add).then_inc(s_a, 1)
                    wait_count(dve, s_bo[b], 16 * (use - 1))
                    dve.tensor_copy(bt[:, b, :], psab[b][:, F:2 * F]).then_inc(s_b, 1)
                each_window(dve, window)


def normalise(dve, c, w, res, stats, mv, std, rstd, sems):
    s_st, s_mv, s_std, s_rstd, s_turn = sems
    dve.bn_stats(stats[:, :], res[:, :]).then_inc(s_st, 1)
    dve.wait_ge(s_st, w + 1)
    dve.sem_inc(s_turn, 1)
    dve.bn_aggr(mv[:, :], stats[:, :]).then_inc(s_mv, 1)
    dve.wait_ge(s_std, w + 1)
    dve.reciprocal(rstd[:, :], std[:, :]).then_inc(s_rstd, 1)
    dve.wait_ge(s_rstd, w + 1)


def attribute_parts(c, a, parts, weights):
    nc = c.nc
    s_w, s_part, s_rest, s_wp, s_sel, s_z = semaphores(nc, c.sems, "ap_w ap_part ap_rest ap_wp ap_sel ap_zeroed")
    K = 9 * 2 * G
    with ExitStack() as t:
        sb = lambda n, s, d: t.enter_context(nc.sbuf_tensor(n, s, d))
        rest = sb("ap_rests", [P, NT, 2], F32)
        wr = sb("ap_wr", [P, F], F32)
        wp = sb("ap_wps", [P, 3, F], BF16)
        pair = sb("ap_pair", [P, K // 2], F32)
        sel = sb("ap_sels", [P, 3, G], F32)
        with nc.Block() as block:
            @block.gpsimd
            def _(pool):
                pool.memset(wr[:, :], 0.0).then_inc(s_z, 1)

            @block.sync
            def _(sp):
                sp.wait_ge(s_z, 1)
                for n in range(K // 2):
                    sp.dma_start(wr[2 * n:2 * n + 2, :], a["eW1"][2 * F:2 * F + 2, :]).then_inc(s_w, 16)

            @block.vector
            def _(dve):
                view = lambda i: parts.rearrange("p (g i x) -> p g i x", i=3, x=2 * G)[:, :, i, :]
                flat = rest[:, :, :].rearrange("p (g k) j -> p g (k j)", k=G)
                attrs = c.rec[:, :, C_ATTR:C_ATTR + 2]
                dve.tensor_copy(rest[:, :, :], attrs).then_inc(s_rest, 1)
                dve.wait_ge(s_rest, 1)
                for i in range(3):
                    dve.tensor_copy(view(i), flat).then_inc(s_part, 1)
                    dve.wait_ge(s_part, i + 1)
                    if i < 2:
                        dve.tensor_tensor(flat, flat, view(i), ALU.subtract).then_inc(s_rest, 1)
                        dve.wait_ge(s_rest, i + 2)
                dve.wait_ge(s_w, 16 * (K // 2))
                for i in range(3):
                    dve.tensor_copy(wp[:, i, :], wr[:, :]).then_inc(s_wp, 1)
                    dve.wait_ge(s_wp, 2 * i + 1)
                    dve.tensor_tensor(wr[:, :], wr[:, :], wp[:, i, :], ALU.subtract).then_inc(s_wp, 1)
                    dve.wait_ge(s_wp, 2 * i + 2)
                dve.tensor_reduce(pair[:, :], c.ident[:, 0:K].rearrange("p (n a) -> p n a", a=2), AX_X,
                                  ALU.add).then_inc(s_sel, 1)
                dve.wait_ge(s_sel, 1)
                dve.tensor_reduce(sel[:, :, :], pair[:, :].rearrange("p (j i k) -> p j k i", j=3, i=3), AX_X,
                                  ALU.add).then_inc(s_sel, 1)
                dve.wait_ge(s_sel, 2)
                n = 2
                for k in range(G):
                    dve.tensor_scalar(weights[:, k, :], wp[:, 0, :], sel[:, 0, k:k + 1], None, ALU.mult).then_inc(s_sel, 1)
                    n += 1
                    for i in (1, 2):
                        dve.wait_ge(s_sel, n)
                        dve.scalar_tensor_tensor(out=weights[:, k, :], in0=wp[:, i, :], scalar=sel[:, i, k:k + 1],
                                                 in1=weights[:, k, :], op0=ALU.mult, op1=ALU.add).then_inc(s_sel, 1)
                        n += 1


def edges(c, a):
    nc = c.nc
    names = ("ed_weights ed_padded ed_onehot ed_onehot_f ed_turned ed_onehot_t ed_index ed_attr ed_attr_turned "
             "ed_attr_t ed_z ed_h ed_o ed_ob ed_f ed_sums ed_added")
    (s_w, s_pad, s_oh, s_ohf, s_tr, s_oht, s_idx, s_at, s_atr, s_att, s_z, s_h, s_o, s_ob, s_f, s_sum,
     s_add) = semaphores(nc, c.sems, names)
    s_b = semaphores(nc, c.stack, "ed_b_in0 ed_b_in1 ed_b_in2 ed_b_in3")
    (s_turn,) = semaphores(nc, c.sems, "ed_gather_turn")
    K = 9 * 2 * G
    with ExitStack() as t:
        sb = lambda n, s, d: t.enter_context(nc.sbuf_tensor(n, s, d))
        parts = c.work[:, 0:NT * 3].bitcast(BF16)
        wc = sb("w_attr", [P, G, F], BF16)
        attribute_parts(c, a, parts, wc)
        w2 = sb("w_2", [P, F], F32)
        b2 = sb("b_2", [P, F], F32)
        oh = sb("ed_oh", [P, RING, G, P], BF16)
        ohf = sb("ed_ohf", [P, 2, G, P], F32)
        oht = sb("ed_oht", [P, 2, G, P], BF16)
        idx = sb("ed_idx", [P, RING, G], I32)
        bg = sb("ed_bg", [P, RING, G, F], F32)
        attr = sb("ed_attrs", [P, RING, P], BF16)
        att = sb("ed_atts", [P, 2, P], BF16)
        h = sb("ed_hs", [P, 2, G * P], F32)
        ob = sb("ed_obs", [P, 2, G * F], F32)
        ef = sb("ed_efs", [P, 2, G, F], F32)
        pst = t.enter_context(nc.psum_tensor("ps_ed_oht", [P, 1024], BF16))
        psa = t.enter_context(nc.psum_tensor("ps_ed_att", [P, 1024], BF16))
        psz = [t.enter_context(nc.psum_tensor(f"ps_z{b}", [P, 512], F32)) for b in range(2)]
        pso = [t.enter_context(nc.psum_tensor(f"ps_ed_o{b}", [P, 512], F32)) for b in range(2)]
        pss = [t.enter_context(nc.psum_tensor(f"ps_ed_s{b}", [P, 512], F32)) for b in range(2)]
        with nc.Block() as block:
            @block.sync
            def _(sp):
                sp.dma_start(w2[:, :], a["eW2"]).then_inc(s_w, 16)
                sp.dma_start(b2[:, :], row_vector(a["eb2"], F)).then_inc(s_w, 16)

            @block.gpsimd
            def _(pool):
                pool.memset(attr[:, :, :], 0.0).then_inc(s_pad, 1)

                def gather(g, r):
                    pool.wait_ge(s_idx, g + 1)
                    wait_count(pool, s_z, g - RING + 1)
                    pool.sem_inc(s_turn, 1)
                    for k in range(G):
                        pool.indirect_dma_start(bg[:, r, k, :], None, c.b_dram[:, :],
                                                bass.IndirectOffsetOnAxis(ap=idx[:, r, k:k + 1], axis=0)
                                                ).then_inc(s_b[r], 16)
                each_group(pool, gather)

            @block.vector
            def _(dve):
                dve.wait_ge(s_pad, 1)
                dve.wait_ge(s_w, 32)
                dve.memset(c.vals[:, :], 0.0).then_inc(s_add, 1)

                def front(g, r):
                    wait_count(dve, s_z, g - RING + 1)
                    wait_count(dve, s_ohf, g - RING + 1)
                    rec = c.rec[:, bass.ds(g * G, G), :]
                    dve.tensor_copy(idx[:, r, :], rec[:, :, C_DST]).then_inc(s_idx, 1)
                    lane_onehot(dve, c, rec[:, :, C_SL], oh[:, r]).then_inc(s_oh, 1)
                    dve.tensor_copy(attr[:, r, 0:K].rearrange("p (j x) -> p j x", j=3),
                                    parts[:, bass.ds(g * 6 * G, 6 * G)].unsqueeze(1).to_broadcast([P, 3, 6 * G])
                                    ).then_inc(s_at, 1)

                def middle(g, r):
                    b = r % 2
                    dve.wait_ge(s_oh, g + 1)
                    wait_count(dve, s_sum, g - 1)
                    dve.tensor_copy(ohf[:, b].rearrange("p k n -> p (k n)"),
                                    oh[:, r].rearrange("p k n -> p (k n)")).then_inc(s_ohf, 1)
                    dve.wait_ge(s_o, g + 1)
                    wait_count(dve, s_f, g - 1)
                    dve.tensor_tensor(ob[:, b, :].rearrange("p (k f) -> p k f", k=G),
                                      pso[b][:, :].rearrange("p (k f) -> p k f", k=G),
                                      b2[:, :].unsqueeze(1).to_broadcast([P, G, F]), ALU.add).then_inc(s_ob, 1)

                def back(g, r):
                    win = load_windows(dve, c, c.dve_regs, "src", g)
                    dve.wait_ge(s_sum, g + 1)
                    for k in range(G):
                        dve.wait_ge(s_add, G * g + k + 1)
                        acc = c.vals[:, bass.ds(win[k] * P, P)]
                        dve.tensor_tensor(acc, acc, pss[r % 2][:, k * P:(k + 1) * P], ALU.add).then_inc(s_add, 1)

                def step(g, r):
                    for by, work in ((2, front), (-1, middle), (-3, back)):
                        at, slot, there = group_at(g, r, by)
                        if there:
                            work(at, slot)
                each_group(dve, step, lead=2, lag=3)

            @block.scalar
            def _(act):
                def turned(g, r):
                    act.wait_ge(s_tr, g + 1)
                    wait_count(act, s_z, g - 1)
                    act.activation(oht[:, r % 2].rearrange("p k n -> p (k n)"), pst[:, 0:G * P],
                                   ACT.Copy).then_inc(s_oht, 1)
                    act.wait_ge(s_atr, g + 1)
                    act.activation(att[:, r % 2, :], psa[:, 0:P], ACT.Copy).then_inc(s_att, 1)

                def hidden(g, r):
                    act.wait_ge(s_z, g + 1)
                    wait_count(act, s_o, g - 1)
                    act.activation(h[:, r % 2, :], psz[r % 2][:, :], ACT.Silu).then_inc(s_h, 1)

                def feature(g, r):
                    act.wait_ge(s_ob, g + 1)
                    wait_count(act, s_sum, g - 1)
                    act.activation(ef[:, r % 2].rearrange("p k f -> p (k f)"), ob[:, r % 2, :],
                                   ACT.Silu).then_inc(s_f, 1)

                def step(g, r):
                    for by, work in ((1, turned), (0, hidden), (-1, feature)):
                        at, slot, there = group_at(g, r, by)
                        if there:
                            work(at, slot)
                each_group(act, step, lead=1, lag=1)

            @block.tensor
            def _(pe):
                pe.wait_ge(s_w, 32)

                def turn(g, r):
                    pe.wait_ge(s_oh, g + 1)
                    wait_count(pe, s_oht, g)
                    for k in range(G):
                        ins = pe.transpose(pst[:, k * P:(k + 1) * P], oh[:, r, k, :], c.identb[:, :])
                    ins.then_inc(s_tr, 1)
                    pe.wait_ge(s_at, g + 1)
                    wait_count(pe, s_att, g)
                    pe.transpose(psa[:, 0:P], attr[:, r, :], c.identb[:, :]).then_inc(s_atr, 1)

                def inputs(g, r):
                    b = r % 2
                    win = load_windows(pe, c, c.pe_regs, "src", g)
                    pe.wait_ge(s_oht, g + 1)
                    pe.wait_ge(s_att, g + 1)
                    wait_count(pe, s_h, g - 1)
                    pe.wait_ge(s_b[r], ring_count(g, r, 16 * G))
                    for k in range(G):
                        z = psz[b][:, k * P:(k + 1) * P]
                        pe.matmul(z, wc[:, k, :], att[:, b, :], start=True, stop=False)
                        for j in range(3):
                            pe.matmul(z, c.tab[:, j, bass.ds(win[k] * F, F)], oht[:, b, k, :],
                                      start=False, stop=False)
                        ins = pe.matmul(z, bg[:, r, k, :], c.ident[:, :], start=False, stop=True)
                    ins.then_inc(s_z, 1)

                def second(g, r):
                    b = r % 2
                    pe.wait_ge(s_h, g + 1)
                    wait_count(pe, s_ob, g - 1)
                    for k in range(G):
                        ins = pe.matmul(pso[b][:, k * F:(k + 1) * F], h[:, b, k * P:(k + 1) * P], w2[:, :],
                                        start=True, stop=True)
                    ins.then_inc(s_o, 1)

                def sums(g, r):
                    b = r % 2
                    pe.wait_ge(s_f, g + 1)
                    pe.wait_ge(s_ohf, g + 1)
                    wait_count(pe, s_add, G * (g - 1) + 1)
                    for k in range(G):
                        ins = pe.matmul(pss[b][:, k * P:(k + 1) * P], ef[:, b, k, :], ohf[:, b, k, :],
                                        start=True, stop=True)
                    ins.then_inc(s_sum, 1)

                def step(g, r):
                    for by, work in ((1, turn), (0, inputs), (-1, second), (-2, sums)):
                        at, slot, there = group_at(g, r, by)
                        if there:
                            work(at, slot)
                each_group(pe, step, lead=1, lag=2)


def nodes2(c, a, out):
    nc = c.nc
    names = "n2_weights n2_pre n2_hid n2_o n2_res n2_sum n2_stats n2_moments n2_std n2_rstd n2_y n2_turn n2_set"
    (s_w, s_pre, s_hid, s_o, s_res, s_sum, s_st, s_mv, s_std, s_rstd, s_y, s_dturn, s_set) = semaphores(nc, c.sems, names)
    s_x = semaphores(nc, c.sems, "n2_x0 n2_x1")
    s_out = semaphores(nc, c.sems, "n2_out0 n2_out1")
    with ExitStack() as t:
        sb = lambda n, s, d: t.enter_context(nc.sbuf_tensor(n, s, d))
        wx = sb("w_nx", [P, F], F32)
        wa = sb("w_na", [P, F], F32)
        w2 = sb("w_n2", [P, F], F32)
        b1 = sb("b_n1", [P, 1], F32)
        b2 = sb("b_n2", [P, F], F32)
        xr = sb("n2_xr", [P, 2, F], F32)
        hid = sb("n2_hids", [P, 2, P], F32)
        res = sb("n2_ress", [P, F], F32)
        stats = sb("n2_statss", [P, nc.vector.BN_STATS_DIM], F32)
        mv = sb("n2_mvs", [P, nc.vector.BN_AGGR_DIM], F32)
        std = sb("n2_stds", [P, 1], F32)
        rstd = sb("n2_rstds", [P, 1], F32)
        eps = sb("n2_eps", [P, 1], F32)
        y = sb("n2_ys", [P, 2, F], F32)
        psh = [t.enter_context(nc.psum_tensor(f"ps_h{b}", [P, 512], F32)) for b in range(2)]
        pso = [t.enter_context(nc.psum_tensor(f"ps_n2o{b}", [P, 512], F32)) for b in range(2)]
        with nc.Block() as block:
            @block.gpsimd
            def _(pool):
                pool.memset(eps[:, :], EPS).then_inc(s_set, 1)
                pool.memset(xr[:, :, :], 0.0).then_inc(s_set, 1)

            @block.sync
            def _(sp):
                sp.dma_start(wx[:, :], a["nW1"][0:F, :]).then_inc(s_w, 16)
                sp.dma_start(wa[:, :], a["nW1"][F:2 * F, :]).then_inc(s_w, 16)
                sp.dma_start(w2[:, :], a["nW2"]).then_inc(s_w, 16)
                sp.dma_start(b1[:, :], a["nb1"].rearrange("(n o) -> n o", o=1)).then_inc(s_w, 16)
                sp.dma_start(b2[:, :], row_vector(a["nb2"], F)).then_inc(s_w, 16)

                def load(w, b):
                    wait_count(sp, s_res, w - 1)
                    sp.dma_start(xr[:, b, :], c.x1_dram[bass.ds(w * P, P), :]).then_inc(s_x[b], 16)

                def store(w, b, rows=P):
                    sp.wait_ge(s_y, w + 1)
                    sp.dma_start(out[bass.ds(w * P, rows), :], y[0:rows, b, :]).then_inc(s_out[b], 16)
                sp.wait_ge(s_set, 2)
                load(0, 0)
                load(1, 1)
                with sp.Fori(0, NW // 2 - 1) as i:
                    for b in range(2):
                        store(2 * i + b, b)
                        load(2 * i + 2 + b, b)
                store(NW - 3, 0)
                load(NW - 1, 0)
                store(NW - 2, 1)
                store(NW - 1, 0, LAST)
                for b in range(2):
                    sp.wait_ge(s_out[b], 16 * (NW // 2 + 1 - b))

            @block.tensor
            def _(pe):
                pe.wait_ge(s_w, 80)

                def window(w, b, use):
                    wait_count(pe, s_hid, w - 1)
                    cols = bass.ds(w * P, P)
                    pe.matmul(psh[b][:, 0:P], wx[:, :], c.x1t[:, cols], start=True, stop=False)
                    pe.matmul(psh[b][:, 0:P], wa[:, :], c.vals[:, cols], start=False, stop=True).then_inc(s_pre, 1)
                    pe.wait_ge(s_hid, w + 1)
                    wait_count(pe, s_res, w - 1)
                    pe.matmul(pso[b][:, 0:F], hid[:, b, :], w2[:, :], start=True, stop=True).then_inc(s_o, 1)
                each_window(pe, window)

            @block.scalar
            def _(act):
                act.wait_ge(s_w, 80)
                act.wait_ge(s_set, 2)

                def window(w, b, use):
                    act.wait_ge(s_pre, w + 1)
                    wait_count(act, s_o, w - 1)
                    act.activation(hid[:, b, :], psh[b][:, 0:P], ACT.Silu, bias=b1[:, 0:1]).then_inc(s_hid, 1)
                    act.wait_ge(s_mv, w + 1)
                    wait_count(act, s_rstd, w)
                    act.activation(std[:, :], mv[:, 1:2], ACT.Sqrt, bias=eps[:, 0:1]).then_inc(s_std, 1)
                each_window(act, window)

            @block.vector
            def _(dve):
                dve.wait_ge(s_w, 80)

                def window(w, b, use):
                    dve.wait_ge(s_x[b], 16 * use)
                    dve.wait_ge(s_o, w + 1)
                    wait_count(dve, s_y, w)
                    dve.tensor_tensor(res[:, :], pso[b][:, 0:F], xr[:, b, :], ALU.add).then_inc(s_res, 1)
                    dve.wait_ge(s_res, w + 1)
                    dve.tensor_tensor(res[:, :], res[:, :], b2[:, :], ALU.add).then_inc(s_sum, 1)
                    dve.wait_ge(s_sum, w + 1)
                    normalise(dve, c, w, res, stats, mv, std, rstd, (s_st, s_mv, s_std, s_rstd, s_dturn))
                    wait_count(dve, s_out[b], 16 * (use - 1))
                    dve.tensor_scalar(y[:, b, :], res[:, :], mv[:, 0:1], rstd[:, 0:1], ALU.subtract,
                                      ALU.mult).then_inc(s_y, 1)
                each_window(dve, window)


def clear_semaphores(c, sems):
    nc = c.nc
    with nc.Block() as block:
        @block.gpsimd
        def _(pool):
            for s in sems:
                pool.sem_clear(s)


def program(nc, a, out):
    with ExitStack() as stack:
        c = Ctx()
        c.nc, c.stack = nc, stack
        dram = lambda n, s: nc.dram_tensor(n, s, F32, kind="Internal").ap()
        c.k_dram = dram("k_rows_dram", [NP, F])
        c.b_dram = dram("b_rows_dram", [NP, F])
        c.x1_dram = dram("x1_rows_dram", [NP, F])
        c.rec_dram = dram("records_dram", [P, NT * R])
        c.rec_rows = c.rec_dram.rearrange("p (t r) -> (p t) r", r=R)
        c.row_dram = dram("contributions_dram", [P, NT * CW])
        c.row_rows = c.row_dram.rearrange("p (t r) -> (p t) r", r=CW)
        c.pe_regs = [nc.tensor.alloc_register(f"pe_window{k}") for k in range(2 * G)]
        c.dve_regs = [nc.vector.alloc_register(f"dve_window{k}") for k in range(2 * G)]
        sb = lambda st, n, s, d: st.enter_context(nc.sbuf_tensor(n, s, d))
        with Epoch() as c.sems:
            constants(c)
            c.work = sb(stack, "work", [P, NP], F32)
            c.vals = sb(stack, "vals", [P, NP], F32)
            c.tab = sb(stack, "tab", [P, 3, NP], BF16)
            project(c, a)
            split_table(c, 0.25)
            with ExitStack() as st:
                e = Ctx()
                e.ids = {s: sb(st, "ids_" + s, [P, ET], I32) for s in SIDES}
                e.hi = {s: sb(st, "win_of_" + s, [P, ET], F32) for s in SIDES}
                e.run = {s: sb(st, "run_" + s, [P, 2, NW], F32) for s in SIDES}
                e.rec = sb(st, "record", [P, ET, R], F32)
                c.rfill = sb(st, "rfill", [P, RF, R], F32)
                c.fill = sb(st, "cfill", [P, CF, CW], F32)
                with ExitStack() as st2:
                    e.tmpi = sb(st2, "tmp_int", [P, 2, ET], I32)
                    e.attr = sb(st2, "attr_in", [P, ET * 2], F32)
                    e.mask = sb(st2, "mask_in", [P, ET * H], F32)
                    load_edges(c, a, e)
                count_windows(c, e)
                place_edges(c, e)
            c.rec = sb(stack, "records", [P, NT, R], F32)
            with ExitStack() as st:
                c.sc = sb(st, "scores", [P, NT * H], F32)
                load_records(c)
                score(c)
                exps(c)
                normalise_values(c)
                split_table(c)
                weigh(c)
            clear_semaphores(c, c.sems.taken)
        with ExitStack() as c.sems:
            collect(c)
            c.x1t = sb(stack, "x1t", [P, NP], F32)
            nodes1(c, a)
            split_table(c)
            edges(c, a)
            nodes2(c, a, out)


def kernel(**inputs):
    import numpy as np
    import concourse.bacc as bacc
    from concourse.bass_utils import run_bass_kernel_spmd

    given = {k.split("gnn_")[-1]: np.asarray(v) for k, v in inputs.items()}
    given["xT"] = given["x"].T
    for w in ("Wq", "Wk", "Wv", "Wo"):
        given[w + "T"] = given.pop(w).T
    nc = bacc.Bacc("TRN2", target_bir_lowering=False, num_devices=1)
    arrays, a = {}, {}
    for name, v in given.items():
        v = np.ascontiguousarray(v)
        arrays[f"in_{name}_dram"] = v
        a[name] = nc.dram_tensor(f"in_{name}_dram", v.shape, mybir.dt.from_np(v.dtype), kind="ExternalInput").ap()
    out = nc.dram_tensor("out_dram", (N, F), F32, kind="ExternalOutput").ap()
    program(nc, a, out)
    r = run_bass_kernel_spmd(nc, [arrays], core_ids=[0])
    return r.results[0]["out_dram"]
```

```python
from contextlib import ExitStack

import concourse.bass as bass
from concourse import mybir

ALU = mybir.AluOpType
ACT = mybir.ActivationFunctionType
AX_X = mybir.AxisListType.X
F32 = mybir.dt.float32
BF16 = mybir.dt.bfloat16
I32 = mybir.dt.int32

P = 128
N = 6250
E = 100000
F = 128
H = 8
D = F // H
NW = -(-N // P)
NP = NW * P
LAST = N - (NW - 1) * P
EL = 125
ET = E // EL
G = 4
NT = -(-(E // P + NW) // (2 * G)) * 2 * G
SLOTS = NT * P
PAIRS = NT // (2 * G)
R = 16
C_ATTR, C_DST, C_SL, C_DL, C_ROW = 8, 10, 11, 12, 13
CW = 132
NOROW = float(1 << 20)
BIG = float(2 ** 100)
EPS = 1e-5
PG = 8
PB = ET // PG
EC = 10
RF = NT // 16
CF = 8


class Ctx:
    pass


def semaphores(nc, stack, names):
    return [stack.enter_context(nc.semaphore(n)) for n in names.split()]


class Epoch(ExitStack):

    def enter_context(self, context):
        got = super().enter_context(context)
        self.taken = [*self.taken, got] if hasattr(self, "taken") else [got]
        return got


def wait_count(eng, sem, count):
    if not isinstance(count, int) or count > 0:
        eng.wait_ge(sem, count)


def constants(c):
    nc, k = c.nc, c.stack
    sb = lambda n, s, d: k.enter_context(nc.sbuf_tensor(n, s, d))
    c.iota = sb("iota", [P, P], F32)
    c.ident = sb("ident", [P, P], F32)
    c.identb = sb("identb", [P, P], BF16)
    c.bigid = sb("bigid", [P, P], BF16)
    c.tri = sb("tri", [P, P], BF16)
    c.ones = sb("ones", [P, P], BF16)
    c.mtab = sb("mtab", [P, NW * H], F32)
    c.dtab = sb("dtab", [P, NW * H], F32)
    c.win = {s: sb("win_" + s, [1, NT], I32) for s in ("src", "dst")}
    (s_set,) = semaphores(nc, c.sems, "const_set")
    with ExitStack() as t:
        ii = t.enter_context(nc.sbuf_tensor("iota_int", [P, P], I32))
        with nc.Block() as block:
            @block.gpsimd
            def _(pool):
                pool.iota(ii[:, :], pattern=[[1, P]], base=0, channel_multiplier=0).then_inc(s_set, 1)
                pool.memset(c.ident[:, :], 0.0).then_inc(s_set, 1)
                pool.memset(c.identb[:, :], 0.0).then_inc(s_set, 1)
                pool.memset(c.bigid[:, :], 0.0).then_inc(s_set, 1)
                pool.memset(c.tri[:, :], 1.0).then_inc(s_set, 1)
                pool.memset(c.ones[:, :], 1.0).then_inc(s_set, 1)
                pool.wait_ge(s_set, 6)
                pool.tensor_copy(c.iota[:, :], ii[:, :])
                for m, v in ((c.ident, 1.0), (c.identb, 1.0), (c.bigid, BIG)):
                    pool.affine_select(out=m[:, :], in_=m[:, :], compare_op=ALU.not_equal, fill=v, base=0,
                                       pattern=[[-1, P]], channel_multiplier=1)
                pool.affine_select(out=c.tri[:, :], in_=c.tri[:, :], compare_op=ALU.is_gt, fill=0.0, base=0,
                                   pattern=[[1, P]], channel_multiplier=-1)


def project(c, a):
    nc = c.nc
    s_w, s_bias, s_x0, s_x1, s_mm0, s_mm1, s_q0, s_q1, s_k0, s_k1 = semaphores(
        nc, c.sems, "w_in bias_in x_in0 x_in1 qkv_ready0 qkv_ready1 qkv_read0 qkv_read1 k_out0 k_out1")
    s_x, s_mm, s_q, s_k = (s_x0, s_x1), (s_mm0, s_mm1), (s_q0, s_q1), (s_k0, s_k1)
    with ExitStack() as t:
        w = t.enter_context(nc.sbuf_tensor("w_qkv", [P, 3 * F], F32))
        bias = t.enter_context(nc.sbuf_tensor("b_qkv", [P, 3 * F], F32))
        xt = t.enter_context(nc.sbuf_tensor("xt", [P, 2, P], F32))
        kt = t.enter_context(nc.sbuf_tensor("k_rows", [P, 2, F], F32))
        ps = [t.enter_context(nc.psum_tensor(f"ps_qkv{b}", [P, 512], F32)) for b in range(2)]
        with nc.Block() as block:
            @block.sync
            def _(sp):
                for j, (m, v) in enumerate((("WqT", "bq"), ("WkT", "bk"), ("WvT", "bv"))):
                    sp.dma_start(w[:, j * F:(j + 1) * F], a[m]).then_inc(s_w, 16)
                    sp.dma_start(bias[:, j * F:(j + 1) * F],
                                 a[v].rearrange("(o n) -> o n", o=1).to_broadcast([P, F])).then_inc(s_bias, 16)

                def load(win, n, cols):
                    sp.dma_start(xt[:, n, 0:cols], a["xT"][:, bass.ds(win * P, cols)]).then_inc(s_x[n], 16)

                def store(win, n, use):
                    sp.wait_ge(s_q[n], 3 * use)
                    sp.dma_start(c.k_dram[bass.ds(win * P, P), :], kt[:, n, :]).then_inc(s_k[n], 16)
                load(0, 0, P)
                load(1, 1, P)
                with sp.Fori(0, NW // 2 - 1) as i:
                    for n in range(2):
                        store(2 * i + n, n, i + 1)
                        load(2 * i + 2 + n, n, P)
                store(NW - 3, 0, NW // 2)
                load(NW - 1, 0, LAST)
                store(NW - 2, 1, NW // 2)
                store(NW - 1, 0, NW // 2 + 1)
                sp.wait_ge(s_k[0], 16 * (NW // 2 + 1))
                sp.wait_ge(s_k[1], 16 * (NW // 2))

            @block.tensor
            def _(pe):
                pe.wait_ge(s_w, 48)

                def mm(n, use, first):
                    pe.wait_ge(s_x[n], 16 * use)
                    if not first:
                        pe.wait_ge(s_q[n], 3 * (use - 1))
                    pe.matmul(ps[n][:, 0:3 * F], xt[:, n, :], w[:, :], start=True, stop=True).then_inc(s_mm[n], 1)
                for n in range(2):
                    mm(n, 1, True)
                with pe.Fori(2, NW // 2 + 1) as i:
                    for n in range(2):
                        mm(n, i, False)
                mm(0, NW // 2 + 1, False)

            @block.vector
            def _(dve):
                dve.wait_ge(s_bias, 48)

                def out(win, n, use, first):
                    dve.wait_ge(s_mm[n], use)
                    if not first:
                        dve.wait_ge(s_k[n], 16 * (use - 1))
                    cols = bass.ds(win * F, F)
                    dve.tensor_tensor(kt[:, n, :], ps[n][:, F:2 * F], bias[:, F:2 * F], ALU.add).then_inc(s_q[n], 1)
                    dve.tensor_tensor(c.work[:, cols], ps[n][:, 0:F], bias[:, 0:F], ALU.add).then_inc(s_q[n], 1)
                    dve.tensor_tensor(c.vals[:, cols], ps[n][:, 2 * F:3 * F], bias[:, 2 * F:3 * F],
                                      ALU.add).then_inc(s_q[n], 1)
                for n in range(2):
                    out(n, n, 1, True)
                with dve.Fori(1, NW // 2) as i:
                    for n in range(2):
                        out(2 * i + n, n, i + 1, False)
                out(NW - 1, 0, NW // 2 + 1, False)


def split_table(c, scale=None):
    nc = c.nc
    c.splits = c.splits + 1 if hasattr(c, "splits") else 0
    s_part, s_rest = semaphores(nc, c.sems, f"part{c.splits} rest{c.splits}")
    with nc.Block() as block:
        @block.vector
        def _(dve):
            n = 0
            if scale is not None:
                dve.tensor_scalar(c.work[:, :], c.work[:, :], scale, None, ALU.mult).then_inc(s_rest, 1)
                dve.wait_ge(s_rest, 1)
                n = 1
            for j in range(3):
                dve.tensor_copy(c.tab[:, j, :], c.work[:, :]).then_inc(s_part, 1)
                if j < 2:
                    dve.wait_ge(s_part, j + 1)
                    dve.tensor_tensor(c.work[:, :], c.work[:, :], c.tab[:, j, :], ALU.subtract).then_inc(s_rest, 1)
                    dve.wait_ge(s_rest, n + j + 1)


SIDES = ("src", "dst")


def load_edges(c, a, e):
    nc = c.nc
    s_def, s_in, s_win, s_lane = semaphores(nc, c.sems, "defaults_set edges_in window_of lane_of")
    (s_fill,) = semaphores(nc, c.stack, "fill_out")
    s_zero, s_rcopy = semaphores(nc, c.sems, "fill_zeroed record_parts")
    c.s_fill = s_fill
    with nc.Block() as block:
        @block.gpsimd
        def _(pool):
            for s in SIDES:
                pool.memset(e.ids[s][:, :], NW * P).then_inc(s_def, 1)
            pool.memset(e.attr[:, :], 0.0).then_inc(s_def, 1)
            pool.memset(e.mask[:, :], 0.0).then_inc(s_def, 1)
            pool.memset(e.rec[:, :, C_ROW:R], 0.0).then_inc(s_def, 1)
            pool.memset(c.rfill[:, :, :], 0.0).then_inc(s_zero, 1)
            pool.memset(c.fill[:, :, :], 0.0).then_inc(s_zero, 1)
            pool.wait_ge(s_zero, 2)
            pool.memset(c.rfill[:, :, C_SL:C_SL + 1], -1.0).then_inc(s_def, 1)
            pool.memset(c.rfill[:, :, C_ROW:C_ROW + 1], NOROW).then_inc(s_def, 1)
            pool.memset(c.fill[:, :, F:F + 1], -1.0).then_inc(s_def, 1)

        @block.sync
        def _(sp):
            sp.wait_ge(s_def, 8)
            for s in SIDES:
                sp.dma_start(e.ids[s][0:EL, :], a[s].rearrange("(p t) -> p t", p=EL)).then_inc(s_in, 16)
            sp.dma_start(e.attr[0:EL, :], a["edge_attr_2"].rearrange("(p t) c -> p (t c)", p=EL)).then_inc(s_in, 16)
            sp.dma_start(e.mask[0:EL, :], a["edge_attr_8"].rearrange("(p t) c -> p (t c)", p=EL)).then_inc(s_in, 16)
            for j in range(NT // RF):
                sp.dma_start(c.rec_dram[:, j * RF * R:(j + 1) * RF * R],
                             c.rfill[:, :, :].rearrange("p t r -> p (t r)")).then_inc(s_fill, 16)
            for j in range(NT // CF):
                sp.dma_start(c.row_dram[:, j * CF * CW:(j + 1) * CF * CW],
                             c.fill[:, :, :].rearrange("p t r -> p (t r)")).then_inc(s_fill, 16)

        @block.vector
        def _(dve):
            dve.wait_ge(s_in, 64)
            for n, s in enumerate(SIDES):
                dve.tensor_scalar(e.tmpi[:, n, :], e.ids[s][:, :], 7, None, ALU.arith_shift_right).then_inc(s_win, 1)
                dve.wait_ge(s_win, 2 * n + 1)
                dve.tensor_copy(e.hi[s][:, :], e.tmpi[:, n, :]).then_inc(s_win, 1)
                dve.wait_ge(s_win, 2 * n + 2)
                dve.tensor_scalar(e.tmpi[:, n, :], e.ids[s][:, :], P - 1, None, ALU.bitwise_and).then_inc(s_lane, 1)
                dve.wait_ge(s_lane, 2 * n + 1)
                col = C_SL if s == "src" else C_DL
                dve.tensor_copy(e.rec[:, :, col], e.tmpi[:, n, :]).then_inc(s_lane, 1)
            dve.tensor_copy(e.rec[:, :, C_DST], e.ids["dst"][:, :]).then_inc(s_rcopy, 1)

        @block.scalar
        def _(act):
            act.wait_ge(s_in, 64)
            act.activation(e.rec[:, :, 0:H], e.mask[:, :].rearrange("p (t h) -> p t h", h=H), ACT.Copy).then_inc(s_rcopy, 1)
            act.activation(e.rec[:, :, C_ATTR:C_ATTR + 2], e.attr[:, :].rearrange("p (t h) -> p t h", h=2),
                           ACT.Copy).then_inc(s_rcopy, 1)


def windows_onehot(dve, c, e, s, t0, n, out):
    return dve.tensor_tensor(out, e.hi[s][:, bass.ds(t0, n)].unsqueeze(2).to_broadcast([P, n, NW]),
                             c.iota[:, 0:NW].unsqueeze(1).to_broadcast([P, n, NW]), ALU.is_equal)


def count_windows(c, e):
    nc = c.nc
    s_oh0, s_oh1, s_mm0, s_mm1, s_sum, s_step, s_turn, s_past, s_row = semaphores(
        nc, c.sems, "count_onehot0 count_onehot1 counted0 counted1 window_sums base_step ends_turned tile_past tile_windows")
    s_oh, s_mm = (s_oh0, s_oh1), (s_mm0, s_mm1)
    (s_z, s_io) = semaphores(nc, c.sems, "zero_set tile_iota")
    with ExitStack() as t:
        sb = lambda n, s, d: t.enter_context(nc.sbuf_tensor(n, s, d))
        oh = sb("count_oh", [P, 2, EC, NW], BF16)
        zero = sb("count_zero", [P, 512], BF16)
        cnt = sb("cnt", [P, 2, NW], F32)
        cnti = sb("cnti", [P, 2, NW], I32)
        cnti2 = sb("cnti2", [P, 2, NW], I32)
        til = sb("tiles", [P, 2, NW], F32)
        ends = sb("ends", [P, 2, NW], F32)
        endc = sb("end_col", [P, 2], F32)
        one = sb("one_f", [P, NW], F32)
        past = sb("past", [P, 2, NT], BF16)
        tio = sb("tile_io", [P, NT], F32)
        tii = sb("tile_ii", [P, NT], I32)
        ps_c = [t.enter_context(nc.psum_tensor(f"ps_count{n}", [P, 512], F32)) for n in range(2)]
        ps_e = t.enter_context(nc.psum_tensor("ps_ends", [P, 512], F32))
        ps_w = [t.enter_context(nc.psum_tensor(f"ps_win{n}", [P, 512], F32)) for n in range(4)]
        IT = ET // EC
        HT = NT // 2
        with nc.Block() as block:
            @block.gpsimd
            def _(pool):
                pool.memset(zero[:, :], 0.0).then_inc(s_z, 1)
                pool.memset(one[:, :], 1.0).then_inc(s_z, 1)
                pool.memset(endc[:, :], 1e9).then_inc(s_z, 1)
                pool.iota(tii[:, :], pattern=[[1, NT]], base=0, channel_multiplier=0).then_inc(s_io, 1)
                pool.wait_ge(s_io, 1)
                pool.tensor_copy(tio[:, :], tii[:, :]).then_inc(s_io, 1)

            @block.vector
            def _(dve):
                def one_hot(i, n, first):
                    if not first:
                        dve.wait_ge(s_mm[n], i)
                    windows_onehot(dve, c, e, SIDES[n], i * EC, EC, oh[:, n]).then_inc(s_oh[n], 1)
                for n in range(2):
                    one_hot(0, n, True)
                with dve.Fori(1, IT) as i:
                    for n in range(2):
                        one_hot(i, n, False)
                for n in range(2):
                    dve.wait_ge(s_mm[n], IT + 1)
                    dve.tensor_reduce(cnt[:, n, :], ps_c[n][:, 0:EC * NW].rearrange("p (j w) -> p w j", w=NW),
                                      AX_X, ALU.add).then_inc(s_sum, 1)
                dve.wait_ge(s_sum, 2)
                dve.wait_ge(s_z, 3)
                steps = [0]

                def step(ins):
                    steps[0] += 1
                    ins.then_inc(s_step, 1)
                    dve.wait_ge(s_step, steps[0])
                step(dve.tensor_scalar(cnti[:, :, :], cnt[:, :, :], float(P - 1), None, ALU.add))
                step(dve.tensor_scalar(cnti2[:, :, :], cnti[:, :, :], 7, None, ALU.arith_shift_right))
                step(dve.tensor_copy(til[:, :, :], cnti2[:, :, :]))
                for n in range(2):
                    step(dve.tensor_tensor_scan(ends[:, n, :], one[:, :], til[:, n, :], 0.0, ALU.mult, ALU.add))
                step(dve.tensor_tensor(til[:, :, :], ends[:, :, :], til[:, :, :], ALU.subtract))
                for n in range(2):
                    step(dve.tensor_scalar(e.run[SIDES[n]][:, 0, :], til[:, n, :], float(P), None, ALU.mult))
                dve.wait_ge(s_turn, 2)
                for n in range(2):
                    step(dve.tensor_copy(endc[0:NW, n:n + 1], ps_e[0:NW, n * P:n * P + 1]))
                dve.wait_ge(s_io, 2)
                for n in range(2):
                    dve.tensor_scalar(past[:, n, :], tio[:, :], endc[:, n:n + 1], None, ALU.is_ge).then_inc(s_past, 1)
                for n in range(2):
                    for h in range(2):
                        dve.wait_ge(s_row, 2 * n + h + 1)
                        dve.tensor_scalar(c.win[SIDES[n]][0:1, h * HT:(h + 1) * HT], ps_w[2 * n + h][0:1, 0:HT],
                                          float(NW - 1), None, ALU.min)

            @block.tensor
            def _(pe):
                pe.wait_ge(s_z, 3)
                for n in range(2):
                    pe.matmul(ps_c[n][:, 0:EC * NW], c.ones[:, :], zero[:, 0:EC * NW], start=True, stop=False)
                with pe.Fori(0, IT) as i:
                    for n in range(2):
                        pe.wait_ge(s_oh[n], i + 1)
                        pe.matmul(ps_c[n][:, 0:EC * NW], c.ones[:, :], oh[:, n].rearrange("p j w -> p (j w)"),
                                  start=False, stop=False, skip_group_check=True).then_inc(s_mm[n], 1)
                for n in range(2):
                    pe.matmul(ps_c[n][:, 0:EC * NW], c.ones[:, :], zero[:, 0:EC * NW], start=False,
                              stop=True).then_inc(s_mm[n], 1)
                pe.wait_ge(s_step, 5)
                for n in range(2):
                    pe.transpose(ps_e[0:NW, n * P:(n + 1) * P], ends[:, n, :], c.ident[:, :]).then_inc(s_turn, 1)
                for n in range(2):
                    pe.wait_ge(s_past, n + 1)
                    for h in range(2):
                        pe.matmul(ps_w[2 * n + h][:, 0:HT], c.ones[:, :], past[:, n, h * HT:(h + 1) * HT],
                                  start=True, stop=True).then_inc(s_row, 1)


def place_edges(c, e):
    nc = c.nc
    names = ("place_onehot before after_start masked slot running slot_int slot_lane slot_tile lane_part tile_part "
             "row_of rec_slot row_index")
    (s_oh, s_cum, s_add, s_msk, s_slot, s_run, s_int, s_lane, s_tile, s_lp, s_tp, s_row, s_rec, s_idx) = semaphores(
        nc, c.sems, names)
    s_sent = semaphores(nc, c.stack, "records_sent0 records_sent1")
    (s_turn, s_init) = semaphores(nc, c.sems, "scatter_turn place_init")
    IT = ET // PG
    with ExitStack() as t:
        sb = lambda n, s, d: t.enter_context(nc.sbuf_tensor(n, s, d))
        oh = {s: sb("place_oh_" + s, [P, PG + 1, NW], BF16) for s in SIDES}
        cum = {s: sb("cum_" + s, [P, PG, NW], F32) for s in SIDES}
        slot = sb("slot", [P, 2, PG], F32)
        sloti = sb("sloti", [P, 2, PG], I32)
        lane = sb("slot_lane_i", [P, 2, PG], I32)
        tile = sb("slot_tile_i", [P, 2, PG], I32)
        lanef = sb("slot_lane_f", [P, 2, PG], F32)
        row = sb("row_f", [P, 2, PG], F32)
        idx = sb("row_idx", [P, 2, PG], I32)
        out = sb("rec_out", [P, 2, PG, R], F32)
        norow = sb("norow", [P, 1], F32)
        lanes = sb("lanes_i", [P, 1], I32)
        ps = {s: t.enter_context(nc.psum_tensor("ps_before_" + s, [P, 512], F32)) for s in SIDES}
        with nc.Block() as block:
            @block.vector
            def _(dve):
                dve.wait_ge(s_init, 4)

                def place(g, half):
                    for n, s in enumerate(SIDES):
                        wait_count(dve, s_cum, 2 * g)
                        windows_onehot(dve, c, e, s, g * PG, PG, oh[s][:, 0:PG]).then_inc(s_oh, 1)
                    for n, s in enumerate(SIDES):
                        dve.wait_ge(s_cum, 2 * g + n + 1)
                        start = e.run[s][:, half:half + 1, :]
                        dve.tensor_tensor(cum[s][:, :, :], ps[s][:, 0:PG * NW].rearrange("p (j w) -> p j w", w=NW),
                                          start.to_broadcast([P, PG, NW]), ALU.add).then_inc(s_add, 1)
                        dve.tensor_tensor(e.run[s][:, 1 - half, :], ps[s][:, PG * NW:(PG + 1) * NW],
                                          e.run[s][:, half, :], ALU.add).then_inc(s_run, 1)
                        dve.wait_ge(s_add, 2 * g + n + 1)
                        dve.tensor_tensor(cum[s][:, :, :], cum[s][:, :, :], oh[s][:, 0:PG], ALU.mult).then_inc(s_msk, 1)
                        dve.wait_ge(s_msk, 2 * g + n + 1)
                        dve.tensor_reduce(slot[:, n, :], cum[s][:, :, :], AX_X, ALU.add).then_inc(s_slot, 1)
                    dve.wait_ge(s_slot, 2 * g + 2)
                    dve.wait_ge(s_run, 2 * g + 2)
                    dve.tensor_copy(sloti[:, :, :], slot[:, :, :]).then_inc(s_int, 1)
                    dve.wait_ge(s_int, g + 1)
                    dve.tensor_scalar(lane[:, :, :], sloti[:, :, :], P - 1, None, ALU.bitwise_and).then_inc(s_lane, 1)
                    dve.tensor_scalar(tile[:, :, :], sloti[:, :, :], 7, None, ALU.arith_shift_right).then_inc(s_tile, 1)
                    dve.wait_ge(s_lane, g + 1)
                    dve.tensor_scalar(lanef[:, :, :], lane[:, :, :], float(NT), norow[:, 0:1], ALU.mult,
                                      ALU.add).then_inc(s_lp, 1)
                    dve.wait_ge(s_lp, g + 1)
                    dve.wait_ge(s_tile, g + 1)
                    wait_count(dve, s_sent[half], 8 * PG * (g - half))
                    dve.tensor_tensor(idx[:, half, :], lanef[:, 0, :], tile[:, 0, :], ALU.add).then_inc(s_idx, 1)
                    dve.tensor_copy(out[:, half, :, :], e.rec[:, bass.ds(g * PG, PG), :]).then_inc(s_rec, 1)
                    dve.wait_ge(s_rec, g + 1)
                    dve.tensor_tensor(out[:, half, :, C_ROW], lanef[:, 1, :], tile[:, 1, :], ALU.add).then_inc(s_row, 1)
                    dve.wait_ge(s_row, g + 1)
                place(0, 0)
                place(1, 1)
                with dve.Fori(1, IT // 2) as i:
                    place(2 * i, 0)
                    place(2 * i + 1, 1)

            @block.tensor
            def _(pe):
                pe.wait_ge(s_init, 4)

                def before(g):
                    for n, s in enumerate(SIDES):
                        pe.wait_ge(s_oh, 2 * g + n + 1)
                        wait_count(pe, s_run, 2 * g)
                        wait_count(pe, s_add, 2 * g)
                        flat = oh[s][:, :, :].rearrange("p j w -> p (j w)")
                        pe.matmul(ps[s][:, 0:(PG + 1) * NW], c.tri[:, :], flat, start=True, stop=False)
                        for j in range(PG):
                            m = PG - j
                            ins = pe.matmul(ps[s][:, (j + 1) * NW:(PG + 1) * NW].rearrange("p (j w) -> p j w", w=NW),
                                            c.ones[:, :], oh[s][:, j:j + 1, :].to_broadcast([P, m, NW]),
                                            start=False, stop=(j == PG - 1))
                        ins.then_inc(s_cum, 1)
                before(0)
                with pe.Fori(1, IT) as g:
                    before(g)

            @block.gpsimd
            def _(pool):
                for s in SIDES:
                    pool.memset(oh[s][:, PG:PG + 1, :], 0.0).then_inc(s_init, 1)
                pool.iota(lanes[:, :], pattern=[[0, 1]], base=0, channel_multiplier=1).then_inc(s_init, 1)
                pool.wait_ge(s_init, 3)
                pool.tensor_scalar(norow[:, :], lanes[:, :], float(EL), NOROW, ALU.is_ge, ALU.mult).then_inc(s_init, 1)
                pool.wait_ge(c.s_fill, 16 * (NT // RF + NT // CF))

                def send(g, half):
                    pool.wait_ge(s_row, g + 1)
                    pool.wait_ge(s_idx, g + 1)
                    pool.sem_inc(s_turn, 1)
                    for j in range(PG):
                        pool.indirect_dma_start(
                            c.rec_rows, bass.IndirectOffsetOnAxis(ap=idx[:, half, j:j + 1], axis=0),
                            out[:, half, j, :], None, bounds_check=SLOTS - 1, oob_is_err=False).then_inc(s_sent[half], 16)
                with pool.Fori(0, IT // 2) as i:
                    for half in range(2):
                        send(2 * i + half, half)
                for half in range(2):
                    pool.wait_ge(s_sent[half], 16 * PG * (IT // 2))


NG = NT // G
RING = 4


def each_group(eng, step, lead=0, lag=0, groups=NG):
    for g in range(-lead, RING):
        step(g, g % RING)
    with eng.Fori(1, groups // RING - 1) as i:
        for r in range(RING):
            step(RING * i + r, r)
    for g in range(groups - RING, groups + lag):
        step(g, g % RING)


def group_at(g, r, by, groups=NG):
    there = not isinstance(g, int) or 0 <= g + by < groups
    return g + by, (r + by) % RING, there


def ring_count(g, r, each):
    return (g - r + RING) * (each // RING)


def load_windows(eng, c, regs, side, g, n=1):
    eng.reg_load(regs[:n * G], c.win[side][0:1, bass.ds(g * G, n * G)])
    return [eng.snap(r, min_val=0, max_val=NW - 1) for r in regs[:n * G]]


def lane_onehot(dve, c, lanes, out):
    return dve.tensor_tensor(out, c.iota[:, :].unsqueeze(1).to_broadcast([P, G, P]),
                             lanes.unsqueeze(2).to_broadcast([P, G, P]), ALU.is_equal)


def load_records(c):
    nc = c.nc
    (s_r,) = semaphores(nc, c.sems, "records_in")
    with nc.Block() as block:
        @block.sync
        def _(sp):
            sp.dma_start(c.rec[:, :, :].rearrange("p t r -> p (t r)"), c.rec_dram[:, :]).then_inc(s_r, 16)
            sp.wait_ge(s_r, 16)

        @block.vector
        def _(dve):
            dve.memset(c.mtab[:, :], -1e30)


def score(c):
    nc = c.nc
    names = ("sc_onehot sc_turned sc_onehot_t sc_onehot_m sc_q sc_index sc_prod sc_dot sc_score sc_hi sc_kept sc_rest "
             "sc_mid sc_rest2 sc_parts sc_parts_turned sc_parts_t sc_spread sc_tilemax sc_max")
    (s_oh, s_tr, s_oht, s_ohm, s_q, s_idx, s_prod, s_dot, s_sc, s_hi, s_kept, s_rest, s_mid, s_rest2, s_parts, s_ptr,
     s_pt, s_mx, s_red, s_max) = semaphores(nc, c.sems, names)
    s_k = semaphores(nc, c.stack, "sc_k_in0 sc_k_in1 sc_k_in2 sc_k_in3")
    s_turn, s_init, s_isel = semaphores(nc, c.sems, "sc_gather_turn sc_init sc_sel_set")
    GH = G * H
    with ExitStack() as t:
        sb = lambda n, s, d: t.enter_context(nc.sbuf_tensor(n, s, d))
        oh = sb("sc_oh", [P, RING, G, P], BF16)
        oht = sb("sc_oht", [P, 2, G, P], BF16)
        ohm = sb("sc_ohm", [P, RING, G, P], BF16)
        idx = sb("sc_idx", [P, RING, G], I32)
        kg = sb("sc_k", [P, RING, G, F], F32)
        prod = sb("sc_prods", [P, G * F], F32)
        dot = sb("sc_dots", [P, G, H], F32)
        rest = sb("sc_rests", [P, 2, GH], F32)
        parts = sb("sc_split", [P, 2, P], BF16)
        pt = sb("sc_split_t", [P, 2, P], BF16)
        red = sb("sc_red", [P, 2, G, H], F32)
        sel = sb("sc_sel", [P, GH, P], BF16)
        psq = [t.enter_context(nc.psum_tensor(f"ps_q{b}", [P, 512], F32)) for b in range(2)]
        pst = t.enter_context(nc.psum_tensor("ps_oht", [P, 1024], BF16))
        psp = t.enter_context(nc.psum_tensor("ps_pt", [P, 1024], BF16))
        psm = [t.enter_context(nc.psum_tensor(f"ps_spread{b}", [P, 1024], F32)) for b in range(2)]
        with nc.Block() as block:
            @block.gpsimd
            def _(pool):
                pool.memset(sel[:, :, :], 0.0).then_inc(s_isel, 1)
                pool.memset(parts[:, :, :], 0.0).then_inc(s_init, 1)
                for j in range(3):
                    pool.wait_ge(s_isel, j + 1)
                    pool.affine_select(out=sel[:, :, :], in_=sel[:, :, :], compare_op=ALU.not_equal, fill=1.0,
                                       base=-j * GH, pattern=[[-1, GH], [0, P]],
                                       channel_multiplier=1).then_inc(s_isel, 1)

                def gather(g, r):
                    pool.wait_ge(s_idx, g + 1)
                    wait_count(pool, s_prod, g - RING + 1)
                    pool.sem_inc(s_turn, 1)
                    for k in range(G):
                        pool.indirect_dma_start(kg[:, r, k, :], None, c.k_dram[:, :],
                                                bass.IndirectOffsetOnAxis(ap=idx[:, r, k:k + 1], axis=0)
                                                ).then_inc(s_k[r], 16)
                each_group(pool, gather)

            @block.vector
            def _(dve):
                dve.wait_ge(s_init, 1)

                def front(g, r):
                    wait_count(dve, s_prod, g - RING + 1)
                    wait_count(dve, s_tr, g - RING + 1)
                    rec = c.rec[:, bass.ds(g * G, G), :]
                    dve.tensor_copy(idx[:, r, :], rec[:, :, C_DST]).then_inc(s_idx, 1)
                    lane_onehot(dve, c, rec[:, :, C_SL], oh[:, r]).then_inc(s_oh, 1)

                flat = dot[:, :, :].rearrange("p k h -> p (k h)")

                def product(g, r):
                    dve.wait_ge(s_q, g + 1)
                    dve.wait_ge(s_k[r], ring_count(g, r, 16 * G))
                    dve.tensor_tensor(prod[:, :], psq[r % 2][:, :], kg[:, r].rearrange("p k f -> p (k f)"),
                                      ALU.mult).then_inc(s_prod, 1)

                def dots(g, r):
                    dve.wait_ge(s_prod, g + 1)
                    wait_count(dve, s_kept, g)
                    dve.tensor_reduce(flat, prod[:, :].rearrange("p (j d) -> p j d", d=D), AX_X,
                                      ALU.add).then_inc(s_dot, 1)

                def add_mask(g, r):
                    dve.wait_ge(s_dot, g + 1)
                    dve.tensor_tensor(dot[:, :, :], dot[:, :, :], c.rec[:, bass.ds(g * G, G), 0:H],
                                      ALU.add).then_inc(s_sc, 1)

                def first_part(g, r):
                    dve.wait_ge(s_sc, g + 1)
                    wait_count(dve, s_ptr, g - 1)
                    dve.tensor_copy(parts[:, r % 2, 0:GH], flat).then_inc(s_hi, 1)
                    dve.tensor_copy(c.sc[:, bass.ds(g * GH, GH)], flat).then_inc(s_kept, 1)

                def first_rest(g, r):
                    dve.wait_ge(s_hi, g + 1)
                    dve.tensor_tensor(rest[:, 0, :], flat, parts[:, r % 2, 0:GH], ALU.subtract).then_inc(s_rest, 1)

                def second_part(g, r):
                    dve.wait_ge(s_rest, g + 1)
                    dve.tensor_copy(parts[:, r % 2, GH:2 * GH], rest[:, 0, :]).then_inc(s_mid, 1)

                def second_rest(g, r):
                    dve.wait_ge(s_mid, g + 1)
                    dve.tensor_tensor(rest[:, 1, :], rest[:, 0, :], parts[:, r % 2, GH:2 * GH],
                                      ALU.subtract).then_inc(s_rest2, 1)

                def third_part(g, r):
                    dve.wait_ge(s_rest2, g + 1)
                    dve.tensor_copy(parts[:, r % 2, 2 * GH:3 * GH], rest[:, 1, :]).then_inc(s_parts, 1)

                def tile_maximum(g, r, k):
                    dve.wait_ge(s_mx, G * g + k + 1)
                    wait_count(dve, s_max, G * (g - 2) + k + 1)
                    dve.tensor_reduce(red[:, r % 2, k, :], psm[k % 2][:, :].rearrange("p (h e) -> p h e", h=H),
                                      AX_X, ALU.max).then_inc(s_red, 1)

                def table_maximum(g, r, k, win):
                    dve.wait_ge(s_red, G * g + k + 1)
                    wait_count(dve, s_max, G * g + k)
                    m = c.mtab[:, bass.ds(win[k] * H, H)]
                    dve.tensor_tensor(m, m, red[:, r % 2, k, :], ALU.max).then_inc(s_max, 1)

                def step(g, r):
                    here = group_at(g, r, 0)[2]
                    before, before_r, any_before = group_at(g, r, -1)
                    old, old_r, any_old = group_at(g, r, -2)
                    ahead, ahead_r, any_ahead = group_at(g, r, 2)
                    win = load_windows(dve, c, c.dve_regs, "src", old) if any_old else None
                    score_work = ((dots,), (add_mask, first_part), (first_rest,), (second_part,))
                    if any_ahead:
                        front(ahead, ahead_r)
                    if here:
                        product(g, r)
                    for k in range(G):
                        if any_old:
                            table_maximum(old, old_r, k, win)
                        if here:
                            for work in score_work[k]:
                                work(g, r)
                        if any_before:
                            tile_maximum(before, before_r, k)
                    if here:
                        second_rest(g, r)
                        third_part(g, r)
                each_group(dve, step, lead=2, lag=2)

            @block.scalar
            def _(act):
                def one_hots(g, r):
                    act.wait_ge(s_tr, g + 1)
                    wait_count(act, s_q, g - 1)
                    act.activation(oht[:, r % 2].rearrange("p k n -> p (k n)"), pst[:, 0:G * P],
                                   ACT.Copy).then_inc(s_oht, 1)
                    wait_count(act, s_mx, G * (g - RING + 1))
                    act.activation(ohm[:, r].rearrange("p k n -> p (k n)"), pst[:, 0:G * P], ACT.Copy,
                                   bias=-1.0).then_inc(s_ohm, 1)

                def split(g, r):
                    act.wait_ge(s_ptr, g + 1)
                    wait_count(act, s_mx, G * (g - 1))
                    act.activation(pt[:, r % 2, :], psp[:, 0:P], ACT.Copy).then_inc(s_pt, 1)

                def step(g, r):
                    for by, work in ((-1, split), (2, one_hots)):
                        at, slot, there = group_at(g, r, by)
                        if there:
                            work(at, slot)
                each_group(act, step, lead=2, lag=1)

            @block.tensor
            def _(pe):
                pe.wait_ge(s_isel, 4)
                pe.wait_ge(s_init, 1)

                def turn(g, r):
                    pe.wait_ge(s_oh, g + 1)
                    wait_count(pe, s_ohm, g)
                    for k in range(G):
                        ins = pe.transpose(pst[:, k * P:(k + 1) * P], oh[:, r, k, :], c.identb[:, :])
                    ins.then_inc(s_tr, 1)

                def queries(g, r):
                    b = r % 2
                    win = load_windows(pe, c, c.pe_regs, "src", g)
                    pe.wait_ge(s_oht, g + 1)
                    wait_count(pe, s_prod, g - 1)
                    for k in range(G):
                        for j in range(3):
                            ins = pe.matmul(psq[b][:, k * F:(k + 1) * F], oht[:, b, k, :],
                                            c.tab[:, j, bass.ds(win[k] * F, F)], start=(j == 0), stop=(j == 2))
                    ins.then_inc(s_q, 1)

                def turn_parts(g, r):
                    pe.wait_ge(s_parts, g + 1)
                    wait_count(pe, s_pt, g)
                    pe.transpose(psp[:, 0:P], parts[:, r % 2, :], c.identb[:, :]).then_inc(s_ptr, 1)

                def spread(g, r, tiles):
                    pe.wait_ge(s_pt, g + 1)
                    pe.wait_ge(s_ohm, g + 1)
                    for k in tiles:
                        wait_count(pe, s_red, G * g + k - 1)
                        for q in range(2):
                            pe.matmul(psm[k % 2][:, q * 512:(q + 1) * 512].rearrange("p (h e) -> p h e", h=4),
                                      c.bigid[:, :], ohm[:, r, k, :].unsqueeze(1).to_broadcast([P, 4, P]),
                                      start=True, stop=False)
                            for h in range(4):
                                kh = k * H + q * 4 + h
                                ins = pe.matmul(psm[k % 2][:, (q * 4 + h) * P:(q * 4 + h + 1) * P], sel[:, kh, :],
                                                pt[:, r % 2, :], start=False, stop=(h == 3))
                        ins.then_inc(s_mx, 1)

                def step(g, r):
                    spread_first = lambda g, r: spread(g, r, (0, 1))
                    spread_last = lambda g, r: spread(g, r, (2, 3))
                    for by, work in ((-1, turn_parts), (-1, spread_first), (2, turn), (1, queries), (-1, spread_last)):
                        at, slot, there = group_at(g, r, by)
                        if there:
                            work(at, slot)
                each_group(pe, step, lead=2, lag=1)


def split_maximum(c, mt):
    nc = c.nc
    s_part, s_rest = semaphores(nc, c.sems, "max_part max_rest")
    with ExitStack() as t:
        rest = t.enter_context(nc.sbuf_tensor("max_rests", [P, NW, H], F32))
        with nc.Block() as block:
            @block.vector
            def _(dve):
                dve.tensor_copy(rest[:, :, :], c.mtab[:, :].rearrange("p (w h) -> p w h", h=H)).then_inc(s_rest, 1)
                for j in range(3):
                    dve.wait_ge(s_rest, j + 1)
                    dve.tensor_copy(mt[:, :, j, :], rest[:, :, :]).then_inc(s_part, 1)
                    if j < 2:
                        dve.wait_ge(s_part, j + 1)
                        dve.tensor_tensor(rest[:, :, :], rest[:, :, :], mt[:, :, j, :], ALU.subtract).then_inc(s_rest, 1)


LG = 4
LT = LG * G
LOTS = NT // LT
SW = 32


def exps(c):
    nc = c.nc
    names = ("ex_onehot ex_turned ex_onehot_t ex_m ex_mm ex_less ex_exp ex_kept ex_part ex_rest ex_sums ex_zero ex_end "
             "ex_total")
    (s_oh, s_tr, s_oht, s_m, s_mm, s_d, s_ex, s_kept, s_part, s_rest, s_sum, s_z, s_end, s_tot) = semaphores(
        nc, c.sems, names)
    with ExitStack() as t:
        sb = lambda n, s, d: t.enter_context(nc.sbuf_tensor(n, s, d))
        mt = sb("max_parts", [P, NW, 3, H], BF16)
        split_maximum(c, mt)
        oh = c.work[:, 0:RING * LT * P // 2].bitcast(BF16).rearrange("p (r k n) -> p r k n", r=RING, n=P)
        oht = sb("ex_oht", [P, 2, G, P], BF16)
        top = sb("ex_tops", [P, LT, H], F32)
        less = sb("ex_lesses", [P, 2, LT, H], F32)
        ex = sb("ex_exps", [P, 2, LT, H], F32)
        rest = sb("ex_rests", [P, 2, LT, H], F32)
        parts = sb("ex_split", [P, 2, LT, 3, H], BF16)
        zero = sb("ex_zeros", [P, 512], BF16)
        pst = [t.enter_context(nc.psum_tensor(f"ps_ex_oht{b}", [P, 1024], BF16)) for b in range(2)]
        psm = [t.enter_context(nc.psum_tensor(f"ps_ex_m{b}", [P, 512], F32)) for b in range(2)]
        psd = t.enter_context(nc.psum_tensor("ps_sums", [P, 2048], F32))
        with nc.Block() as block:
            @block.gpsimd
            def _(pool):
                pool.memset(zero[:, :], 0.0).then_inc(s_z, 1)

            @block.vector
            def _(dve):
                def front(g, r):
                    wait_count(dve, s_sum, g - RING + 1)
                    dve.tensor_tensor(oh[:, r], c.iota[:, :].unsqueeze(1).to_broadcast([P, LT, P]),
                                      c.rec[:, bass.ds(g * LT, LT), C_SL].unsqueeze(2).to_broadcast([P, LT, P]),
                                      ALU.is_equal).then_inc(s_oh, 1)

                def difference(g, r):
                    b = r % 2
                    dve.wait_ge(s_m, LG * (g + 1))
                    wait_count(dve, s_d, g)
                    dve.tensor_reduce(top[:, :, :], psm[b][:, 0:LT * 3 * H].rearrange("p (k j h) -> p k h j", j=3, h=H),
                                      AX_X, ALU.add).then_inc(s_mm, 1)
                    dve.wait_ge(s_mm, g + 1)
                    wait_count(dve, s_ex, g - 1)
                    dve.tensor_tensor(less[:, b, :, :],
                                      c.sc[:, bass.ds(g * LT * H, LT * H)].rearrange("p (k h) -> p k h", h=H),
                                      top[:, :, :], ALU.subtract).then_inc(s_d, 1)

                def split(g, r):
                    b = r % 2
                    dve.wait_ge(s_ex, g + 1)
                    wait_count(dve, s_sum, g - 1)
                    dve.tensor_copy(parts[:, b, :, 0, :], ex[:, b, :, :]).then_inc(s_part, 1)
                    dve.tensor_copy(c.sc[:, bass.ds(g * LT * H, LT * H)],
                                    ex[:, b, :, :].rearrange("p k h -> p (k h)")).then_inc(s_kept, 1)
                    dve.wait_ge(s_part, 3 * g + 1)
                    dve.tensor_tensor(rest[:, 0, :, :], ex[:, b, :, :], parts[:, b, :, 0, :],
                                      ALU.subtract).then_inc(s_rest, 1)
                    dve.wait_ge(s_rest, 2 * g + 1)
                    dve.tensor_copy(parts[:, b, :, 1, :], rest[:, 0, :, :]).then_inc(s_part, 1)
                    dve.wait_ge(s_part, 3 * g + 2)
                    dve.tensor_tensor(rest[:, 1, :, :], rest[:, 0, :, :], parts[:, b, :, 1, :],
                                      ALU.subtract).then_inc(s_rest, 1)
                    dve.wait_ge(s_rest, 2 * g + 2)
                    dve.tensor_copy(parts[:, b, :, 2, :], rest[:, 1, :, :]).then_inc(s_part, 1)

                def step(g, r):
                    for by, work in ((1, front), (0, difference), (-1, split)):
                        at, slot, there = group_at(g, r, by, LOTS)
                        if there:
                            work(at, slot)
                each_group(dve, step, lead=1, lag=1, groups=LOTS)
                dve.wait_ge(s_end, 1)
                dve.tensor_reduce(c.dtab[:, :].rearrange("p (w h) -> p w h", h=H),
                                  psd[:, 0:NW * SW].rearrange("p (w x) -> p w x", x=SW)[:, :, 0:3 * H].rearrange(
                                      "p w (j h) -> p w h j", j=3), AX_X, ALU.add).then_inc(s_tot, 1)
                dve.wait_ge(s_tot, 1)
                dve.tensor_scalar(c.dtab[:, :], c.dtab[:, :], 1e-20, None, ALU.max)

            @block.scalar
            def _(act):
                def turned(g, q):
                    act.wait_ge(s_tr, LG * g + q + 1)
                    wait_count(act, s_m, LG * g + q - 1)
                    act.activation(oht[:, q % 2].rearrange("p k n -> p (k n)"), pst[q % 2][:, 0:G * P],
                                   ACT.Copy).then_inc(s_oht, 1)

                def exp(g, r):
                    act.wait_ge(s_d, g + 1)
                    wait_count(act, s_part, 3 * (g - 1))
                    act.activation(ex[:, r % 2].rearrange("p k h -> p (k h)"),
                                   less[:, r % 2].rearrange("p k h -> p (k h)"), ACT.Exp).then_inc(s_ex, 1)

                def step(g, r):
                    here = group_at(g, r, 0, LOTS)[2]
                    before, slot, any_before = group_at(g, r, -1, LOTS)
                    for q in range(LG):
                        if here:
                            turned(g, q)
                        if q == 0 and any_before:
                            exp(before, slot)
                each_group(act, step, lag=1, groups=LOTS)

            @block.tensor
            def _(pe):
                pe.wait_ge(s_z, 1)
                for n in range(4):
                    pe.matmul(psd[:, n * 512:(n + 1) * 512], c.ones[:, :], zero[:, :], start=True, stop=False)

                def turn(g, r, q):
                    if q == 0:
                        pe.wait_ge(s_oh, g + 1)
                    wait_count(pe, s_oht, LG * g + q - 1)
                    for k in range(G):
                        ins = pe.transpose(pst[q % 2][:, k * P:(k + 1) * P], oh[:, r, q * G + k, :], c.identb[:, :])
                    ins.then_inc(s_tr, 1)

                def maxima(g, r, q, win):
                    pe.wait_ge(s_oht, LG * g + q + 1)
                    if q == 0:
                        wait_count(pe, s_d, g - 1)
                    for k in range(G):
                        at = (q * G + k) * 3 * H
                        ins = pe.matmul(psm[r % 2][:, at:at + 3 * H], oht[:, q % 2, k, :],
                                        mt[:, bass.ds(win[k], 1), :, :].rearrange("p w j h -> p (w j h)"),
                                        start=True, stop=True)
                    ins.then_inc(s_m, 1)

                def sums(g, r, q, win):
                    if q == 0:
                        pe.wait_ge(s_part, 3 * (g + 1))
                    for k in range(G):
                        at = q * G + k
                        ins = pe.matmul(psd[:, bass.ds(win[k] * SW, 3 * H)], oh[:, r, at, :],
                                        parts[:, r % 2, at].rearrange("p j h -> p (j h)"), start=False, stop=False,
                                        skip_group_check=True)
                    if q == LG - 1:
                        ins.then_inc(s_sum, 1)

                def step(g, r):
                    here = group_at(g, r, 0, LOTS)[2]
                    old, old_r, any_old = group_at(g, r, -2, LOTS)
                    if here:
                        turn(g, r, 0)
                    for q in range(LG):
                        if any_old:
                            if q % 2 == 0:
                                old_win = load_windows(pe, c, c.pe_regs, "src", old * LG + q, 2)
                            sums(old, old_r, q, old_win[q % 2 * G:(q % 2 + 1) * G])
                        if here:
                            if q < LG - 1:
                                turn(g, r, q + 1)
                            if q % 2 == 0:
                                win = load_windows(pe, c, c.more_pe_regs, "src", g * LG + q, 2)
                            maxima(g, r, q, win[q % 2 * G:(q % 2 + 1) * G])
                each_group(pe, step, lag=2, groups=LOTS)
                for n in range(4):
                    ins = pe.matmul(psd[:, n * 512:(n + 1) * 512], c.ones[:, :], zero[:, :], start=False, stop=True)
                ins.then_inc(s_end, 1)


def normalise_values(c):
    nc = c.nc
    (s_rec,) = semaphores(nc, c.sems, "sums_inverted")
    with nc.Block() as block:
        @block.vector
        def _(dve):
            dve.reciprocal(c.mtab[:, :], c.dtab[:, :]).then_inc(s_rec, 1)
            dve.wait_ge(s_rec, 1)
            dve.tensor_tensor(c.work[:, :].rearrange("p (j d) -> p j d", d=D),
                              c.vals[:, :].rearrange("p (j d) -> p j d", d=D),
                              c.mtab[:, :].unsqueeze(2).to_broadcast([P, NW * H, D]), ALU.mult)


def weigh(c):
    nc = c.nc
    names = "we_onehot we_turned we_onehot_t we_v we_index we_contrib we_lane"
    (s_oh, s_tr, s_oht, s_v, s_idx, s_con, s_lane) = semaphores(nc, c.sems, names)
    s_sent = semaphores(nc, c.stack, "we_sent0 we_sent1")
    s_turn, s_pad = semaphores(nc, c.sems, "we_scatter_turn we_padded")
    with ExitStack() as t:
        sb = lambda n, s, d: t.enter_context(nc.sbuf_tensor(n, s, d))
        oh = sb("we_oh", [P, 2, G, P], BF16)
        oht = sb("we_oht", [P, 2, G, P], BF16)
        idx = sb("we_idx", [P, 2, G], I32)
        con = sb("we_rows", [P, 2, G, CW], F32)
        pst = t.enter_context(nc.psum_tensor("ps_we_oht", [P, 1024], BF16))
        psv = [t.enter_context(nc.psum_tensor(f"ps_v{b}", [P, 512], F32)) for b in range(2)]
        with nc.Block() as block:
            @block.gpsimd
            def _(pool):
                def scatter(g, b):
                    pool.wait_ge(s_con, g + 1)
                    pool.wait_ge(s_lane, g + 1)
                    pool.wait_ge(s_idx, g + 1)
                    pool.sem_inc(s_turn, 1)
                    for k in range(G):
                        pool.indirect_dma_start(c.row_rows, bass.IndirectOffsetOnAxis(ap=idx[:, b, k:k + 1], axis=0),
                                                con[:, b, k, :], None, bounds_check=SLOTS - 1, oob_is_err=False
                                                ).then_inc(s_sent[b], 16)
                pool.wait_ge(s_pad, 1)
                with pool.Fori(0, PAIRS) as i:
                    for b in range(2):
                        scatter(2 * i + b, b)
                for b in range(2):
                    pool.wait_ge(s_sent[b], 16 * G * PAIRS)

            @block.vector
            def _(dve):
                dve.memset(con[:, :, :, F + 1:CW], 0.0).then_inc(s_pad, 1)

                def front(g, b):
                    wait_count(dve, s_tr, g - 1)
                    lane_onehot(dve, c, c.rec[:, bass.ds(g * G, G), C_SL], oh[:, b]).then_inc(s_oh, 1)

                def middle(g, b):
                    wait_count(dve, s_sent[b], 8 * G * (g - b))
                    rec = c.rec[:, bass.ds(g * G, G), :]
                    dve.tensor_copy(idx[:, b, :], rec[:, :, C_ROW]).then_inc(s_idx, 1)
                    dve.tensor_copy(con[:, b, :, F], rec[:, :, C_DL]).then_inc(s_lane, 1)
                    dve.wait_ge(s_v, g + 1)
                    ex = c.sc[:, bass.ds(g * G * H, G * H)].rearrange("p (k h) -> p k h", h=H)
                    dve.tensor_tensor(con[:, b, :, 0:F].rearrange("p k (h d) -> p k h d", d=D),
                                      psv[b][:, :].rearrange("p (k h d) -> p k h d", h=H, d=D),
                                      ex.unsqueeze(3).to_broadcast([P, G, H, D]), ALU.mult).then_inc(s_con, 1)

                def pair(i, last):
                    for b in range(2):
                        middle(2 * i + b, b)
                        if not last:
                            front(2 * i + 2 + b, b)
                for b in range(2):
                    front(b, b)
                pair(0, False)
                with dve.Fori(1, PAIRS - 1) as i:
                    pair(i, False)
                pair(PAIRS - 1, True)

            @block.scalar
            def _(act):
                def turned(g, b):
                    act.wait_ge(s_tr, g + 1)
                    wait_count(act, s_v, g - 1)
                    act.activation(oht[:, b].rearrange("p k n -> p (k n)"), pst[:, 0:G * P], ACT.Copy).then_inc(s_oht, 1)
                for b in range(2):
                    turned(b, b)
                with act.Fori(1, PAIRS) as i:
                    for b in range(2):
                        turned(2 * i + b, b)

            @block.tensor
            def _(pe):
                def values(g, b):
                    win = load_windows(pe, c, c.pe_regs, "src", g)
                    pe.wait_ge(s_oh, g + 1)
                    wait_count(pe, s_oht, g)
                    for k in range(G):
                        ins = pe.transpose(pst[:, k * P:(k + 1) * P], oh[:, b, k, :], c.identb[:, :])
                    ins.then_inc(s_tr, 1)
                    pe.wait_ge(s_oht, g + 1)
                    wait_count(pe, s_con, g - 1)
                    for k in range(G):
                        for j in range(3):
                            ins = pe.matmul(psv[b][:, k * F:(k + 1) * F], oht[:, b, k, :],
                                            c.tab[:, j, bass.ds(win[k] * F, F)], start=(j == 0), stop=(j == 2))
                    ins.then_inc(s_v, 1)
                for b in range(2):
                    values(b, b)
                with pe.Fori(1, PAIRS) as i:
                    for b in range(2):
                        values(2 * i + b, b)


CB = 4


def collect(c):
    nc = c.nc
    s_oh, s_mm, s_add, s_z = semaphores(nc, c.sems, "co_onehot co_sums co_added co_zeroed")
    s_in = semaphores(nc, c.sems, "co_in0 co_in1 co_in2 co_in3")
    with ExitStack() as t:
        sb = lambda n, s, d: t.enter_context(nc.sbuf_tensor(n, s, d))
        cin = sb("co_rows", [P, CB, G, CW], F32)
        oh = sb("co_oh", [P, 2, G, P], F32)
        ps = [t.enter_context(nc.psum_tensor(f"ps_co{b}", [P, 512], F32)) for b in range(2)]
        IT = NT // (G * CB)
        with nc.Block() as block:
            @block.sync
            def _(sp):
                def load(g, r):
                    wait_count(sp, s_mm, g - CB + 1)
                    sp.dma_start(cin[:, r].rearrange("p k c -> p (k c)"),
                                 c.row_dram[:, bass.ds(g * G * CW, G * CW)]).then_inc(s_in[r], 16)
                for r in range(CB):
                    load(r, r)
                with sp.Fori(1, IT) as i:
                    for r in range(CB):
                        load(CB * i + r, r)

            @block.vector
            def _(dve):
                dve.memset(c.vals[:, :], 0.0).then_inc(s_add, 1)

                def front(g, r, use):
                    dve.wait_ge(s_in[r], 16 * use)
                    wait_count(dve, s_mm, g - 1)
                    lane_onehot(dve, c, cin[:, r, :, F], oh[:, r % 2]).then_inc(s_oh, 1)

                def back(g, r):
                    win = load_windows(dve, c, c.dve_regs, "dst", g)
                    dve.wait_ge(s_mm, g + 1)
                    for k in range(G):
                        dve.wait_ge(s_add, G * g + k + 1)
                        acc = c.vals[:, bass.ds(win[k] * P, P)]
                        dve.tensor_tensor(acc, acc, ps[r % 2][:, k * P:(k + 1) * P], ALU.add).then_inc(s_add, 1)

                def lot(i, last):
                    for r in range(CB):
                        if not (last and r == CB - 1):
                            front(CB * i + r + 1, (r + 1) % CB, i + 1 + (r + 1) // CB)
                        back(CB * i + r, r)
                front(0, 0, 1)
                lot(0, False)
                with dve.Fori(1, IT - 1) as i:
                    lot(i, False)
                lot(IT - 1, True)

            @block.tensor
            def _(pe):
                def sums(g, r):
                    pe.wait_ge(s_oh, g + 1)
                    wait_count(pe, s_add, G * (g - 1) + 1)
                    for k in range(G):
                        ins = pe.matmul(ps[r % 2][:, k * P:(k + 1) * P], cin[:, r, k, 0:F], oh[:, r % 2, k, :],
                                        start=True, stop=True)
                    ins.then_inc(s_mm, 1)
                for r in range(CB):
                    sums(r, r)
                with pe.Fori(1, IT) as i:
                    for r in range(CB):
                        sums(CB * i + r, r)


def each_window(eng, body):
    for b in range(2):
        body(b, b, 1)
    with eng.Fori(1, NW // 2) as i:
        for b in range(2):
            body(2 * i + b, b, i + 1)
    body(NW - 1, 0, NW // 2 + 1)


def row_vector(v, n):
    return v.rearrange("(o n) -> o n", o=1).to_broadcast([P, n])


def nodes1(c, a):
    nc = c.nc
    names = ("n1_weights n1_acc n1_o n1_res n1_sum n1_stats n1_moments n1_std n1_rstd n1_shift n1_x1 n1_turn n1_x1t "
             "n1_ab n1_a n1_b n1_act_turn n1_x1tab n1_dve_turn n1_set")
    (s_w, s_acc, s_o, s_res, s_sum, s_st, s_mv, s_std, s_rstd, s_shift, s_x1, s_tr, s_x1t, s_ab, s_a, s_b, s_turn,
     s_x1tab, s_dturn, s_set) = semaphores(nc, c.sems, names)
    s_x = semaphores(nc, c.sems, "n1_x0 n1_x1in")
    s_bo = semaphores(nc, c.sems, "n1_b_out0 n1_b_out1")
    s_xo = semaphores(nc, c.sems, "n1_x1_out0 n1_x1_out1")
    with ExitStack() as t:
        sb = lambda n, s, d: t.enter_context(nc.sbuf_tensor(n, s, d))
        wo = sb("w_o", [P, F], F32)
        bo = sb("b_o", [P, F], F32)
        w1 = sb("w_1", [P, 2 * F], F32)
        b1 = sb("b_1", [P, F], F32)
        accs = sb("n1_accs", [P, 2, P], F32)
        xr = sb("n1_xr", [P, 2, F], F32)
        res = sb("n1_ress", [P, F], F32)
        stats = sb("n1_statss", [P, nc.vector.BN_STATS_DIM], F32)
        mv = sb("n1_mvs", [P, nc.vector.BN_AGGR_DIM], F32)
        std = sb("n1_stds", [P, 1], F32)
        rstd = sb("n1_rstds", [P, 1], F32)
        eps = sb("n1_eps", [P, 1], F32)
        x1 = sb("n1_x1s", [P, 2, F], F32)
        x1t = sb("n1_x1ts", [P, 2, P], F32)
        bt = sb("n1_bts", [P, 2, F], F32)
        pso = [t.enter_context(nc.psum_tensor(f"ps_o{b}", [P, 512], F32)) for b in range(2)]
        psx = [t.enter_context(nc.psum_tensor(f"ps_x{b}", [P, 512], F32)) for b in range(2)]
        psab = [t.enter_context(nc.psum_tensor(f"ps_ab{b}", [P, 512], F32)) for b in range(2)]
        with nc.Block() as block:
            @block.gpsimd
            def _(pool):
                pool.memset(eps[:, :], EPS).then_inc(s_set, 1)
                pool.memset(xr[:, :, :], 0.0).then_inc(s_set, 1)

            @block.sync
            def _(sp):
                sp.dma_start(wo[:, :], a["WoT"]).then_inc(s_w, 16)
                sp.dma_start(bo[:, :], row_vector(a["bo"], F)).then_inc(s_w, 16)
                sp.dma_start(w1[:, 0:F], a["eW1"][0:F, :]).then_inc(s_w, 16)
                sp.dma_start(w1[:, F:2 * F], a["eW1"][F:2 * F, :]).then_inc(s_w, 16)
                sp.dma_start(b1[:, :], row_vector(a["eb1"], F)).then_inc(s_w, 16)

                def load(w, b, use):
                    wait_count(sp, s_res, w - 1)
                    rows = LAST if isinstance(w, int) and w == NW - 1 else P
                    sp.dma_start(xr[0:rows, b, :], a["x"][bass.ds(w * P, rows), :]).then_inc(s_x[b], 16)

                def store(w, b, use):
                    sp.wait_ge(s_x1, w + 1)
                    sp.dma_start(c.x1_dram[bass.ds(w * P, P), :], x1[:, b, :]).then_inc(s_xo[b], 16)
                    sp.wait_ge(s_b, w + 1)
                    sp.dma_start(c.b_dram[bass.ds(w * P, P), :], bt[:, b, :]).then_inc(s_bo[b], 16)
                sp.wait_ge(s_set, 2)
                load(0, 0, 1)
                load(1, 1, 1)
                with sp.Fori(0, NW // 2 - 1) as i:
                    for b in range(2):
                        store(2 * i + b, b, 0)
                        load(2 * i + 2 + b, b, 0)
                store(NW - 3, 0, 0)
                load(NW - 1, 0, 0)
                store(NW - 2, 1, 0)
                store(NW - 1, 0, 0)
                for b in range(2):
                    sp.wait_ge(s_xo[b], 16 * (NW // 2 + 1 - b))
                    sp.wait_ge(s_bo[b], 16 * (NW // 2 + 1 - b))

            @block.scalar
            def _(act):
                act.wait_ge(s_set, 2)

                def window(w, b, use):
                    wait_count(act, s_o, w - 1)
                    act.sem_inc(s_turn, 1)
                    act.activation(accs[:, b, :], c.vals[:, bass.ds(w * P, P)], ACT.Copy).then_inc(s_acc, 1)
                    act.wait_ge(s_mv, w + 1)
                    wait_count(act, s_rstd, w)
                    act.activation(std[:, :], mv[:, 1:2], ACT.Sqrt, bias=eps[:, 0:1]).then_inc(s_std, 1)
                    act.wait_ge(s_tr, w + 1)
                    wait_count(act, s_ab, w - 1)
                    act.activation(x1t[:, b, :], psx[b][:, 0:P], ACT.Copy).then_inc(s_x1t, 1)
                    act.wait_ge(s_x1t, w + 1)
                    act.sem_inc(s_turn, 1)
                    act.activation(c.x1t[:, bass.ds(w * P, P)], x1t[:, b, :], ACT.Copy).then_inc(s_x1tab, 1)
                each_window(act, window)

            @block.tensor
            def _(pe):
                pe.wait_ge(s_w, 80)

                def window(w, b, use):
                    pe.wait_ge(s_acc, w + 1)
                    wait_count(pe, s_res, w - 1)
                    pe.matmul(pso[b][:, 0:F], accs[:, b, :], wo[:, :], start=True, stop=True).then_inc(s_o, 1)
                    pe.wait_ge(s_x1, w + 1)
                    wait_count(pe, s_x1t, w - 1)
                    pe.transpose(psx[b][:, 0:P], x1[:, b, :], c.ident[:, :]).then_inc(s_tr, 1)
                    pe.wait_ge(s_x1t, w + 1)
                    wait_count(pe, s_b, w - 1)
                    pe.matmul(psab[b][:, 0:2 * F], x1t[:, b, :], w1[:, :], start=True, stop=True).then_inc(s_ab, 1)
                each_window(pe, window)

            @block.vector
            def _(dve):
                dve.wait_ge(s_w, 80)

                def window(w, b, use):
                    dve.wait_ge(s_x[b], 16 * use)
                    dve.wait_ge(s_o, w + 1)
                    dve.tensor_tensor(res[:, :], pso[b][:, 0:F], xr[:, b, :], ALU.add).then_inc(s_res, 1)
                    dve.wait_ge(s_res, w + 1)
                    dve.tensor_tensor(res[:, :], res[:, :], bo[:, :], ALU.add).then_inc(s_sum, 1)
                    dve.wait_ge(s_sum, w + 1)
                    normalise(dve, c, w, res, stats, mv, std, rstd, (s_st, s_mv, s_std, s_rstd, s_dturn))
                    wait_count(dve, s_xo[b], 16 * (use - 1))
                    wait_count(dve, s_tr, w - 1)
                    dve.tensor_scalar(x1[:, b, :], res[:, :], mv[:, 0:1], rstd[:, 0:1], ALU.subtract,
                                      ALU.mult).then_inc(s_x1, 1)
                    dve.wait_ge(s_ab, w + 1)
                    dve.tensor_tensor(c.work[:, bass.ds(w * F, F)], psab[b][:, 0:F], b1[:, :], ALU.add).then_inc(s_a, 1)
                    wait_count(dve, s_bo[b], 16 * (use - 1))
                    dve.tensor_copy(bt[:, b, :], psab[b][:, F:2 * F]).then_inc(s_b, 1)
                each_window(dve, window)


def normalise(dve, c, w, res, stats, mv, std, rstd, sems):
    s_st, s_mv, s_std, s_rstd, s_turn = sems
    dve.bn_stats(stats[:, :], res[:, :]).then_inc(s_st, 1)
    dve.wait_ge(s_st, w + 1)
    dve.sem_inc(s_turn, 1)
    dve.bn_aggr(mv[:, :], stats[:, :]).then_inc(s_mv, 1)
    dve.wait_ge(s_std, w + 1)
    dve.reciprocal(rstd[:, :], std[:, :]).then_inc(s_rstd, 1)
    dve.wait_ge(s_rstd, w + 1)


def attribute_parts(c, a, parts, weights):
    nc = c.nc
    s_w, s_part, s_rest, s_wp, s_sel, s_z = semaphores(nc, c.sems, "ap_w ap_part ap_rest ap_wp ap_sel ap_zeroed")
    K = 9 * 2 * G
    with ExitStack() as t:
        sb = lambda n, s, d: t.enter_context(nc.sbuf_tensor(n, s, d))
        rest = sb("ap_rests", [P, NT, 2], F32)
        wr = sb("ap_wr", [P, F], F32)
        wp = sb("ap_wps", [P, 3, F], BF16)
        pair = sb("ap_pair", [P, K // 2], F32)
        sel = sb("ap_sels", [P, 3, G], F32)
        with nc.Block() as block:
            @block.gpsimd
            def _(pool):
                pool.memset(wr[:, :], 0.0).then_inc(s_z, 1)

            @block.sync
            def _(sp):
                sp.wait_ge(s_z, 1)
                for n in range(K // 2):
                    sp.dma_start(wr[2 * n:2 * n + 2, :], a["eW1"][2 * F:2 * F + 2, :]).then_inc(s_w, 16)

            @block.vector
            def _(dve):
                view = lambda i: parts.rearrange("p (g i x) -> p g i x", i=3, x=2 * G)[:, :, i, :]
                flat = rest[:, :, :].rearrange("p (g k) j -> p g (k j)", k=G)
                attrs = c.rec[:, :, C_ATTR:C_ATTR + 2]
                dve.tensor_copy(rest[:, :, :], attrs).then_inc(s_rest, 1)
                dve.wait_ge(s_rest, 1)
                for i in range(3):
                    dve.tensor_copy(view(i), flat).then_inc(s_part, 1)
                    dve.wait_ge(s_part, i + 1)
                    if i < 2:
                        dve.tensor_tensor(flat, flat, view(i), ALU.subtract).then_inc(s_rest, 1)
                        dve.wait_ge(s_rest, i + 2)
                dve.wait_ge(s_w, 16 * (K // 2))
                for i in range(3):
                    dve.tensor_copy(wp[:, i, :], wr[:, :]).then_inc(s_wp, 1)
                    dve.wait_ge(s_wp, 2 * i + 1)
                    dve.tensor_tensor(wr[:, :], wr[:, :], wp[:, i, :], ALU.subtract).then_inc(s_wp, 1)
                    dve.wait_ge(s_wp, 2 * i + 2)
                dve.tensor_reduce(pair[:, :], c.ident[:, 0:K].rearrange("p (n a) -> p n a", a=2), AX_X,
                                  ALU.add).then_inc(s_sel, 1)
                dve.wait_ge(s_sel, 1)
                dve.tensor_reduce(sel[:, :, :], pair[:, :].rearrange("p (j i k) -> p j k i", j=3, i=3), AX_X,
                                  ALU.add).then_inc(s_sel, 1)
                dve.wait_ge(s_sel, 2)
                n = 2
                for k in range(G):
                    dve.tensor_scalar(weights[:, k, :], wp[:, 0, :], sel[:, 0, k:k + 1], None, ALU.mult).then_inc(s_sel, 1)
                    n += 1
                    for i in (1, 2):
                        dve.wait_ge(s_sel, n)
                        dve.scalar_tensor_tensor(out=weights[:, k, :], in0=wp[:, i, :], scalar=sel[:, i, k:k + 1],
                                                 in1=weights[:, k, :], op0=ALU.mult, op1=ALU.add).then_inc(s_sel, 1)
                        n += 1


def edges(c, a):
    nc = c.nc
    names = ("ed_weights ed_padded ed_onehot ed_onehot_f ed_turned ed_onehot_t ed_index ed_attr ed_attr_turned "
             "ed_attr_t ed_z ed_h ed_o ed_ob ed_f ed_sums ed_added")
    (s_w, s_pad, s_oh, s_ohf, s_tr, s_oht, s_idx, s_at, s_atr, s_att, s_z, s_h, s_o, s_ob, s_f, s_sum,
     s_add) = semaphores(nc, c.sems, names)
    s_b = semaphores(nc, c.stack, "ed_b_in0 ed_b_in1 ed_b_in2 ed_b_in3")
    (s_turn,) = semaphores(nc, c.sems, "ed_gather_turn")
    K = 9 * 2 * G
    with ExitStack() as t:
        sb = lambda n, s, d: t.enter_context(nc.sbuf_tensor(n, s, d))
        parts = c.work[:, 0:NT * 3].bitcast(BF16)
        wc = sb("w_attr", [P, G, F], BF16)
        attribute_parts(c, a, parts, wc)
        w2 = sb("w_2", [P, F], F32)
        b2 = sb("b_2", [P, F], F32)
        oh = sb("ed_oh", [P, RING, G, P], BF16)
        ohf = sb("ed_ohf", [P, 2, G, P], F32)
        oht = sb("ed_oht", [P, 2, G, P], BF16)
        idx = sb("ed_idx", [P, RING, G], I32)
        bg = sb("ed_bg", [P, RING, G, F], F32)
        attr = sb("ed_attrs", [P, RING, P], BF16)
        att = sb("ed_atts", [P, 2, P], BF16)
        h = sb("ed_hs", [P, 2, G * P], F32)
        ob = sb("ed_obs", [P, 2, G * F], F32)
        ef = sb("ed_efs", [P, 2, G, F], F32)
        pst = t.enter_context(nc.psum_tensor("ps_ed_oht", [P, 1024], BF16))
        psa = t.enter_context(nc.psum_tensor("ps_ed_att", [P, 1024], BF16))
        psz = [t.enter_context(nc.psum_tensor(f"ps_z{b}", [P, 512], F32)) for b in range(2)]
        pso = [t.enter_context(nc.psum_tensor(f"ps_ed_o{b}", [P, 512], F32)) for b in range(2)]
        pss = [t.enter_context(nc.psum_tensor(f"ps_ed_s{b}", [P, 512], F32)) for b in range(2)]
        with nc.Block() as block:
            @block.sync
            def _(sp):
                sp.dma_start(w2[:, :], a["eW2"]).then_inc(s_w, 16)
                sp.dma_start(b2[:, :], row_vector(a["eb2"], F)).then_inc(s_w, 16)

            @block.gpsimd
            def _(pool):
                pool.memset(attr[:, :, :], 0.0).then_inc(s_pad, 1)

                def gather(g, r):
                    pool.wait_ge(s_idx, g + 1)
                    wait_count(pool, s_z, g - RING + 1)
                    pool.sem_inc(s_turn, 1)
                    for k in range(G):
                        pool.indirect_dma_start(bg[:, r, k, :], None, c.b_dram[:, :],
                                                bass.IndirectOffsetOnAxis(ap=idx[:, r, k:k + 1], axis=0)
                                                ).then_inc(s_b[r], 16)
                each_group(pool, gather)

            @block.vector
            def _(dve):
                dve.wait_ge(s_pad, 1)
                dve.wait_ge(s_w, 32)
                dve.memset(c.vals[:, :], 0.0).then_inc(s_add, 1)

                def front(g, r):
                    wait_count(dve, s_z, g - RING + 1)
                    wait_count(dve, s_ohf, g - RING + 1)
                    rec = c.rec[:, bass.ds(g * G, G), :]
                    dve.tensor_copy(idx[:, r, :], rec[:, :, C_DST]).then_inc(s_idx, 1)
                    lane_onehot(dve, c, rec[:, :, C_SL], oh[:, r]).then_inc(s_oh, 1)
                    dve.tensor_copy(attr[:, r, 0:K].rearrange("p (j x) -> p j x", j=3),
                                    parts[:, bass.ds(g * 6 * G, 6 * G)].unsqueeze(1).to_broadcast([P, 3, 6 * G])
                                    ).then_inc(s_at, 1)

                def middle(g, r):
                    b = r % 2
                    dve.wait_ge(s_oh, g + 1)
                    wait_count(dve, s_sum, g - 1)
                    dve.tensor_copy(ohf[:, b].rearrange("p k n -> p (k n)"),
                                    oh[:, r].rearrange("p k n -> p (k n)")).then_inc(s_ohf, 1)
                    dve.wait_ge(s_o, g + 1)
                    wait_count(dve, s_f, g - 1)
                    dve.tensor_tensor(ob[:, b, :].rearrange("p (k f) -> p k f", k=G),
                                      pso[b][:, :].rearrange("p (k f) -> p k f", k=G),
                                      b2[:, :].unsqueeze(1).to_broadcast([P, G, F]), ALU.add).then_inc(s_ob, 1)

                def back(g, r):
                    win = load_windows(dve, c, c.dve_regs, "src", g)
                    dve.wait_ge(s_sum, g + 1)
                    for k in range(G):
                        dve.wait_ge(s_add, G * g + k + 1)
                        acc = c.vals[:, bass.ds(win[k] * P, P)]
                        dve.tensor_tensor(acc, acc, pss[r % 2][:, k * P:(k + 1) * P], ALU.add).then_inc(s_add, 1)

                def step(g, r):
                    for by, work in ((2, front), (-1, middle), (-3, back)):
                        at, slot, there = group_at(g, r, by)
                        if there:
                            work(at, slot)
                each_group(dve, step, lead=2, lag=3)

            @block.scalar
            def _(act):
                def turned(g, r):
                    act.wait_ge(s_tr, g + 1)
                    wait_count(act, s_z, g - 1)
                    act.activation(oht[:, r % 2].rearrange("p k n -> p (k n)"), pst[:, 0:G * P],
                                   ACT.Copy).then_inc(s_oht, 1)
                    act.wait_ge(s_atr, g + 1)
                    act.activation(att[:, r % 2, :], psa[:, 0:P], ACT.Copy).then_inc(s_att, 1)

                def hidden(g, r):
                    act.wait_ge(s_z, g + 1)
                    wait_count(act, s_o, g - 1)
                    act.activation(h[:, r % 2, :], psz[r % 2][:, :], ACT.Silu).then_inc(s_h, 1)

                def feature(g, r):
                    act.wait_ge(s_ob, g + 1)
                    wait_count(act, s_sum, g - 1)
                    act.activation(ef[:, r % 2].rearrange("p k f -> p (k f)"), ob[:, r % 2, :],
                                   ACT.Silu).then_inc(s_f, 1)

                def step(g, r):
                    for by, work in ((1, turned), (0, hidden), (-1, feature)):
                        at, slot, there = group_at(g, r, by)
                        if there:
                            work(at, slot)
                each_group(act, step, lead=1, lag=1)

            @block.tensor
            def _(pe):
                pe.wait_ge(s_w, 32)

                def turn(g, r):
                    pe.wait_ge(s_oh, g + 1)
                    wait_count(pe, s_oht, g)
                    for k in range(G):
                        ins = pe.transpose(pst[:, k * P:(k + 1) * P], oh[:, r, k, :], c.identb[:, :])
                    ins.then_inc(s_tr, 1)
                    pe.wait_ge(s_at, g + 1)
                    wait_count(pe, s_att, g)
                    pe.transpose(psa[:, 0:P], attr[:, r, :], c.identb[:, :]).then_inc(s_atr, 1)

                def inputs(g, r):
                    b = r % 2
                    win = load_windows(pe, c, c.pe_regs, "src", g)
                    pe.wait_ge(s_oht, g + 1)
                    pe.wait_ge(s_att, g + 1)
                    wait_count(pe, s_h, g - 1)
                    pe.wait_ge(s_b[r], ring_count(g, r, 16 * G))
                    for k in range(G):
                        z = psz[b][:, k * P:(k + 1) * P]
                        pe.matmul(z, wc[:, k, :], att[:, b, :], start=True, stop=False)
                        for j in range(3):
                            pe.matmul(z, c.tab[:, j, bass.ds(win[k] * F, F)], oht[:, b, k, :],
                                      start=False, stop=False)
                        ins = pe.matmul(z, bg[:, r, k, :], c.ident[:, :], start=False, stop=True)
                    ins.then_inc(s_z, 1)

                def second(g, r):
                    b = r % 2
                    pe.wait_ge(s_h, g + 1)
                    wait_count(pe, s_ob, g - 1)
                    for k in range(G):
                        ins = pe.matmul(pso[b][:, k * F:(k + 1) * F], h[:, b, k * P:(k + 1) * P], w2[:, :],
                                        start=True, stop=True)
                    ins.then_inc(s_o, 1)

                def sums(g, r):
                    b = r % 2
                    pe.wait_ge(s_f, g + 1)
                    pe.wait_ge(s_ohf, g + 1)
                    wait_count(pe, s_add, G * (g - 1) + 1)
                    for k in range(G):
                        ins = pe.matmul(pss[b][:, k * P:(k + 1) * P], ef[:, b, k, :], ohf[:, b, k, :],
                                        start=True, stop=True)
                    ins.then_inc(s_sum, 1)

                def step(g, r):
                    for by, work in ((1, turn), (0, inputs), (-1, second), (-2, sums)):
                        at, slot, there = group_at(g, r, by)
                        if there:
                            work(at, slot)
                each_group(pe, step, lead=1, lag=2)


def nodes2(c, a, out):
    nc = c.nc
    names = "n2_weights n2_pre n2_hid n2_o n2_res n2_sum n2_stats n2_moments n2_std n2_rstd n2_y n2_turn n2_set"
    (s_w, s_pre, s_hid, s_o, s_res, s_sum, s_st, s_mv, s_std, s_rstd, s_y, s_dturn, s_set) = semaphores(nc, c.sems, names)
    s_x = semaphores(nc, c.sems, "n2_x0 n2_x1")
    s_out = semaphores(nc, c.sems, "n2_out0 n2_out1")
    with ExitStack() as t:
        sb = lambda n, s, d: t.enter_context(nc.sbuf_tensor(n, s, d))
        wx = sb("w_nx", [P, F], F32)
        wa = sb("w_na", [P, F], F32)
        w2 = sb("w_n2", [P, F], F32)
        b1 = sb("b_n1", [P, 1], F32)
        b2 = sb("b_n2", [P, F], F32)
        xr = sb("n2_xr", [P, 2, F], F32)
        hid = sb("n2_hids", [P, 2, P], F32)
        res = sb("n2_ress", [P, F], F32)
        stats = sb("n2_statss", [P, nc.vector.BN_STATS_DIM], F32)
        mv = sb("n2_mvs", [P, nc.vector.BN_AGGR_DIM], F32)
        std = sb("n2_stds", [P, 1], F32)
        rstd = sb("n2_rstds", [P, 1], F32)
        eps = sb("n2_eps", [P, 1], F32)
        y = sb("n2_ys", [P, 2, F], F32)
        psh = [t.enter_context(nc.psum_tensor(f"ps_h{b}", [P, 512], F32)) for b in range(2)]
        pso = [t.enter_context(nc.psum_tensor(f"ps_n2o{b}", [P, 512], F32)) for b in range(2)]
        with nc.Block() as block:
            @block.gpsimd
            def _(pool):
                pool.memset(eps[:, :], EPS).then_inc(s_set, 1)
                pool.memset(xr[:, :, :], 0.0).then_inc(s_set, 1)

            @block.sync
            def _(sp):
                sp.dma_start(wx[:, :], a["nW1"][0:F, :]).then_inc(s_w, 16)
                sp.dma_start(wa[:, :], a["nW1"][F:2 * F, :]).then_inc(s_w, 16)
                sp.dma_start(w2[:, :], a["nW2"]).then_inc(s_w, 16)
                sp.dma_start(b1[:, :], a["nb1"].rearrange("(n o) -> n o", o=1)).then_inc(s_w, 16)
                sp.dma_start(b2[:, :], row_vector(a["nb2"], F)).then_inc(s_w, 16)

                def load(w, b):
                    wait_count(sp, s_res, w - 1)
                    sp.dma_start(xr[:, b, :], c.x1_dram[bass.ds(w * P, P), :]).then_inc(s_x[b], 16)

                def store(w, b, rows=P):
                    sp.wait_ge(s_y, w + 1)
                    sp.dma_start(out[bass.ds(w * P, rows), :], y[0:rows, b, :]).then_inc(s_out[b], 16)
                sp.wait_ge(s_set, 2)
                load(0, 0)
                load(1, 1)
                with sp.Fori(0, NW // 2 - 1) as i:
                    for b in range(2):
                        store(2 * i + b, b)
                        load(2 * i + 2 + b, b)
                store(NW - 3, 0)
                load(NW - 1, 0)
                store(NW - 2, 1)
                store(NW - 1, 0, LAST)
                for b in range(2):
                    sp.wait_ge(s_out[b], 16 * (NW // 2 + 1 - b))

            @block.tensor
            def _(pe):
                pe.wait_ge(s_w, 80)

                def window(w, b, use):
                    wait_count(pe, s_hid, w - 1)
                    cols = bass.ds(w * P, P)
                    pe.matmul(psh[b][:, 0:P], wx[:, :], c.x1t[:, cols], start=True, stop=False)
                    pe.matmul(psh[b][:, 0:P], wa[:, :], c.vals[:, cols], start=False, stop=True).then_inc(s_pre, 1)
                    pe.wait_ge(s_hid, w + 1)
                    wait_count(pe, s_res, w - 1)
                    pe.matmul(pso[b][:, 0:F], hid[:, b, :], w2[:, :], start=True, stop=True).then_inc(s_o, 1)
                each_window(pe, window)

            @block.scalar
            def _(act):
                act.wait_ge(s_w, 80)
                act.wait_ge(s_set, 2)

                def window(w, b, use):
                    act.wait_ge(s_pre, w + 1)
                    wait_count(act, s_o, w - 1)
                    act.activation(hid[:, b, :], psh[b][:, 0:P], ACT.Silu, bias=b1[:, 0:1]).then_inc(s_hid, 1)
                    act.wait_ge(s_mv, w + 1)
                    wait_count(act, s_rstd, w)
                    act.activation(std[:, :], mv[:, 1:2], ACT.Sqrt, bias=eps[:, 0:1]).then_inc(s_std, 1)
                each_window(act, window)

            @block.vector
            def _(dve):
                dve.wait_ge(s_w, 80)

                def window(w, b, use):
                    dve.wait_ge(s_x[b], 16 * use)
                    dve.wait_ge(s_o, w + 1)
                    wait_count(dve, s_y, w)
                    dve.tensor_tensor(res[:, :], pso[b][:, 0:F], xr[:, b, :], ALU.add).then_inc(s_res, 1)
                    dve.wait_ge(s_res, w + 1)
                    dve.tensor_tensor(res[:, :], res[:, :], b2[:, :], ALU.add).then_inc(s_sum, 1)
                    dve.wait_ge(s_sum, w + 1)
                    normalise(dve, c, w, res, stats, mv, std, rstd, (s_st, s_mv, s_std, s_rstd, s_dturn))
                    wait_count(dve, s_out[b], 16 * (use - 1))
                    dve.tensor_scalar(y[:, b, :], res[:, :], mv[:, 0:1], rstd[:, 0:1], ALU.subtract,
                                      ALU.mult).then_inc(s_y, 1)
                each_window(dve, window)


def clear_semaphores(c, sems):
    nc = c.nc
    with nc.Block() as block:
        @block.gpsimd
        def _(pool):
            for s in sems:
                pool.sem_clear(s)


def program(nc, a, out):
    with ExitStack() as stack:
        c = Ctx()
        c.nc, c.stack = nc, stack
        dram = lambda n, s: nc.dram_tensor(n, s, F32, kind="Internal").ap()
        c.k_dram = dram("k_rows_dram", [NP, F])
        c.b_dram = dram("b_rows_dram", [NP, F])
        c.x1_dram = dram("x1_rows_dram", [NP, F])
        c.rec_dram = dram("records_dram", [P, NT * R])
        c.rec_rows = c.rec_dram.rearrange("p (t r) -> (p t) r", r=R)
        c.row_dram = dram("contributions_dram", [P, NT * CW])
        c.row_rows = c.row_dram.rearrange("p (t r) -> (p t) r", r=CW)
        c.pe_regs = [nc.tensor.alloc_register(f"pe_window{k}") for k in range(2 * G)]
        c.more_pe_regs = [nc.tensor.alloc_register(f"pe_window_b{k}") for k in range(2 * G)]
        c.dve_regs = [nc.vector.alloc_register(f"dve_window{k}") for k in range(2 * G)]
        sb = lambda st, n, s, d: st.enter_context(nc.sbuf_tensor(n, s, d))
        with Epoch() as c.sems:
            constants(c)
            c.work = sb(stack, "work", [P, NP], F32)
            c.vals = sb(stack, "vals", [P, NP], F32)
            c.tab = sb(stack, "tab", [P, 3, NP], BF16)
            project(c, a)
            split_table(c, 0.25)
            with ExitStack() as st:
                e = Ctx()
                e.ids = {s: sb(st, "ids_" + s, [P, ET], I32) for s in SIDES}
                e.hi = {s: sb(st, "win_of_" + s, [P, ET], F32) for s in SIDES}
                e.run = {s: sb(st, "run_" + s, [P, 2, NW], F32) for s in SIDES}
                e.rec = sb(st, "record", [P, ET, R], F32)
                c.rfill = sb(st, "rfill", [P, RF, R], F32)
                c.fill = sb(st, "cfill", [P, CF, CW], F32)
                with ExitStack() as st2:
                    e.tmpi = sb(st2, "tmp_int", [P, 2, ET], I32)
                    e.attr = sb(st2, "attr_in", [P, ET * 2], F32)
                    e.mask = sb(st2, "mask_in", [P, ET * H], F32)
                    load_edges(c, a, e)
                count_windows(c, e)
                place_edges(c, e)
            c.rec = sb(stack, "records", [P, NT, R], F32)
            with ExitStack() as st:
                c.sc = sb(st, "scores", [P, NT * H], F32)
                load_records(c)
                score(c)
                exps(c)
                normalise_values(c)
                split_table(c)
                weigh(c)
            clear_semaphores(c, c.sems.taken)
        with ExitStack() as c.sems:
            collect(c)
            c.x1t = sb(stack, "x1t", [P, NP], F32)
            nodes1(c, a)
            split_table(c)
            edges(c, a)
            nodes2(c, a, out)


def kernel(**inputs):
    import numpy as np
    import concourse.bacc as bacc
    from concourse.bass_utils import run_bass_kernel_spmd

    given = {k.split("gnn_")[-1]: np.asarray(v) for k, v in inputs.items()}
    given["xT"] = given["x"].T
    for w in ("Wq", "Wk", "Wv", "Wo"):
        given[w + "T"] = given.pop(w).T
    nc = bacc.Bacc("TRN2", target_bir_lowering=False, num_devices=1)
    arrays, a = {}, {}
    for name, v in given.items():
        v = np.ascontiguousarray(v)
        arrays[f"in_{name}_dram"] = v
        a[name] = nc.dram_tensor(f"in_{name}_dram", v.shape, mybir.dt.from_np(v.dtype), kind="ExternalInput").ap()
    out = nc.dram_tensor("out_dram", (N, F), F32, kind="ExternalOutput").ap()
    program(nc, a, out)
    r = run_bass_kernel_spmd(nc, [arrays], core_ids=[0])
    return r.results[0]["out_dram"]
```

```python
from contextlib import ExitStack

import concourse.bass as bass
from concourse import mybir

ALU = mybir.AluOpType
ACT = mybir.ActivationFunctionType
AX_X = mybir.AxisListType.X
F32 = mybir.dt.float32
BF16 = mybir.dt.bfloat16
I32 = mybir.dt.int32

P = 128
N = 6250
E = 100000
F = 128
H = 8
D = F // H
NW = -(-N // P)
NP = NW * P
LAST = N - (NW - 1) * P
EL = 125
ET = E // EL
G = 4
NT = -(-(E // P + NW) // (2 * G)) * 2 * G
SLOTS = NT * P
NTD = -(-(E // (G * P) + NW) // 4) * 4 * G
PAIRS = NT // (2 * G)
R = 16
C_ATTR, C_DST, C_SL, C_DL, C_ROW = 8, 10, 11, 12, 13
CW = 132
NOROW = float(1 << 20)
BIG = float(2 ** 100)
EPS = 1e-5
PG = 8
PB = ET // PG
EC = 10
RF = NT // 16
CF = 8


class Ctx:
    pass


def semaphores(nc, stack, names):
    return [stack.enter_context(nc.semaphore(n)) for n in names.split()]


class Epoch(ExitStack):

    def __init__(self):
        super().__init__()
        self.taken = []

    def enter_context(self, context):
        got = super().enter_context(context)
        self.taken.append(got)
        return got


def wait_count(eng, sem, count):
    if not isinstance(count, int) or count > 0:
        eng.wait_ge(sem, count)


def constants(c):
    nc, k = c.nc, c.stack
    sb = lambda n, s, d: k.enter_context(nc.sbuf_tensor(n, s, d))
    c.iota = sb("iota", [P, P], F32)
    c.ident = sb("ident", [P, P], F32)
    c.identb = sb("identb", [P, P], BF16)
    c.bigid = sb("bigid", [P, P], BF16)
    c.tri = sb("tri", [P, P], BF16)
    c.ones = sb("ones", [P, P], BF16)
    c.mtab = sb("mtab", [P, NW * H], F32)
    c.dtab = sb("dtab", [P, NW * H], F32)
    c.win = {"src": sb("win_src", [1, NT], I32), "dst": sb("win_dst", [1, NTD // G], I32)}
    (s_set,) = semaphores(nc, c.sems, "const_set")
    with ExitStack() as t:
        ii = t.enter_context(nc.sbuf_tensor("iota_int", [P, P], I32))
        with nc.Block() as block:
            @block.gpsimd
            def _(pool):
                pool.iota(ii[:, :], pattern=[[1, P]], base=0, channel_multiplier=0).then_inc(s_set, 1)
                pool.memset(c.ident[:, :], 0.0).then_inc(s_set, 1)
                pool.memset(c.identb[:, :], 0.0).then_inc(s_set, 1)
                pool.memset(c.bigid[:, :], 0.0).then_inc(s_set, 1)
                pool.memset(c.tri[:, :], 1.0).then_inc(s_set, 1)
                pool.memset(c.ones[:, :], 1.0).then_inc(s_set, 1)
                pool.wait_ge(s_set, 6)
                pool.tensor_copy(c.iota[:, :], ii[:, :])
                for m, v in ((c.ident, 1.0), (c.identb, 1.0), (c.bigid, BIG)):
                    pool.affine_select(out=m[:, :], in_=m[:, :], compare_op=ALU.not_equal, fill=v, base=0,
                                       pattern=[[-1, P]], channel_multiplier=1)
                pool.affine_select(out=c.tri[:, :], in_=c.tri[:, :], compare_op=ALU.is_gt, fill=0.0, base=0,
                                   pattern=[[1, P]], channel_multiplier=-1)


def split_table(c, name):
    nc = c.nc
    s_part, s_rest = semaphores(nc, c.sems, f"{name}_part {name}_rest")
    with nc.Block() as block:
        @block.vector
        def _(dve):
            for j in range(3):
                dve.tensor_copy(c.tab[:, j, :], c.work[:, :]).then_inc(s_part, 1)
                if j < 2:
                    dve.wait_ge(s_part, j + 1)
                    dve.tensor_tensor(c.work[:, :], c.work[:, :], c.tab[:, j, :], ALU.subtract).then_inc(s_rest, 1)
                    dve.wait_ge(s_rest, j + 1)


SIDES = ("src", "dst")


def load_edges(c, a, e):
    nc = c.nc
    s_def, s_ids, s_in, s_win, s_lane = semaphores(nc, c.sems, "defaults_set ids_in edges_in window_of lane_of")
    c.s_rfill, c.s_cfill = semaphores(nc, c.stack, "records_filled contributions_filled")
    s_zero, s_rcopy = semaphores(nc, c.sems, "fill_zeroed record_parts")
    with nc.Block() as block:
        @block.gpsimd
        def _(pool):
            for s in SIDES:
                pool.memset(e.ids[s][:, :], NW * P).then_inc(s_def, 1)
            pool.memset(e.attr[:, :], 0.0).then_inc(s_def, 1)
            pool.memset(e.mask[:, :], 0.0).then_inc(s_def, 1)
            pool.memset(e.rec[:, :, C_ROW:R], 0.0).then_inc(s_def, 1)
            pool.memset(c.rfill[:, :, :], 0.0).then_inc(s_zero, 1)
            pool.memset(c.fill[:, :, :], 0.0).then_inc(s_zero, 1)
            pool.wait_ge(s_zero, 2)
            pool.memset(c.rfill[:, :, C_SL:C_SL + 1], -1.0).then_inc(s_def, 1)
            pool.memset(c.rfill[:, :, C_ROW:C_ROW + 1], NOROW).then_inc(s_def, 1)
            pool.memset(c.fill[:, :, F:F + 1], -1.0).then_inc(s_def, 1)

        @block.sync
        def _(sp):
            sp.wait_ge(s_def, 8)
            for s in SIDES:
                sp.dma_start(e.ids[s][0:EL, :], a[s].rearrange("(p t) -> p t", p=EL)).then_inc(s_ids, 16)
            sp.dma_start(e.attr[0:EL, :], a["edge_attr_2"].rearrange("(p t) c -> p (t c)", p=EL)).then_inc(s_in, 16)
            sp.dma_start(e.mask[0:EL, :], a["edge_attr_8"].rearrange("(p t) c -> p (t c)", p=EL)).then_inc(s_in, 16)
            for j in range(NT // RF):
                sp.dma_start(c.rec_dram[:, j * RF * R:(j + 1) * RF * R],
                             c.rfill[:, :, :].rearrange("p t r -> p (t r)")).then_inc(c.s_rfill, 16)

        @block.vector
        def _(dve):
            dve.wait_ge(s_ids, 32)
            for n, s in enumerate(SIDES):
                dve.tensor_scalar(e.tmpi[:, n, :], e.ids[s][:, :], 7, None, ALU.arith_shift_right).then_inc(s_win, 1)
                dve.wait_ge(s_win, 2 * n + 1)
                dve.tensor_copy(e.hi[s][:, :], e.tmpi[:, n, :]).then_inc(s_win, 1)
                dve.wait_ge(s_win, 2 * n + 2)
                dve.tensor_scalar(e.tmpi[:, n, :], e.ids[s][:, :], P - 1, None, ALU.bitwise_and).then_inc(s_lane, 1)
                dve.wait_ge(s_lane, 2 * n + 1)
                col = C_SL if s == "src" else C_DL
                dve.tensor_copy(e.rec[:, :, col], e.tmpi[:, n, :]).then_inc(s_lane, 1)
            dve.tensor_copy(e.rec[:, :, C_DST], e.ids["dst"][:, :]).then_inc(s_rcopy, 1)

        @block.scalar
        def _(act):
            act.wait_ge(s_in, 32)
            act.activation(e.rec[:, :, 0:H], e.mask[:, :].rearrange("p (t h) -> p t h", h=H), ACT.Copy).then_inc(s_rcopy, 1)
            act.activation(e.rec[:, :, C_ATTR:C_ATTR + 2], e.attr[:, :].rearrange("p (t h) -> p t h", h=2),
                           ACT.Copy).then_inc(s_rcopy, 1)


def windows_onehot(dve, c, e, s, t0, n, out):
    return dve.tensor_tensor(out, e.hi[s][:, bass.ds(t0, n)].unsqueeze(2).to_broadcast([P, n, NW]),
                             c.iota[:, 0:NW].unsqueeze(1).to_broadcast([P, n, NW]), ALU.is_equal)


def count_windows(c, e):
    nc = c.nc
    s_oh0, s_oh1, s_mm0, s_mm1, s_sum, s_step, s_turn, s_past, s_row = semaphores(
        nc, c.sems, "count_onehot0 count_onehot1 counted0 counted1 window_sums base_step ends_turned tile_past tile_windows")
    s_oh, s_mm = (s_oh0, s_oh1), (s_mm0, s_mm1)
    (s_z, s_io) = semaphores(nc, c.sems, "zero_set tile_iota")
    with ExitStack() as t:
        sb = lambda n, s, d: t.enter_context(nc.sbuf_tensor(n, s, d))
        oh = sb("count_oh", [P, 2, 2, EC, NW], BF16)
        zero = sb("count_zero", [P, 512], BF16)
        cnt = sb("cnt", [P, 2, NW], F32)
        cnti = sb("cnti", [P, 2, NW], I32)
        cnti2 = sb("cnti2", [P, 2, NW], I32)
        til = sb("tiles", [P, 2, NW], F32)
        ends = sb("ends", [P, 2, NW], F32)
        endc = sb("end_col", [P, 2], F32)
        one = sb("one_f", [P, NW], F32)
        past = sb("past", [P, 2, NT], BF16)
        tio = sb("tile_io", [P, NT], F32)
        tii = sb("tile_ii", [P, NT], I32)
        ps_c = [t.enter_context(nc.psum_tensor(f"ps_count{n}", [P, 512], F32)) for n in range(2)]
        ps_e = t.enter_context(nc.psum_tensor("ps_ends", [P, 512], F32))
        ps_w = [t.enter_context(nc.psum_tensor(f"ps_win{n}", [P, 512], F32)) for n in range(3)]
        IT = ET // EC
        HT = NT // 2
        UNIT = (P, G * P)
        PIECES = ((0, 0, HT), (0, HT, HT), (1, 0, NTD // G))
        with nc.Block() as block:
            @block.gpsimd
            def _(pool):
                pool.memset(zero[:, :], 0.0).then_inc(s_z, 1)
                pool.memset(one[:, :], 1.0).then_inc(s_z, 1)
                pool.memset(endc[:, :], 1e9).then_inc(s_z, 1)
                pool.iota(tii[:, :], pattern=[[1, NT]], base=0, channel_multiplier=0).then_inc(s_io, 1)
                pool.wait_ge(s_io, 1)
                pool.tensor_copy(tio[:, :], tii[:, :]).then_inc(s_io, 1)

            @block.vector
            def _(dve):
                def one_hots(i, half):
                    for n in range(2):
                        wait_count(dve, s_mm[n], i - 1)
                        windows_onehot(dve, c, e, SIDES[n], i * EC, EC, oh[:, n, half]).then_inc(s_oh[n], 1)
                for half in range(2):
                    one_hots(half, half)
                with dve.Fori(1, IT // 2) as i:
                    for half in range(2):
                        one_hots(2 * i + half, half)
                for n in range(2):
                    dve.wait_ge(s_mm[n], IT + 1)
                    dve.tensor_reduce(cnt[:, n, :], ps_c[n][:, 0:EC * NW].rearrange("p (j w) -> p w j", w=NW),
                                      AX_X, ALU.add).then_inc(s_sum, 1)
                dve.wait_ge(s_sum, 2)
                dve.wait_ge(s_z, 3)
                steps = [0]

                def step(ins):
                    steps[0] += 1
                    ins.then_inc(s_step, 1)
                    dve.wait_ge(s_step, steps[0])
                for n in range(2):
                    step(dve.tensor_scalar(cnti[:, n, :], cnt[:, n, :], float(UNIT[n] - 1), None, ALU.add))
                    step(dve.tensor_scalar(cnti2[:, n, :], cnti[:, n, :], UNIT[n].bit_length() - 1, None,
                                           ALU.arith_shift_right))
                step(dve.tensor_copy(til[:, :, :], cnti2[:, :, :]))
                for n in range(2):
                    step(dve.tensor_tensor_scan(ends[:, n, :], one[:, :], til[:, n, :], 0.0, ALU.mult, ALU.add))
                step(dve.tensor_tensor(til[:, :, :], ends[:, :, :], til[:, :, :], ALU.subtract))
                for n in range(2):
                    step(dve.tensor_scalar(e.run[SIDES[n]][:, 0, :], til[:, n, :], float(UNIT[n]), None, ALU.mult))
                dve.wait_ge(s_turn, 2)
                for n in range(2):
                    step(dve.tensor_copy(endc[0:NW, n:n + 1], ps_e[0:NW, n * P:n * P + 1]))
                dve.wait_ge(s_io, 2)
                for n in range(2):
                    dve.tensor_scalar(past[:, n, :], tio[:, :], endc[:, n:n + 1], None, ALU.is_ge).then_inc(s_past, 1)
                for j, (n, at, size) in enumerate(PIECES):
                    dve.wait_ge(s_row, j + 1)
                    dve.tensor_scalar(c.win[SIDES[n]][0:1, at:at + size], ps_w[j][0:1, 0:size], float(NW - 1), None,
                                      ALU.min)

            @block.tensor
            def _(pe):
                pe.wait_ge(s_z, 3)
                for n in range(2):
                    pe.matmul(ps_c[n][:, 0:EC * NW], c.ones[:, :], zero[:, 0:EC * NW], start=True, stop=False)
                with pe.Fori(0, IT // 2) as i:
                    for half in range(2):
                        for n in range(2):
                            pe.wait_ge(s_oh[n], 2 * i + half + 1)
                            pe.matmul(ps_c[n][:, 0:EC * NW], c.ones[:, :],
                                      oh[:, n, half].rearrange("p j w -> p (j w)"), start=False, stop=False,
                                      skip_group_check=True).then_inc(s_mm[n], 1)
                for n in range(2):
                    pe.matmul(ps_c[n][:, 0:EC * NW], c.ones[:, :], zero[:, 0:EC * NW], start=False,
                              stop=True).then_inc(s_mm[n], 1)
                pe.wait_ge(s_step, 7)
                for n in range(2):
                    pe.transpose(ps_e[0:NW, n * P:(n + 1) * P], ends[:, n, :], c.ident[:, :]).then_inc(s_turn, 1)
                for j, (n, at, size) in enumerate(PIECES):
                    pe.wait_ge(s_past, n + 1)
                    pe.matmul(ps_w[j][:, 0:size], c.ones[:, :], past[:, n, at:at + size],
                              start=True, stop=True).then_inc(s_row, 1)


def place_and_project(c, e, a):
    nc = c.nc
    names = ("place_onehot before after_start masked slot running slot_int slot_lane slot_tile lane_part "
             "row_of rec_slot row_index")
    (s_oh, s_cum, s_add, s_msk, s_slot, s_run, s_int, s_lane, s_tile, s_lp, s_row, s_rec, s_idx) = semaphores(
        nc, c.sems, names)
    s_sent = semaphores(nc, c.stack, "records_sent0 records_sent1")
    (s_turn, s_init) = semaphores(nc, c.sems, "scatter_turn place_init")
    s_x = semaphores(nc, c.sems, "x_in0 x_in1")
    s_kout = semaphores(nc, c.sems, "k_out0 k_out1")
    s_w, s_one, s_mm, s_q, s_k, s_v, s_vturn, s_qp, s_qr, s_tab = semaphores(
        nc, c.sems, "w_in one_set qkv_ready q_read k_read v_read v_turn q_part q_rest q_table")
    IT = ET // PG
    LOT = 4
    with ExitStack() as t:
        sb = lambda n, s, d: t.enter_context(nc.sbuf_tensor(n, s, d))
        oh = {s: sb("place_oh_" + s, [P, 2, PG + 1, NW], BF16) for s in SIDES}
        cum = {s: sb("cum_" + s, [P, PG, NW], F32) for s in SIDES}
        slot = sb("slot", [P, 2, PG], F32)
        sloti = sb("sloti", [P, 2, PG], I32)
        lane = sb("slot_lane_i", [P, 2, PG], I32)
        tile = sb("slot_tile_i", [P, 2, PG], I32)
        lanef = sb("slot_lane_f", [P, 2, PG], F32)
        idx = sb("row_idx", [P, 2, PG], I32)
        out = sb("rec_out", [P, 2, PG, R], F32)
        norow = sb("norow", [P, 1], F32)
        lanes = sb("lanes_i", [P, 1], I32)
        w = sb("w_qkv", [P, 3 * F], F32)
        bias = sb("b_qkv", [1, 3 * F], F32)
        one = sb("one_row", [1, P], F32)
        xt = sb("xt", [P, 2, P], F32)
        kt = sb("k_rows", [P, 2, F], F32)
        qt = sb("q_rows", [P, 2, F], F32)
        qp = sb("q_parts", [P, 3, F], BF16)
        qr = sb("q_rests", [P, 2, F], F32)
        ps = {s: [t.enter_context(nc.psum_tensor(f"ps_before_{s}{b}", [P, 512], F32)) for b in range(2)]
              for s in SIDES}
        psx = [t.enter_context(nc.psum_tensor(f"ps_qkv{b}", [P, 512], F32)) for b in range(2)]
        with nc.Block() as block:
            @block.sync
            def _(sp):
                for j, (m, v) in enumerate((("WqT", "bq"), ("WkT", "bk"), ("WvT", "bv"))):
                    sp.dma_start(w[:, j * F:(j + 1) * F], a[m]).then_inc(s_w, 16)
                    sp.dma_start(bias[:, j * F:(j + 1) * F], a[v].rearrange("(o n) -> o n", o=1)).then_inc(s_w, 16)

                def load(win, n, cols=P):
                    wait_count(sp, s_mm, win - 1)
                    sp.dma_start(xt[:, n, 0:cols], a["xT"][:, bass.ds(win * P, cols)]).then_inc(s_x[n], 16)

                def store(win, n):
                    sp.wait_ge(s_k, win + 1)
                    sp.dma_start(c.k_dram[bass.ds(win * P, P), :], kt[:, n, :]).then_inc(s_kout[n], 16)
                load(0, 0)
                load(1, 1)
                with sp.Fori(0, NW // 2 - 1) as i:
                    for n in range(2):
                        store(2 * i + n, n)
                        load(2 * i + 2 + n, n)
                store(NW - 3, 0)
                load(NW - 1, 0, LAST)
                store(NW - 2, 1)
                store(NW - 1, 0)
                sp.wait_ge(s_kout[0], 16 * (NW // 2 + 1))
                sp.wait_ge(s_kout[1], 16 * (NW // 2))
                sp.wait_ge(c.s_cfill, 16 * (NTD // CF))

            @block.vector
            def _(dve):
                dve.wait_ge(s_init, 4)

                def one_hots(g, half):
                    wait_count(dve, s_cum, 2 * (g - 1))
                    wait_count(dve, s_msk, 2 * (g - 1))
                    for s in SIDES:
                        windows_onehot(dve, c, e, s, g * PG, PG, oh[s][:, half, 0:PG]).then_inc(s_oh, 1)

                def query_part(win, n, j):
                    src = qt[:, n, :] if j == 0 else qr[:, j - 1, :]
                    if j == 0:
                        dve.wait_ge(s_q, win + 1)
                        wait_count(dve, s_tab, win)
                    else:
                        dve.wait_ge(s_qr, 2 * win + j)
                    dve.tensor_copy(qp[:, j, :], src).then_inc(s_qp, 1)

                def query_rest(win, n, j):
                    src = qt[:, n, :] if j == 0 else qr[:, j - 1, :]
                    dve.wait_ge(s_qp, 3 * win + j + 1)
                    dve.tensor_tensor(qr[:, j, :], src, qp[:, j, :], ALU.subtract).then_inc(s_qr, 1)

                def query_table(win):
                    dve.wait_ge(s_qp, 3 * win + 3)
                    dve.sem_inc(s_vturn, 1)
                    dve.tensor_copy(c.tab[:, :, bass.ds(win * F, F)], qp[:, :, :]).then_inc(s_tab, 1)

                def place(g, half, win=None, win_half=None, ahead=True):
                    if ahead:
                        one_hots(g + 1, 1 - half)
                    if win is not None:
                        query_part(win, win_half, 0)
                    for n, s in enumerate(SIDES):
                        dve.wait_ge(s_cum, 2 * g + n + 1)
                        start = e.run[s][:, half:half + 1, :]
                        before = ps[s][half]
                        dve.tensor_tensor(cum[s][:, :, :], before[:, 0:PG * NW].rearrange("p (j w) -> p j w", w=NW),
                                          start.to_broadcast([P, PG, NW]), ALU.add).then_inc(s_add, 1)
                        dve.tensor_tensor(e.run[s][:, 1 - half, :], before[:, PG * NW:(PG + 1) * NW],
                                          e.run[s][:, half, :], ALU.add).then_inc(s_run, 1)
                        if win is not None:
                            query_rest(win, win_half, n)
                        dve.wait_ge(s_add, 2 * g + n + 1)
                        dve.tensor_tensor(cum[s][:, :, :], cum[s][:, :, :], oh[s][:, half, 0:PG],
                                          ALU.mult).then_inc(s_msk, 1)
                        if win is not None:
                            query_part(win, win_half, n + 1)
                        dve.wait_ge(s_msk, 2 * g + n + 1)
                        dve.tensor_reduce(slot[:, n, :], cum[s][:, :, :], AX_X, ALU.add).then_inc(s_slot, 1)
                    if win is not None:
                        query_table(win)
                    dve.wait_ge(s_slot, 2 * g + 2)
                    dve.wait_ge(s_run, 2 * g + 2)
                    dve.tensor_copy(sloti[:, :, :], slot[:, :, :]).then_inc(s_int, 1)
                    dve.wait_ge(s_int, g + 1)
                    dve.tensor_scalar(lane[:, :, :], sloti[:, :, :], P - 1, None, ALU.bitwise_and).then_inc(s_lane, 1)
                    dve.tensor_scalar(tile[:, :, :], sloti[:, :, :], 7, None, ALU.arith_shift_right).then_inc(s_tile, 1)
                    dve.wait_ge(s_lane, g + 1)
                    for n, tiles in enumerate((NT, NTD)):
                        dve.tensor_scalar(lanef[:, n, :], lane[:, n, :], float(tiles), norow[:, 0:1], ALU.mult,
                                          ALU.add).then_inc(s_lp, 1)
                    dve.wait_ge(s_lp, 2 * g + 2)
                    dve.wait_ge(s_tile, g + 1)
                    wait_count(dve, s_sent[half], 8 * PG * (g - half))
                    dve.tensor_tensor(idx[:, half, :], lanef[:, 0, :], tile[:, 0, :], ALU.add).then_inc(s_idx, 1)
                    dve.tensor_copy(out[:, half, :, :], e.rec[:, bass.ds(g * PG, PG), :]).then_inc(s_rec, 1)
                    dve.wait_ge(s_rec, g + 1)
                    dve.tensor_tensor(out[:, half, :, C_ROW], lanef[:, 1, :], tile[:, 1, :], ALU.add).then_inc(s_row, 1)
                    dve.wait_ge(s_row, g + 1)

                def lot(i, last=False):
                    for n in range(LOT):
                        win = 2 * i + n // 2 if n % 2 == 0 and not (last and n) else None
                        place(LOT * i + n, n % 2, win, n // 2, not (last and n == LOT - 1))
                one_hots(0, 0)
                lot(0)
                with dve.Fori(1, IT // LOT - 1) as i:
                    lot(i)
                lot(IT // LOT - 1, True)

            @block.scalar
            def _(act):
                def window(win, n):
                    act.wait_ge(s_mm, win + 1)
                    wait_count(act, s_qp, 3 * (win - 1))
                    act.activation(qt[:, n, :], psx[n][:, 0:F], ACT.Copy, scale=0.25).then_inc(s_q, 1)
                    wait_count(act, s_kout[n], 8 * (win - n))
                    act.activation(kt[:, n, :], psx[n][:, F:2 * F], ACT.Copy).then_inc(s_k, 1)
                    act.activation(c.vals[:, bass.ds(win * F, F)], psx[n][:, 2 * F:3 * F], ACT.Copy).then_inc(s_v, 1)

                def fill(j):
                    act.dma_start(c.row_dram[:, bass.ds(j * CF * CW, CF * CW)],
                                  c.fill[:, :, :].rearrange("p t r -> p (t r)")).then_inc(c.s_cfill, 16)
                fills = NTD // CF // (NW // 2)
                for n in range(2):
                    window(n, n)
                with act.Fori(1, NW // 2) as i:
                    for n in range(2):
                        window(2 * i + n, n)
                    for n in range(fills):
                        fill((i - 1) * fills + n)
                window(NW - 1, 0)
                for j in range((NW // 2 - 1) * fills, NTD // CF):
                    fill(j)

            @block.tensor
            def _(pe):
                pe.wait_ge(s_init, 4)
                pe.wait_ge(s_w, 96)
                pe.wait_ge(s_one, 1)

                def project(win, n):
                    pe.wait_ge(s_x[n], 8 * (win - n) + 16)
                    wait_count(pe, s_v, win - 1)
                    pe.matmul(psx[n][:, 0:3 * F], one[:, :], bias[:, :], start=True, stop=False)
                    pe.matmul(psx[n][:, 0:3 * F], xt[:, n, :], w[:, :], start=False, stop=True).then_inc(s_mm, 1)

                def before(g, half):
                    for n, s in enumerate(SIDES):
                        pe.wait_ge(s_oh, 2 * g + n + 1)
                        wait_count(pe, s_run, 2 * (g - 1))
                        to = ps[s][half]
                        flat = oh[s][:, half].rearrange("p j w -> p (j w)")
                        pe.matmul(to[:, 0:(PG + 1) * NW], c.tri[:, :], flat, start=True, stop=False)
                        for j in range(PG):
                            m = PG - j
                            ins = pe.matmul(to[:, (j + 1) * NW:(PG + 1) * NW].rearrange("p (j w) -> p j w", w=NW),
                                            c.ones[:, :], oh[s][:, half, j:j + 1, :].to_broadcast([P, m, NW]),
                                            start=False, stop=(j == PG - 1))
                        ins.then_inc(s_cum, 1)

                def lot(i, last=False):
                    for n in range(LOT):
                        before(LOT * i + n, n % 2)
                        if n % 2 == 0 and not (last and n):
                            project(2 * i + n // 2, n // 2)
                lot(0)
                with pe.Fori(1, IT // LOT - 1) as i:
                    lot(i)
                lot(IT // LOT - 1, True)

            @block.gpsimd
            def _(pool):
                for s in SIDES:
                    pool.memset(oh[s][:, :, PG:PG + 1, :], 0.0).then_inc(s_init, 1)
                pool.iota(lanes[:, :], pattern=[[0, 1]], base=0, channel_multiplier=1).then_inc(s_init, 1)
                pool.memset(one[:, :], 1.0).then_inc(s_one, 1)
                pool.wait_ge(s_init, 3)
                pool.tensor_scalar(norow[:, :], lanes[:, :], float(EL), NOROW, ALU.is_ge, ALU.mult).then_inc(s_init, 1)
                pool.wait_ge(c.s_rfill, 16 * (NT // RF))

                def send(g, half):
                    pool.wait_ge(s_row, g + 1)
                    pool.wait_ge(s_idx, g + 1)
                    pool.sem_inc(s_turn, 1)
                    for j in range(PG):
                        pool.indirect_dma_start(
                            c.rec_rows, bass.IndirectOffsetOnAxis(ap=idx[:, half, j:j + 1], axis=0),
                            out[:, half, j, :], None, bounds_check=SLOTS - 1, oob_is_err=False).then_inc(s_sent[half], 16)
                with pool.Fori(0, IT // 2) as i:
                    for half in range(2):
                        send(2 * i + half, half)
                for half in range(2):
                    pool.wait_ge(s_sent[half], 16 * PG * (IT // 2))


NG = NT // G
RING = 4


def each_group(eng, step, lead=0, lag=0, groups=NG):
    for g in range(-lead, RING):
        step(g, g % RING)
    with eng.Fori(1, groups // RING - 1) as i:
        for r in range(RING):
            step(RING * i + r, r)
    for g in range(groups - RING, groups + lag):
        step(g, g % RING)


def group_at(g, r, by, groups=NG):
    there = not isinstance(g, int) or 0 <= g + by < groups
    return g + by, (r + by) % RING, there


def ring_count(g, r, each):
    return (g - r + RING) * (each // RING)


def load_windows(eng, c, regs, side, g, n=1):
    eng.reg_load(regs[:n * G], c.win[side][0:1, bass.ds(g * G, n * G)])
    return [eng.snap(r, min_val=0, max_val=NW - 1) for r in regs[:n * G]]


def lane_onehot(dve, c, lanes, out):
    return dve.tensor_tensor(out, c.iota[:, :].unsqueeze(1).to_broadcast([P, G, P]),
                             lanes.unsqueeze(2).to_broadcast([P, G, P]), ALU.is_equal)


def load_records(c):
    nc = c.nc
    (s_r,) = semaphores(nc, c.sems, "records_in")
    with nc.Block() as block:
        @block.sync
        def _(sp):
            sp.dma_start(c.rec[:, :, :].rearrange("p t r -> p (t r)"), c.rec_dram[:, :]).then_inc(s_r, 16)
            sp.wait_ge(s_r, 16)

        @block.vector
        def _(dve):
            dve.memset(c.mtab[:, :], -1e30)


def score(c):
    nc = c.nc
    names = ("sc_onehot sc_turned sc_onehot_t sc_onehot_m sc_q sc_index sc_prod sc_dot sc_score sc_hi sc_kept sc_rest "
             "sc_mid sc_rest2 sc_parts sc_parts_turned sc_parts_t sc_spread sc_tilemax sc_max")
    (s_oh, s_tr, s_oht, s_ohm, s_q, s_idx, s_prod, s_dot, s_sc, s_hi, s_kept, s_rest, s_mid, s_rest2, s_parts, s_ptr,
     s_pt, s_mx, s_red, s_max) = semaphores(nc, c.sems, names)
    s_k = semaphores(nc, c.stack, "sc_k_in0 sc_k_in1 sc_k_in2 sc_k_in3")
    s_turn, s_init, s_isel, s_one, s_lane, s_far = semaphores(
        nc, c.sems, "sc_gather_turn sc_init sc_sel_set sc_one_set sc_lanes_in sc_distances")
    GH = G * H
    with ExitStack() as t:
        sb = lambda n, s, d: t.enter_context(nc.sbuf_tensor(n, s, d))
        oh = sb("sc_oh", [P, RING, G, P], BF16)
        oht = sb("sc_oht", [P, 2, G, P], BF16)
        ohm = sb("sc_ohm", [P, RING, G, P], BF16)
        idx = sb("sc_idx", [P, RING, G], I32)
        lanes = sb("sc_lanes", [P, RING, G], F32)
        far = sb("sc_far", [P, G, P], F32)
        one = sb("sc_one", [P, 1], F32)
        kg = sb("sc_k", [P, RING, G, F], F32)
        prod = sb("sc_prods", [P, G * F], F32)
        dot = sb("sc_dots", [P, G, H], F32)
        rest = sb("sc_rests", [P, 2, GH], F32)
        parts = sb("sc_split", [P, 2, P], BF16)
        pt = sb("sc_split_t", [P, 2, P], BF16)
        red = sb("sc_red", [P, 2, G, H], F32)
        sel = sb("sc_sel", [P, GH, P], BF16)
        psq = [t.enter_context(nc.psum_tensor(f"ps_q{b}", [P, 512], F32)) for b in range(2)]
        pst = t.enter_context(nc.psum_tensor("ps_oht", [P, 1024], BF16))
        psp = t.enter_context(nc.psum_tensor("ps_pt", [P, 1024], BF16))
        psm = [t.enter_context(nc.psum_tensor(f"ps_spread{b}", [P, 1024], F32)) for b in range(2)]
        with nc.Block() as block:
            @block.gpsimd
            def _(pool):
                pool.memset(sel[:, :, :], 0.0).then_inc(s_isel, 1)
                pool.memset(parts[:, :, :], 0.0).then_inc(s_init, 1)
                pool.memset(one[:, :], 1.0).then_inc(s_one, 1)
                for j in range(3):
                    pool.wait_ge(s_isel, j + 1)
                    pool.affine_select(out=sel[:, :, :], in_=sel[:, :, :], compare_op=ALU.not_equal, fill=1.0,
                                       base=-j * GH, pattern=[[-1, GH], [0, P]],
                                       channel_multiplier=1).then_inc(s_isel, 1)

                def gather(g, r):
                    pool.wait_ge(s_idx, g + 1)
                    wait_count(pool, s_prod, g - RING + 1)
                    pool.sem_inc(s_turn, 1)
                    for k in range(G):
                        pool.indirect_dma_start(kg[:, r, k, :], None, c.k_dram[:, :],
                                                bass.IndirectOffsetOnAxis(ap=idx[:, r, k:k + 1], axis=0)
                                                ).then_inc(s_k[r], 16)
                each_group(pool, gather)

            @block.vector
            def _(dve):
                dve.wait_ge(s_init, 1)

                def front(g, r):
                    wait_count(dve, s_prod, g - RING + 1)
                    wait_count(dve, s_oh, g - RING + 1)
                    rec = c.rec[:, bass.ds(g * G, G), :]
                    dve.tensor_copy(idx[:, r, :], rec[:, :, C_DST]).then_inc(s_idx, 1)
                    dve.tensor_copy(lanes[:, r, :], rec[:, :, C_SL]).then_inc(s_lane, 1)

                flat = dot[:, :, :].rearrange("p k h -> p (k h)")

                def product(g, r):
                    dve.wait_ge(s_q, g + 1)
                    dve.wait_ge(s_k[r], ring_count(g, r, 16 * G))
                    dve.tensor_tensor(prod[:, :], psq[r % 2][:, :], kg[:, r].rearrange("p k f -> p (k f)"),
                                      ALU.mult).then_inc(s_prod, 1)

                def dots(g, r):
                    dve.wait_ge(s_prod, g + 1)
                    wait_count(dve, s_kept, g)
                    dve.tensor_reduce(flat, prod[:, :].rearrange("p (j d) -> p j d", d=D), AX_X,
                                      ALU.add).then_inc(s_dot, 1)

                def add_mask(g, r):
                    dve.wait_ge(s_dot, g + 1)
                    dve.tensor_tensor(dot[:, :, :], dot[:, :, :], c.rec[:, bass.ds(g * G, G), 0:H],
                                      ALU.add).then_inc(s_sc, 1)

                def first_part(g, r):
                    dve.wait_ge(s_sc, g + 1)
                    wait_count(dve, s_ptr, g - 1)
                    dve.tensor_copy(parts[:, r % 2, 0:GH], flat).then_inc(s_hi, 1)
                    dve.tensor_copy(c.sc[:, bass.ds(g * GH, GH)], flat).then_inc(s_kept, 1)

                def first_rest(g, r):
                    dve.wait_ge(s_hi, g + 1)
                    dve.tensor_tensor(rest[:, 0, :], flat, parts[:, r % 2, 0:GH], ALU.subtract).then_inc(s_rest, 1)

                def second_part(g, r):
                    dve.wait_ge(s_rest, g + 1)
                    dve.tensor_copy(parts[:, r % 2, GH:2 * GH], rest[:, 0, :]).then_inc(s_mid, 1)

                def second_rest(g, r):
                    dve.wait_ge(s_mid, g + 1)
                    dve.tensor_tensor(rest[:, 1, :], rest[:, 0, :], parts[:, r % 2, GH:2 * GH],
                                      ALU.subtract).then_inc(s_rest2, 1)

                def third_part(g, r):
                    dve.wait_ge(s_rest2, g + 1)
                    dve.tensor_copy(parts[:, r % 2, 2 * GH:3 * GH], rest[:, 1, :]).then_inc(s_parts, 1)

                def tile_maximum(g, r, k):
                    dve.wait_ge(s_mx, G * g + k + 1)
                    wait_count(dve, s_max, G * (g - 2) + k + 1)
                    dve.tensor_reduce(red[:, r % 2, k, :], psm[k % 2][:, :].rearrange("p (h e) -> p h e", h=H),
                                      AX_X, ALU.max).then_inc(s_red, 1)

                def table_maximum(g, r, k, win):
                    dve.wait_ge(s_red, G * g + k + 1)
                    wait_count(dve, s_max, G * g + k)
                    m = c.mtab[:, bass.ds(win[k] * H, H)]
                    dve.tensor_tensor(m, m, red[:, r % 2, k, :], ALU.max).then_inc(s_max, 1)

                def step(g, r):
                    here = group_at(g, r, 0)[2]
                    before, before_r, any_before = group_at(g, r, -1)
                    old, old_r, any_old = group_at(g, r, -2)
                    ahead, ahead_r, any_ahead = group_at(g, r, 3)
                    score_work = ((dots,), (add_mask, first_part), (first_rest,), (second_part,))
                    if any_ahead:
                        front(ahead, ahead_r)
                    if here:
                        product(g, r)
                    win = load_windows(dve, c, c.dve_regs, "src", old) if any_old else None
                    for k in range(G):
                        if any_old:
                            table_maximum(old, old_r, k, win)
                        if here:
                            for work in score_work[k]:
                                work(g, r)
                        if any_before:
                            tile_maximum(before, before_r, k)
                    if here:
                        second_rest(g, r)
                        third_part(g, r)
                each_group(dve, step, lead=3, lag=2)

            @block.scalar
            def _(act):
                act.wait_ge(s_one, 1)

                def distances(g, r):
                    act.wait_ge(s_lane, g + 1)
                    wait_count(act, s_oh, g)
                    for k in range(G):
                        act.activation(far[:, k, :], c.iota[:, :], ACT.Square, bias=lanes[:, r, k:k + 1],
                                       scale=-1.0).then_inc(s_far, 1)

                def near(g, r):
                    act.wait_ge(s_far, G * (g + 1))
                    wait_count(act, s_tr, g - RING + 1)
                    act.activation(oh[:, r].rearrange("p k n -> p (k n)"), far[:, :, :].rearrange("p k n -> p (k n)"),
                                   ACT.Relu, bias=one[:, 0:1], scale=-2.0).then_inc(s_oh, 1)

                def one_hots(g, r):
                    act.wait_ge(s_tr, g + 1)
                    wait_count(act, s_q, g - 1)
                    act.activation(oht[:, r % 2].rearrange("p k n -> p (k n)"), pst[:, 0:G * P],
                                   ACT.Copy).then_inc(s_oht, 1)
                    wait_count(act, s_mx, G * (g - RING + 1))
                    act.activation(ohm[:, r].rearrange("p k n -> p (k n)"), pst[:, 0:G * P], ACT.Copy,
                                   bias=-1.0).then_inc(s_ohm, 1)

                def split(g, r):
                    act.wait_ge(s_ptr, g + 1)
                    wait_count(act, s_mx, G * (g - 1))
                    act.activation(pt[:, r % 2, :], psp[:, 0:P], ACT.Copy).then_inc(s_pt, 1)

                def step(g, r):
                    for by, work in ((-1, split), (3, distances), (3, near), (2, one_hots)):
                        at, slot, there = group_at(g, r, by)
                        if there:
                            work(at, slot)
                each_group(act, step, lead=3, lag=1)

            @block.tensor
            def _(pe):
                pe.wait_ge(s_isel, 4)
                pe.wait_ge(s_init, 1)

                def turn(g, r):
                    pe.wait_ge(s_oh, g + 1)
                    wait_count(pe, s_ohm, g)
                    for k in range(G):
                        ins = pe.transpose(pst[:, k * P:(k + 1) * P], oh[:, r, k, :], c.identb[:, :])
                    ins.then_inc(s_tr, 1)

                def queries(g, r):
                    b = r % 2
                    win = load_windows(pe, c, c.pe_regs, "src", g)
                    pe.wait_ge(s_oht, g + 1)
                    wait_count(pe, s_prod, g - 1)
                    for k in range(G):
                        for j in range(3):
                            ins = pe.matmul(psq[b][:, k * F:(k + 1) * F], oht[:, b, k, :],
                                            c.tab[:, j, bass.ds(win[k] * F, F)], start=(j == 0), stop=(j == 2))
                    ins.then_inc(s_q, 1)

                def turn_parts(g, r):
                    pe.wait_ge(s_parts, g + 1)
                    wait_count(pe, s_pt, g)
                    pe.transpose(psp[:, 0:P], parts[:, r % 2, :], c.identb[:, :]).then_inc(s_ptr, 1)

                def spread(g, r, tiles):
                    pe.wait_ge(s_pt, g + 1)
                    pe.wait_ge(s_ohm, g + 1)
                    for k in tiles:
                        wait_count(pe, s_red, G * g + k - 1)
                        for q in range(2):
                            pe.matmul(psm[k % 2][:, q * 512:(q + 1) * 512].rearrange("p (h e) -> p h e", h=4),
                                      c.bigid[:, :], ohm[:, r, k, :].unsqueeze(1).to_broadcast([P, 4, P]),
                                      start=True, stop=False)
                            for h in range(4):
                                kh = k * H + q * 4 + h
                                ins = pe.matmul(psm[k % 2][:, (q * 4 + h) * P:(q * 4 + h + 1) * P], sel[:, kh, :],
                                                pt[:, r % 2, :], start=False, stop=(h == 3))
                        ins.then_inc(s_mx, 1)

                def step(g, r):
                    spread_first = lambda g, r: spread(g, r, (0, 1))
                    spread_last = lambda g, r: spread(g, r, (2, 3))
                    for by, work in ((-1, turn_parts), (-1, spread_first), (2, turn), (1, queries), (-1, spread_last)):
                        at, slot, there = group_at(g, r, by)
                        if there:
                            work(at, slot)
                each_group(pe, step, lead=2, lag=1)


def split_maximum(c, mt):
    nc = c.nc
    s_part, s_rest = semaphores(nc, c.sems, "max_part max_rest")
    with ExitStack() as t:
        rest = t.enter_context(nc.sbuf_tensor("max_rests", [P, NW, H], F32))
        with nc.Block() as block:
            @block.vector
            def _(dve):
                dve.tensor_copy(rest[:, :, :], c.mtab[:, :].rearrange("p (w h) -> p w h", h=H)).then_inc(s_rest, 1)
                for j in range(3):
                    dve.wait_ge(s_rest, j + 1)
                    dve.tensor_copy(mt[:, :, j, :], rest[:, :, :]).then_inc(s_part, 1)
                    if j < 2:
                        dve.wait_ge(s_part, j + 1)
                        dve.tensor_tensor(rest[:, :, :], rest[:, :, :], mt[:, :, j, :], ALU.subtract).then_inc(s_rest, 1)


LG = 4
LT = LG * G
LOTS = NT // LT
SW = 32


def exps(c):
    nc = c.nc
    names = ("ex_onehot ex_turned ex_onehot_t ex_m ex_mm ex_less ex_exp ex_kept ex_part ex_rest ex_sums ex_zero ex_end "
             "ex_total")
    (s_oh, s_tr, s_oht, s_m, s_mm, s_d, s_ex, s_kept, s_part, s_rest, s_sum, s_z, s_end, s_tot) = semaphores(
        nc, c.sems, names)
    with ExitStack() as t:
        sb = lambda n, s, d: t.enter_context(nc.sbuf_tensor(n, s, d))
        mt = sb("max_parts", [P, NW, 3, H], BF16)
        split_maximum(c, mt)
        oh = c.work[:, 0:RING * LT * P // 2].bitcast(BF16).rearrange("p (r k n) -> p r k n", r=RING, n=P)
        oht = sb("ex_oht", [P, 2, G, P], BF16)
        top = sb("ex_tops", [P, LT, H], F32)
        less = sb("ex_lesses", [P, 2, LT, H], F32)
        ex = sb("ex_exps", [P, 2, LT, H], F32)
        rest = sb("ex_rests", [P, 2, LT, H], F32)
        parts = sb("ex_split", [P, 2, LT, 3, H], BF16)
        zero = sb("ex_zeros", [P, 512], BF16)
        pst = [t.enter_context(nc.psum_tensor(f"ps_ex_oht{b}", [P, 1024], BF16)) for b in range(2)]
        psm = [t.enter_context(nc.psum_tensor(f"ps_ex_m{b}", [P, 512], F32)) for b in range(2)]
        psd = t.enter_context(nc.psum_tensor("ps_sums", [P, 2048], F32))
        with nc.Block() as block:
            @block.gpsimd
            def _(pool):
                pool.memset(zero[:, :], 0.0).then_inc(s_z, 1)

            @block.vector
            def _(dve):
                def front(g, r):
                    wait_count(dve, s_sum, g - RING + 1)
                    dve.tensor_tensor(oh[:, r], c.iota[:, :].unsqueeze(1).to_broadcast([P, LT, P]),
                                      c.rec[:, bass.ds(g * LT, LT), C_SL].unsqueeze(2).to_broadcast([P, LT, P]),
                                      ALU.is_equal).then_inc(s_oh, 1)

                def difference(g, r):
                    b = r % 2
                    dve.wait_ge(s_m, LG * (g + 1))
                    wait_count(dve, s_d, g)
                    dve.tensor_reduce(top[:, :, :], psm[b][:, 0:LT * 3 * H].rearrange("p (k j h) -> p k h j", j=3, h=H),
                                      AX_X, ALU.add).then_inc(s_mm, 1)
                    dve.wait_ge(s_mm, g + 1)
                    wait_count(dve, s_ex, g - 1)
                    dve.tensor_tensor(less[:, b, :, :],
                                      c.sc[:, bass.ds(g * LT * H, LT * H)].rearrange("p (k h) -> p k h", h=H),
                                      top[:, :, :], ALU.subtract).then_inc(s_d, 1)

                def split(g, r):
                    b = r % 2
                    dve.wait_ge(s_ex, g + 1)
                    wait_count(dve, s_sum, g - 1)
                    dve.tensor_copy(parts[:, b, :, 0, :], ex[:, b, :, :]).then_inc(s_part, 1)
                    dve.tensor_copy(c.sc[:, bass.ds(g * LT * H, LT * H)],
                                    ex[:, b, :, :].rearrange("p k h -> p (k h)")).then_inc(s_kept, 1)
                    dve.wait_ge(s_part, 3 * g + 1)
                    dve.tensor_tensor(rest[:, 0, :, :], ex[:, b, :, :], parts[:, b, :, 0, :],
                                      ALU.subtract).then_inc(s_rest, 1)
                    dve.wait_ge(s_rest, 2 * g + 1)
                    dve.tensor_copy(parts[:, b, :, 1, :], rest[:, 0, :, :]).then_inc(s_part, 1)
                    dve.wait_ge(s_part, 3 * g + 2)
                    dve.tensor_tensor(rest[:, 1, :, :], rest[:, 0, :, :], parts[:, b, :, 1, :],
                                      ALU.subtract).then_inc(s_rest, 1)
                    dve.wait_ge(s_rest, 2 * g + 2)
                    dve.tensor_copy(parts[:, b, :, 2, :], rest[:, 1, :, :]).then_inc(s_part, 1)

                def step(g, r):
                    for by, work in ((1, front), (0, difference), (-1, split)):
                        at, slot, there = group_at(g, r, by, LOTS)
                        if there:
                            work(at, slot)
                each_group(dve, step, lead=1, lag=1, groups=LOTS)
                dve.wait_ge(s_end, 1)
                dve.tensor_reduce(c.dtab[:, :].rearrange("p (w h) -> p w h", h=H),
                                  psd[:, 0:NW * SW].rearrange("p (w x) -> p w x", x=SW)[:, :, 0:3 * H].rearrange(
                                      "p w (j h) -> p w h j", j=3), AX_X, ALU.add).then_inc(s_tot, 1)
                dve.wait_ge(s_tot, 1)
                dve.tensor_scalar(c.dtab[:, :], c.dtab[:, :], 1e-20, None, ALU.max)

            @block.scalar
            def _(act):
                def turned(g, q):
                    act.wait_ge(s_tr, LG * g + q + 1)
                    wait_count(act, s_m, LG * g + q - 1)
                    act.activation(oht[:, q % 2].rearrange("p k n -> p (k n)"), pst[q % 2][:, 0:G * P],
                                   ACT.Copy).then_inc(s_oht, 1)

                def exp(g, r):
                    act.wait_ge(s_d, g + 1)
                    wait_count(act, s_part, 3 * (g - 1))
                    act.activation(ex[:, r % 2].rearrange("p k h -> p (k h)"),
                                   less[:, r % 2].rearrange("p k h -> p (k h)"), ACT.Exp).then_inc(s_ex, 1)

                def step(g, r):
                    here = group_at(g, r, 0, LOTS)[2]
                    before, slot, any_before = group_at(g, r, -1, LOTS)
                    for q in range(LG):
                        if here:
                            turned(g, q)
                        if q == 0 and any_before:
                            exp(before, slot)
                each_group(act, step, lag=1, groups=LOTS)

            @block.tensor
            def _(pe):
                pe.wait_ge(s_z, 1)
                for n in range(4):
                    pe.matmul(psd[:, n * 512:(n + 1) * 512], c.ones[:, :], zero[:, :], start=True, stop=False)

                def turn(g, r, q):
                    if q == 0:
                        pe.wait_ge(s_oh, g + 1)
                    wait_count(pe, s_oht, LG * g + q - 1)
                    for k in range(G):
                        ins = pe.transpose(pst[q % 2][:, k * P:(k + 1) * P], oh[:, r, q * G + k, :], c.identb[:, :])
                    ins.then_inc(s_tr, 1)

                def maxima(g, r, q, win):
                    pe.wait_ge(s_oht, LG * g + q + 1)
                    if q == 0:
                        wait_count(pe, s_d, g - 1)
                    for k in range(G):
                        at = (q * G + k) * 3 * H
                        ins = pe.matmul(psm[r % 2][:, at:at + 3 * H], oht[:, q % 2, k, :],
                                        mt[:, bass.ds(win[k], 1), :, :].rearrange("p w j h -> p (w j h)"),
                                        start=True, stop=True)
                    ins.then_inc(s_m, 1)

                def sums(g, r, q, win):
                    if q == 0:
                        pe.wait_ge(s_part, 3 * (g + 1))
                    for k in range(G):
                        at = q * G + k
                        ins = pe.matmul(psd[:, bass.ds(win[k] * SW, 3 * H)], oh[:, r, at, :],
                                        parts[:, r % 2, at].rearrange("p j h -> p (j h)"), start=False, stop=False,
                                        skip_group_check=True)
                    if q == LG - 1:
                        ins.then_inc(s_sum, 1)

                def step(g, r):
                    here = group_at(g, r, 0, LOTS)[2]
                    old, old_r, any_old = group_at(g, r, -2, LOTS)
                    if here:
                        turn(g, r, 0)
                    for q in range(LG):
                        if any_old:
                            if q % 2 == 0:
                                old_win = load_windows(pe, c, c.pe_regs, "src", old * LG + q, 2)
                            sums(old, old_r, q, old_win[q % 2 * G:(q % 2 + 1) * G])
                        if here:
                            if q < LG - 1:
                                turn(g, r, q + 1)
                            if q % 2 == 0:
                                win = load_windows(pe, c, c.more_pe_regs, "src", g * LG + q, 2)
                            maxima(g, r, q, win[q % 2 * G:(q % 2 + 1) * G])
                each_group(pe, step, lag=2, groups=LOTS)
                for n in range(4):
                    ins = pe.matmul(psd[:, n * 512:(n + 1) * 512], c.ones[:, :], zero[:, :], start=False, stop=True)
                ins.then_inc(s_end, 1)


def normalise_values(c):
    nc = c.nc
    (s_rec,) = semaphores(nc, c.sems, "sums_inverted")
    with nc.Block() as block:
        @block.vector
        def _(dve):
            dve.reciprocal(c.mtab[:, :], c.dtab[:, :]).then_inc(s_rec, 1)
            dve.wait_ge(s_rec, 1)
            dve.tensor_tensor(c.work[:, :].rearrange("p (j d) -> p j d", d=D),
                              c.vals[:, :].rearrange("p (j d) -> p j d", d=D),
                              c.mtab[:, :].unsqueeze(2).to_broadcast([P, NW * H, D]), ALU.mult)


def weigh(c):
    nc = c.nc
    names = "we_onehot we_turned we_onehot_t we_v we_index we_contrib we_lane"
    (s_oh, s_tr, s_oht, s_v, s_idx, s_con, s_lane) = semaphores(nc, c.sems, names)
    s_sent = semaphores(nc, c.stack, "we_sent0 we_sent1")
    s_turn, s_pad = semaphores(nc, c.sems, "we_scatter_turn we_padded")
    with ExitStack() as t:
        sb = lambda n, s, d: t.enter_context(nc.sbuf_tensor(n, s, d))
        oh = sb("we_oh", [P, 2, G, P], BF16)
        oht = sb("we_oht", [P, 2, G, P], BF16)
        idx = sb("we_idx", [P, 2, G], I32)
        con = sb("we_rows", [P, 2, G, CW], F32)
        pst = t.enter_context(nc.psum_tensor("ps_we_oht", [P, 1024], BF16))
        psv = [t.enter_context(nc.psum_tensor(f"ps_v{b}", [P, 512], F32)) for b in range(2)]
        with nc.Block() as block:
            @block.gpsimd
            def _(pool):
                def scatter(g, b):
                    pool.wait_ge(s_con, g + 1)
                    pool.wait_ge(s_lane, g + 1)
                    pool.wait_ge(s_idx, g + 1)
                    pool.sem_inc(s_turn, 1)
                    for k in range(G):
                        pool.indirect_dma_start(c.row_rows, bass.IndirectOffsetOnAxis(ap=idx[:, b, k:k + 1], axis=0),
                                                con[:, b, k, :], None, bounds_check=NTD * P - 1, oob_is_err=False
                                                ).then_inc(s_sent[b], 16)
                pool.wait_ge(s_pad, 1)
                with pool.Fori(0, PAIRS) as i:
                    for b in range(2):
                        scatter(2 * i + b, b)
                for b in range(2):
                    pool.wait_ge(s_sent[b], 16 * G * PAIRS)

            @block.vector
            def _(dve):
                dve.memset(con[:, :, :, F + 1:CW], 0.0).then_inc(s_pad, 1)

                def front(g, b):
                    wait_count(dve, s_tr, g - 1)
                    lane_onehot(dve, c, c.rec[:, bass.ds(g * G, G), C_SL], oh[:, b]).then_inc(s_oh, 1)

                def middle(g, b):
                    wait_count(dve, s_sent[b], 8 * G * (g - b))
                    rec = c.rec[:, bass.ds(g * G, G), :]
                    dve.tensor_copy(idx[:, b, :], rec[:, :, C_ROW]).then_inc(s_idx, 1)
                    dve.tensor_copy(con[:, b, :, F], rec[:, :, C_DL]).then_inc(s_lane, 1)
                    dve.wait_ge(s_v, g + 1)
                    ex = c.sc[:, bass.ds(g * G * H, G * H)].rearrange("p (k h) -> p k h", h=H)
                    dve.tensor_tensor(con[:, b, :, 0:F].rearrange("p k (h d) -> p k h d", d=D),
                                      psv[b][:, :].rearrange("p (k h d) -> p k h d", h=H, d=D),
                                      ex.unsqueeze(3).to_broadcast([P, G, H, D]), ALU.mult).then_inc(s_con, 1)

                def pair(i, last):
                    for b in range(2):
                        middle(2 * i + b, b)
                        if not last:
                            front(2 * i + 2 + b, b)
                for b in range(2):
                    front(b, b)
                pair(0, False)
                with dve.Fori(1, PAIRS - 1) as i:
                    pair(i, False)
                pair(PAIRS - 1, True)

            @block.scalar
            def _(act):
                def turned(g, b):
                    act.wait_ge(s_tr, g + 1)
                    wait_count(act, s_v, g - 1)
                    act.activation(oht[:, b].rearrange("p k n -> p (k n)"), pst[:, 0:G * P], ACT.Copy).then_inc(s_oht, 1)
                for b in range(2):
                    turned(b, b)
                with act.Fori(1, PAIRS) as i:
                    for b in range(2):
                        turned(2 * i + b, b)

            @block.tensor
            def _(pe):
                def values(g, b):
                    win = load_windows(pe, c, c.pe_regs, "src", g)
                    pe.wait_ge(s_oh, g + 1)
                    wait_count(pe, s_oht, g)
                    for k in range(G):
                        ins = pe.transpose(pst[:, k * P:(k + 1) * P], oh[:, b, k, :], c.identb[:, :])
                    ins.then_inc(s_tr, 1)
                    pe.wait_ge(s_oht, g + 1)
                    wait_count(pe, s_con, g - 1)
                    for k in range(G):
                        for j in range(3):
                            ins = pe.matmul(psv[b][:, k * F:(k + 1) * F], oht[:, b, k, :],
                                            c.tab[:, j, bass.ds(win[k] * F, F)], start=(j == 0), stop=(j == 2))
                    ins.then_inc(s_v, 1)
                for b in range(2):
                    values(b, b)
                with pe.Fori(1, PAIRS) as i:
                    for b in range(2):
                        values(2 * i + b, b)


def collect(c):
    nc = c.nc
    groups = NTD // G
    s_oh, s_mm, s_add = semaphores(nc, c.sems, "co_onehot co_sums co_added")
    s_in = semaphores(nc, c.sems, "co_in0 co_in1 co_in2 co_in3")
    with ExitStack() as t:
        sb = lambda n, s, d: t.enter_context(nc.sbuf_tensor(n, s, d))
        cin = sb("co_rows", [P, RING, G, CW], F32)
        oh = sb("co_oh", [P, 2, G, P], F32)
        ps = [t.enter_context(nc.psum_tensor(f"ps_co{b}", [P, 512], F32)) for b in range(2)]
        with nc.Block() as block:
            @block.sync
            def _(sp):
                def load(g, r):
                    wait_count(sp, s_mm, g - RING + 1)
                    sp.dma_start(cin[:, r].rearrange("p k c -> p (k c)"),
                                 c.row_dram[:, bass.ds(g * G * CW, G * CW)]).then_inc(s_in[r], 16)
                each_group(sp, load, groups=groups)

            @block.vector
            def _(dve):
                dve.memset(c.vals[:, :], 0.0).then_inc(s_add, 1)

                def one_hots(g, r):
                    dve.wait_ge(s_in[r], ring_count(g, r, 16))
                    wait_count(dve, s_mm, g - 1)
                    lane_onehot(dve, c, cin[:, r, :, F], oh[:, r % 2]).then_inc(s_oh, 1)

                def add(g, r):
                    dve.reg_load(c.dve_regs[0], c.win["dst"][0:1, bass.ds(g, 1)])
                    win = dve.snap(c.dve_regs[0], min_val=0, max_val=NW - 1)
                    dve.wait_ge(s_mm, g + 1)
                    dve.wait_ge(s_add, g + 1)
                    acc = c.vals[:, bass.ds(win * P, P)]
                    dve.tensor_tensor(acc, acc, ps[r % 2][:, 0:P], ALU.add).then_inc(s_add, 1)

                def step(g, r):
                    for by, work in ((1, one_hots), (-1, add)):
                        at, slot, there = group_at(g, r, by, groups)
                        if there:
                            work(at, slot)
                each_group(dve, step, lead=1, lag=1, groups=groups)

            @block.tensor
            def _(pe):
                def sums(g, r):
                    pe.wait_ge(s_oh, g + 1)
                    wait_count(pe, s_add, g)
                    for k in range(G):
                        ins = pe.matmul(ps[r % 2][:, 0:P], cin[:, r, k, 0:F], oh[:, r % 2, k, :],
                                        start=(k == 0), stop=(k == G - 1))
                    ins.then_inc(s_mm, 1)
                each_group(pe, sums, groups=groups)


BW = 4
BATCHES = NW // BW + 1
CH = 7


def each_batch(eng, step, lead=0, lag=0):
    for g in range(-lead, 2):
        step(g, g % 2)
    with eng.Fori(1, BATCHES // 2 - 1) as i:
        for b in range(2):
            step(2 * i + b, b)
    for g in range(BATCHES // 2 * 2 - 2, BATCHES + lag):
        step(g, g % 2)


def batch_size(g):
    return NW % BW if isinstance(g, int) and g == BATCHES - 1 else BW


def batch_rows(rows, g):
    m = batch_size(g)
    return rows[bass.ds(g * BW * P, m * P), :].rearrange("(w p) f -> p w f", p=P)


def at_batches(g, b, works):
    for by, work in works:
        if not isinstance(g, int) or 0 <= g + by < BATCHES:
            work(g + by, (b + by) % 2, batch_size(g + by))


def batch_count(g, b):
    return (g - b + 2) * 8


def row_vector(v, n):
    return v.rearrange("(o n) -> o n", o=1).to_broadcast([P, n])


def add_projected(c, a):
    nc = c.nc
    s_w, s_set, s_turn, s_acc, s_o, s_res = semaphores(nc, c.sems, "ap_in ap_set ap_turn ap_acc ap_o ap_res")
    s_x = semaphores(nc, c.sems, "ap_x_in0 ap_x_in1")
    with ExitStack() as t:
        sb = lambda n, s, d: t.enter_context(nc.sbuf_tensor(n, s, d))
        wo = sb("w_o", [P, F], F32)
        bo = sb("b_o", [1, F], F32)
        one = sb("ap_one", [1, P], F32)
        accs = sb("ap_accs", [P, 2, BW * P], F32)
        xr = sb("ap_xr", [P, 2, BW, F], F32)
        pso = [t.enter_context(nc.psum_tensor(f"ps_o{b}", [P, 512], F32)) for b in range(2)]
        with nc.Block() as block:
            @block.gpsimd
            def _(pool):
                pool.memset(one[:, :], 1.0).then_inc(s_set, 1)
                pool.memset(xr[:, :, :, :], 0.0).then_inc(s_set, 1)

            @block.sync
            def _(sp):
                sp.dma_start(wo[:, :], a["WoT"]).then_inc(s_w, 16)
                sp.dma_start(bo[:, :], a["bo"].rearrange("(o n) -> o n", o=1)).then_inc(s_w, 16)
                sp.wait_ge(s_set, 2)

                def load(g, b, m):
                    wait_count(sp, s_res, g - 1)
                    if m == BW:
                        sp.dma_start(xr[:, b, :, :], batch_rows(a["x"], g)).then_inc(s_x[b], 16)
                    else:
                        sp.dma_start(xr[0:LAST, b, 0, :], a["x"][N - LAST:N, :]).then_inc(s_x[b], 16)
                each_batch(sp, lambda g, b: load(g, b, batch_size(g)))

            @block.scalar
            def _(act):
                def sums_in(g, b):
                    n = batch_size(g) * P
                    wait_count(act, s_o, g - 1)
                    act.sem_inc(s_turn, 1)
                    act.activation(accs[:, b, 0:n], c.vals[:, bass.ds(g * BW * P, n)], ACT.Copy).then_inc(s_acc, 1)
                each_batch(act, sums_in)

            @block.tensor
            def _(pe):
                pe.wait_ge(s_w, 32)
                pe.wait_ge(s_set, 1)

                def project(g, b):
                    m = batch_size(g)
                    pe.wait_ge(s_acc, g + 1)
                    wait_count(pe, s_res, g - 1)
                    bias_rows(pe, pso[b], one, bo, m)
                    for k in range(m):
                        ins = pe.matmul(pso[b][:, k * F:(k + 1) * F], accs[:, b, k * P:(k + 1) * P], wo[:, :],
                                        start=False, stop=(k == m - 1))
                    ins.then_inc(s_o, 1)
                each_batch(pe, project)

            @block.vector
            def _(dve):
                def add(g, b):
                    m = batch_size(g)
                    dve.wait_ge(s_x[b], batch_count(g, b))
                    dve.wait_ge(s_o, g + 1)
                    dve.tensor_tensor(c.work[:, bass.ds(g * BW * F, m * F)], pso[b][:, 0:m * F],
                                      xr[:, b, 0:m, :].rearrange("p w f -> p (w f)"), ALU.add).then_inc(s_res, 1)
                each_batch(dve, add)


def bias_rows(pe, ps, one, bias, m):
    pe.matmul(ps[:, 0:m * F].rearrange("p (w f) -> p w f", f=F), one[:, :],
              bias[:, :].unsqueeze(1).to_broadcast([1, m, F]), start=True, stop=False)


def normalise_table(c, name, rows, last):
    nc = c.nc
    (s_eps, s_sum, s_mean, s_cen, s_sq, s_var, s_std, s_rstd, s_norm, s_out) = semaphores(
        nc, c.sems, " ".join(f"{name}_{n}" for n in "eps sum mean centred square var std rstd normed out".split()))
    with ExitStack() as t:
        sb = lambda n, s, d: t.enter_context(nc.sbuf_tensor(name + n, s, d))
        sq = sb("_squares", [P, 2, CH, F], F32)
        total = sb("_totals", [P, NW], F32)
        mean = sb("_means", [P, NW], F32)
        var = sb("_vars", [P, NW], F32)
        std = sb("_stds", [P, NW], F32)
        rstd = sb("_rstds", [P, NW], F32)
        eps = sb("_epss", [P, 1], F32)
        table = c.work[:, :].rearrange("p (w f) -> p w f", f=F)
        with nc.Block() as block:
            @block.gpsimd
            def _(pool):
                pool.memset(eps[:, :], EPS).then_inc(s_eps, 1)

            @block.vector
            def _(dve):
                def subtotal(j, ws):
                    dve.tensor_reduce(total[:, ws], table[:, ws, :], AX_X, ALU.add).then_inc(s_sum, 1)

                def means(j, ws):
                    dve.wait_ge(s_sum, j + 1)
                    dve.tensor_scalar(mean[:, ws], total[:, ws], 1.0 / F, None, ALU.mult).then_inc(s_mean, 1)

                def centre(j, ws):
                    dve.wait_ge(s_mean, j + 1)
                    dve.tensor_tensor(table[:, ws, :], table[:, ws, :],
                                      mean[:, ws].unsqueeze(2).to_broadcast([P, CH, F]), ALU.subtract).then_inc(s_cen, 1)

                def variance(j, ws):
                    dve.wait_ge(s_sq, j + 1)
                    dve.tensor_reduce(var[:, ws], sq[:, j % 2], AX_X, ALU.add).then_inc(s_var, 1)

                def inverse(j, ws):
                    dve.wait_ge(s_std, j + 1)
                    dve.reciprocal(rstd[:, ws], std[:, ws]).then_inc(s_rstd, 1)

                def scale(j, ws):
                    dve.wait_ge(s_rstd, j + 1)
                    dve.tensor_tensor(table[:, ws, :], table[:, ws, :],
                                      rstd[:, ws].unsqueeze(2).to_broadcast([P, CH, F]), ALU.mult).then_inc(s_norm, 1)
                for j in range(NW // CH + 2):
                    for by, work in ((0, subtotal), (-2, inverse), (0, means), (-2, scale), (0, centre), (-1, variance)):
                        if 0 <= j + by < NW // CH:
                            work(j + by, slice((j + by) * CH, (j + by + 1) * CH))

            @block.scalar
            def _(act):
                act.wait_ge(s_eps, 1)

                def squares(j):
                    act.wait_ge(s_cen, j + 1)
                    wait_count(act, s_var, j - 1)
                    act.activation(sq[:, j % 2], table[:, j * CH:(j + 1) * CH, :], ACT.Square).then_inc(s_sq, 1)

                def deviations(j):
                    ws = slice(j * CH, (j + 1) * CH)
                    act.wait_ge(s_var, j + 1)
                    act.activation(std[:, ws], var[:, ws], ACT.Sqrt, bias=eps[:, 0:1], scale=1.0 / F).then_inc(s_std, 1)
                for j in range(NW // CH + 1):
                    if j < NW // CH:
                        squares(j)
                    if j > 0:
                        deviations(j - 1)

            @block.sync
            def _(sp):
                stores = 0
                for j in range(NW // CH):
                    sp.wait_ge(s_norm, j + 1)
                    full = CH if j < NW // CH - 1 or last == P else CH - 1
                    sp.dma_start(rows[j * CH * P:(j * CH + full) * P, :].rearrange("(w p) f -> p w f", p=P),
                                 table[:, j * CH:j * CH + full, :]).then_inc(s_out, 16)
                    stores += 1
                if last < P:
                    sp.dma_start(rows[(NW - 1) * P:(NW - 1) * P + last, :],
                                 c.work[0:last, (NW - 1) * F:NW * F]).then_inc(s_out, 16)
                    stores += 1
                sp.wait_ge(s_out, 16 * stores)


def edge_inputs(c, a):
    nc = c.nc
    s_w, s_set, s_turn, s_dturn, s_xs, s_tr, s_x1t, s_x1tab, s_ab, s_a, s_b = semaphores(
        nc, c.sems, "ei_in ei_set ei_turn ei_dve_turn ei_rows ei_turned ei_x1t ei_x1_table ei_ab ei_a ei_b")
    s_bo = semaphores(nc, c.sems, "ei_b_out0 ei_b_out1")
    with ExitStack() as t:
        sb = lambda n, s, d: t.enter_context(nc.sbuf_tensor(n, s, d))
        w1 = sb("w_1", [P, 2 * F], F32)
        b1 = sb("b_1", [1, F], F32)
        one = sb("ei_one", [1, P], F32)
        xs = sb("ei_xs", [P, 2, BW * F], F32)
        x1t = sb("ei_x1ts", [P, 2, BW * P], F32)
        bt = sb("ei_bts", [P, 2, BW, F], F32)
        psx = [t.enter_context(nc.psum_tensor(f"ps_x{b}", [P, 512], F32)) for b in range(2)]
        psa = [t.enter_context(nc.psum_tensor(f"ps_a{b}", [P, 512], F32)) for b in range(2)]
        psb = [t.enter_context(nc.psum_tensor(f"ps_b{b}", [P, 512], F32)) for b in range(2)]
        with nc.Block() as block:
            @block.gpsimd
            def _(pool):
                pool.memset(one[:, :], 1.0).then_inc(s_set, 1)

            @block.sync
            def _(sp):
                sp.dma_start(w1[:, 0:F], a["eW1"][0:F, :]).then_inc(s_w, 16)
                sp.dma_start(w1[:, F:2 * F], a["eW1"][F:2 * F, :]).then_inc(s_w, 16)
                sp.dma_start(b1[:, :], a["eb1"].rearrange("(o n) -> o n", o=1)).then_inc(s_w, 16)

                def store(g, b):
                    sp.wait_ge(s_b, g + 1)
                    sp.dma_start(batch_rows(c.b_dram, g), bt[:, b, 0:batch_size(g), :]).then_inc(s_bo[b], 16)
                each_batch(sp, store)
                for b in range(2):
                    sp.wait_ge(s_bo[b], 16 * len(range(b, BATCHES, 2)))

            @block.scalar
            def _(act):
                def rows_in(g, b, m):
                    wait_count(act, s_tr, g - 1)
                    act.sem_inc(s_turn, 1)
                    act.activation(xs[:, b, 0:m * F], c.work[:, bass.ds(g * BW * F, m * F)], ACT.Copy).then_inc(s_xs, 1)

                def turned(g, b, m):
                    act.wait_ge(s_tr, g + 1)
                    wait_count(act, s_ab, g - 1)
                    wait_count(act, s_x1tab, g - 1)
                    act.activation(x1t[:, b, 0:m * P], psx[b][:, 0:m * P], ACT.Copy).then_inc(s_x1t, 1)

                def destination_half(g, b, m):
                    act.wait_ge(s_ab, g + 1)
                    wait_count(act, s_bo[b], batch_count(g, b) - 16)
                    act.activation(bt[:, b, 0:m, :].rearrange("p w f -> p (w f)"), psb[b][:, 0:m * F],
                                   ACT.Copy).then_inc(s_b, 1)
                each_batch(act, lambda g, b: at_batches(g, b, ((1, rows_in), (0, turned), (-1, destination_half))),
                           lead=1, lag=1)

            @block.tensor
            def _(pe):
                pe.wait_ge(s_w, 48)
                pe.wait_ge(s_set, 1)

                def turn(g, b, m):
                    pe.wait_ge(s_xs, g + 1)
                    wait_count(pe, s_x1t, g - 1)
                    for k in range(m):
                        ins = pe.transpose(psx[b][:, k * P:(k + 1) * P], xs[:, b, k * F:(k + 1) * F], c.ident[:, :])
                    ins.then_inc(s_tr, 1)

                def halves(g, b, m):
                    pe.wait_ge(s_x1t, g + 1)
                    wait_count(pe, s_a, g - 1)
                    wait_count(pe, s_b, g - 1)
                    bias_rows(pe, psa[b], one, b1, m)
                    for k in range(m):
                        x = x1t[:, b, k * P:(k + 1) * P]
                        pe.matmul(psa[b][:, k * F:(k + 1) * F], x, w1[:, 0:F], start=False, stop=(k == m - 1))
                        ins = pe.matmul(psb[b][:, k * F:(k + 1) * F], x, w1[:, F:2 * F], start=True, stop=True)
                    ins.then_inc(s_ab, 1)
                each_batch(pe, lambda g, b: at_batches(g, b, ((0, turn), (-1, halves))), lag=1)

            @block.vector
            def _(dve):
                def table(g, b, m):
                    dve.wait_ge(s_x1t, g + 1)
                    dve.sem_inc(s_dturn, 1)
                    dve.tensor_copy(c.x1t[:, bass.ds(g * BW * P, m * P)], x1t[:, b, 0:m * P]).then_inc(s_x1tab, 1)

                def source_half(g, b, m):
                    dve.wait_ge(s_ab, g + 1)
                    dve.sem_inc(s_dturn, 1)
                    dve.tensor_copy(c.work[:, bass.ds(g * BW * F, m * F)], psa[b][:, 0:m * F]).then_inc(s_a, 1)
                each_batch(dve, lambda g, b: at_batches(g, b, ((0, table), (-1, source_half))), lag=1)


def attribute_parts(c, a, parts, weights):
    nc = c.nc
    s_w, s_part, s_rest, s_wp, s_sel, s_z = semaphores(nc, c.sems, "ap_w ap_part ap_rest ap_wp ap_sel ap_zeroed")
    K = 9 * 2 * G
    with ExitStack() as t:
        sb = lambda n, s, d: t.enter_context(nc.sbuf_tensor(n, s, d))
        rest = sb("ap_rests", [P, NT, 2], F32)
        wr = sb("ap_wr", [P, F], F32)
        wp = sb("ap_wps", [P, 3, F], BF16)
        pair = sb("ap_pair", [P, K // 2], F32)
        sel = sb("ap_sels", [P, 3, G], F32)
        with nc.Block() as block:
            @block.gpsimd
            def _(pool):
                pool.memset(wr[:, :], 0.0).then_inc(s_z, 1)

            @block.sync
            def _(sp):
                sp.wait_ge(s_z, 1)
                for n in range(K // 2):
                    sp.dma_start(wr[2 * n:2 * n + 2, :], a["eW1"][2 * F:2 * F + 2, :]).then_inc(s_w, 16)

            @block.vector
            def _(dve):
                view = lambda i: parts.rearrange("p (g i x) -> p g i x", i=3, x=2 * G)[:, :, i, :]
                flat = rest[:, :, :].rearrange("p (g k) j -> p g (k j)", k=G)
                attrs = c.rec[:, :, C_ATTR:C_ATTR + 2]
                dve.tensor_copy(rest[:, :, :], attrs).then_inc(s_rest, 1)
                dve.wait_ge(s_rest, 1)
                for i in range(3):
                    dve.tensor_copy(view(i), flat).then_inc(s_part, 1)
                    dve.wait_ge(s_part, i + 1)
                    if i < 2:
                        dve.tensor_tensor(flat, flat, view(i), ALU.subtract).then_inc(s_rest, 1)
                        dve.wait_ge(s_rest, i + 2)
                dve.wait_ge(s_w, 16 * (K // 2))
                for i in range(3):
                    dve.tensor_copy(wp[:, i, :], wr[:, :]).then_inc(s_wp, 1)
                    dve.wait_ge(s_wp, 2 * i + 1)
                    dve.tensor_tensor(wr[:, :], wr[:, :], wp[:, i, :], ALU.subtract).then_inc(s_wp, 1)
                    dve.wait_ge(s_wp, 2 * i + 2)
                dve.tensor_reduce(pair[:, :], c.ident[:, 0:K].rearrange("p (n a) -> p n a", a=2), AX_X,
                                  ALU.add).then_inc(s_sel, 1)
                dve.wait_ge(s_sel, 1)
                dve.tensor_reduce(sel[:, :, :], pair[:, :].rearrange("p (j i k) -> p j k i", j=3, i=3), AX_X,
                                  ALU.add).then_inc(s_sel, 1)
                dve.wait_ge(s_sel, 2)
                n = 2
                for k in range(G):
                    dve.tensor_scalar(weights[:, k, :], wp[:, 0, :], sel[:, 0, k:k + 1], None, ALU.mult).then_inc(s_sel, 1)
                    n += 1
                    for i in (1, 2):
                        dve.wait_ge(s_sel, n)
                        dve.scalar_tensor_tensor(out=weights[:, k, :], in0=wp[:, i, :], scalar=sel[:, i, k:k + 1],
                                                 in1=weights[:, k, :], op0=ALU.mult, op1=ALU.add).then_inc(s_sel, 1)
                        n += 1


def edges(c, a):
    nc = c.nc
    names = ("ed_weights ed_padded ed_onehot ed_onehot_f ed_turned ed_onehot_t ed_index ed_attr ed_attr_turned "
             "ed_attr_t ed_z ed_h ed_o ed_ob ed_f ed_sums ed_added")
    (s_w, s_pad, s_oh, s_ohf, s_tr, s_oht, s_idx, s_at, s_atr, s_att, s_z, s_h, s_o, s_ob, s_f, s_sum,
     s_add) = semaphores(nc, c.sems, names)
    s_b = semaphores(nc, c.stack, "ed_b_in0 ed_b_in1 ed_b_in2 ed_b_in3")
    (s_turn,) = semaphores(nc, c.sems, "ed_gather_turn")
    K = 9 * 2 * G
    with ExitStack() as t:
        sb = lambda n, s, d: t.enter_context(nc.sbuf_tensor(n, s, d))
        parts = c.work[:, 0:NT * 3].bitcast(BF16)
        wc = sb("w_attr", [P, G, F], BF16)
        attribute_parts(c, a, parts, wc)
        w2 = sb("w_2", [P, F], F32)
        b2 = sb("b_2", [P, F], F32)
        oh = sb("ed_oh", [P, RING, G, P], BF16)
        ohf = sb("ed_ohf", [P, 2, G, P], F32)
        oht = sb("ed_oht", [P, 2, G, P], BF16)
        idx = sb("ed_idx", [P, RING, G], I32)
        bg = sb("ed_bg", [P, RING, G, F], F32)
        attr = sb("ed_attrs", [P, RING, P], BF16)
        att = sb("ed_atts", [P, 2, P], BF16)
        h = sb("ed_hs", [P, 2, G * P], F32)
        ob = sb("ed_obs", [P, 2, G * F], F32)
        ef = sb("ed_efs", [P, 2, G, F], F32)
        pst = t.enter_context(nc.psum_tensor("ps_ed_oht", [P, 1024], BF16))
        psa = t.enter_context(nc.psum_tensor("ps_ed_att", [P, 1024], BF16))
        psz = [t.enter_context(nc.psum_tensor(f"ps_z{b}", [P, 512], F32)) for b in range(2)]
        pso = [t.enter_context(nc.psum_tensor(f"ps_ed_o{b}", [P, 512], F32)) for b in range(2)]
        pss = [t.enter_context(nc.psum_tensor(f"ps_ed_s{b}", [P, 512], F32)) for b in range(2)]
        with nc.Block() as block:
            @block.sync
            def _(sp):
                sp.dma_start(w2[:, :], a["eW2"]).then_inc(s_w, 16)
                sp.dma_start(b2[:, :], row_vector(a["eb2"], F)).then_inc(s_w, 16)

            @block.gpsimd
            def _(pool):
                pool.memset(attr[:, :, :], 0.0).then_inc(s_pad, 1)

                def gather(g, r):
                    pool.wait_ge(s_idx, g + 1)
                    wait_count(pool, s_z, g - RING + 1)
                    pool.sem_inc(s_turn, 1)
                    for k in range(G):
                        pool.indirect_dma_start(bg[:, r, k, :], None, c.b_dram[:, :],
                                                bass.IndirectOffsetOnAxis(ap=idx[:, r, k:k + 1], axis=0)
                                                ).then_inc(s_b[r], 16)
                each_group(pool, gather)

            @block.vector
            def _(dve):
                dve.wait_ge(s_pad, 1)
                dve.wait_ge(s_w, 32)
                dve.memset(c.vals[:, :], 0.0).then_inc(s_add, 1)

                def front(g, r):
                    wait_count(dve, s_z, g - RING + 1)
                    wait_count(dve, s_ohf, g - RING + 1)
                    rec = c.rec[:, bass.ds(g * G, G), :]
                    dve.tensor_copy(idx[:, r, :], rec[:, :, C_DST]).then_inc(s_idx, 1)
                    lane_onehot(dve, c, rec[:, :, C_SL], oh[:, r]).then_inc(s_oh, 1)
                    dve.tensor_copy(attr[:, r, 0:K].rearrange("p (j x) -> p j x", j=3),
                                    parts[:, bass.ds(g * 6 * G, 6 * G)].unsqueeze(1).to_broadcast([P, 3, 6 * G])
                                    ).then_inc(s_at, 1)

                def middle(g, r):
                    b = r % 2
                    dve.wait_ge(s_oh, g + 1)
                    wait_count(dve, s_sum, g - 1)
                    dve.tensor_copy(ohf[:, b].rearrange("p k n -> p (k n)"),
                                    oh[:, r].rearrange("p k n -> p (k n)")).then_inc(s_ohf, 1)
                    dve.wait_ge(s_o, g + 1)
                    wait_count(dve, s_f, g - 1)
                    dve.tensor_tensor(ob[:, b, :].rearrange("p (k f) -> p k f", k=G),
                                      pso[b][:, :].rearrange("p (k f) -> p k f", k=G),
                                      b2[:, :].unsqueeze(1).to_broadcast([P, G, F]), ALU.add).then_inc(s_ob, 1)

                def back(g, r):
                    win = load_windows(dve, c, c.dve_regs, "src", g)
                    dve.wait_ge(s_sum, g + 1)
                    for k in range(G):
                        dve.wait_ge(s_add, G * g + k + 1)
                        acc = c.vals[:, bass.ds(win[k] * P, P)]
                        dve.tensor_tensor(acc, acc, pss[r % 2][:, k * P:(k + 1) * P], ALU.add).then_inc(s_add, 1)

                def step(g, r):
                    for by, work in ((2, front), (-1, middle), (-3, back)):
                        at, slot, there = group_at(g, r, by)
                        if there:
                            work(at, slot)
                each_group(dve, step, lead=2, lag=3)

            @block.scalar
            def _(act):
                def turned(g, r):
                    act.wait_ge(s_tr, g + 1)
                    wait_count(act, s_z, g - 1)
                    act.activation(oht[:, r % 2].rearrange("p k n -> p (k n)"), pst[:, 0:G * P],
                                   ACT.Copy).then_inc(s_oht, 1)
                    act.wait_ge(s_atr, g + 1)
                    act.activation(att[:, r % 2, :], psa[:, 0:P], ACT.Copy).then_inc(s_att, 1)

                def hidden(g, r):
                    act.wait_ge(s_z, g + 1)
                    wait_count(act, s_o, g - 1)
                    act.activation(h[:, r % 2, :], psz[r % 2][:, :], ACT.Silu).then_inc(s_h, 1)

                def feature(g, r):
                    act.wait_ge(s_ob, g + 1)
                    wait_count(act, s_sum, g - 1)
                    act.activation(ef[:, r % 2].rearrange("p k f -> p (k f)"), ob[:, r % 2, :],
                                   ACT.Silu).then_inc(s_f, 1)

                def step(g, r):
                    for by, work in ((1, turned), (0, hidden), (-1, feature)):
                        at, slot, there = group_at(g, r, by)
                        if there:
                            work(at, slot)
                each_group(act, step, lead=1, lag=1)

            @block.tensor
            def _(pe):
                pe.wait_ge(s_w, 32)

                def turn(g, r):
                    pe.wait_ge(s_oh, g + 1)
                    wait_count(pe, s_oht, g)
                    for k in range(G):
                        ins = pe.transpose(pst[:, k * P:(k + 1) * P], oh[:, r, k, :], c.identb[:, :])
                    ins.then_inc(s_tr, 1)
                    pe.wait_ge(s_at, g + 1)
                    wait_count(pe, s_att, g)
                    pe.transpose(psa[:, 0:P], attr[:, r, :], c.identb[:, :]).then_inc(s_atr, 1)

                def inputs(g, r):
                    b = r % 2
                    win = load_windows(pe, c, c.pe_regs, "src", g)
                    pe.wait_ge(s_oht, g + 1)
                    pe.wait_ge(s_att, g + 1)
                    wait_count(pe, s_h, g - 1)
                    pe.wait_ge(s_b[r], ring_count(g, r, 16 * G))
                    for k in range(G):
                        z = psz[b][:, k * P:(k + 1) * P]
                        pe.matmul(z, wc[:, k, :], att[:, b, :], start=True, stop=False)
                        for j in range(3):
                            pe.matmul(z, c.tab[:, j, bass.ds(win[k] * F, F)], oht[:, b, k, :],
                                      start=False, stop=False)
                        ins = pe.matmul(z, bg[:, r, k, :], c.ident[:, :], start=False, stop=True)
                    ins.then_inc(s_z, 1)

                def second(g, r):
                    b = r % 2
                    pe.wait_ge(s_h, g + 1)
                    wait_count(pe, s_ob, g - 1)
                    for k in range(G):
                        ins = pe.matmul(pso[b][:, k * F:(k + 1) * F], h[:, b, k * P:(k + 1) * P], w2[:, :],
                                        start=True, stop=True)
                    ins.then_inc(s_o, 1)

                def sums(g, r):
                    b = r % 2
                    pe.wait_ge(s_f, g + 1)
                    pe.wait_ge(s_ohf, g + 1)
                    wait_count(pe, s_add, G * (g - 1) + 1)
                    for k in range(G):
                        ins = pe.matmul(pss[b][:, k * P:(k + 1) * P], ef[:, b, k, :], ohf[:, b, k, :],
                                        start=True, stop=True)
                    ins.then_inc(s_sum, 1)

                def step(g, r):
                    for by, work in ((1, turn), (0, inputs), (-1, second), (-2, sums)):
                        at, slot, there = group_at(g, r, by)
                        if there:
                            work(at, slot)
                each_group(pe, step, lead=1, lag=2)


def node_mlp(c, a):
    nc = c.nc
    s_w, s_set, s_pre, s_hid, s_o, s_res = semaphores(nc, c.sems, "nm_in nm_set nm_pre nm_hid nm_o nm_res")
    s_x = semaphores(nc, c.sems, "nm_x1_in0 nm_x1_in1")
    with ExitStack() as t:
        sb = lambda n, s, d: t.enter_context(nc.sbuf_tensor(n, s, d))
        wx = sb("w_nx", [P, F], F32)
        wa = sb("w_na", [P, F], F32)
        w2 = sb("w_n2", [P, F], F32)
        b1 = sb("b_n1", [P, 1], F32)
        b2 = sb("b_n2", [1, F], F32)
        one = sb("nm_one", [1, P], F32)
        xr = sb("nm_xr", [P, 2, BW, F], F32)
        hid = sb("nm_hids", [P, 2, BW * P], F32)
        psh = [t.enter_context(nc.psum_tensor(f"ps_h{b}", [P, 512], F32)) for b in range(2)]
        pso = [t.enter_context(nc.psum_tensor(f"ps_nm_o{b}", [P, 512], F32)) for b in range(2)]
        with nc.Block() as block:
            @block.gpsimd
            def _(pool):
                pool.memset(one[:, :], 1.0).then_inc(s_set, 1)

            @block.sync
            def _(sp):
                sp.dma_start(wx[:, :], a["nW1"][0:F, :]).then_inc(s_w, 16)
                sp.dma_start(wa[:, :], a["nW1"][F:2 * F, :]).then_inc(s_w, 16)
                sp.dma_start(w2[:, :], a["nW2"]).then_inc(s_w, 16)
                sp.dma_start(b1[:, :], a["nb1"].rearrange("(n o) -> n o", o=1)).then_inc(s_w, 16)
                sp.dma_start(b2[:, :], a["nb2"].rearrange("(o n) -> o n", o=1)).then_inc(s_w, 16)

                def load(g, b):
                    wait_count(sp, s_res, g - 1)
                    sp.dma_start(xr[:, b, 0:batch_size(g), :], batch_rows(c.x1_dram, g)).then_inc(s_x[b], 16)
                each_batch(sp, load)

            @block.tensor
            def _(pe):
                pe.wait_ge(s_w, 80)
                pe.wait_ge(s_set, 1)

                def first(g, b, m):
                    wait_count(pe, s_hid, g - 1)
                    cols = bass.ds(g * BW * P, m * P)
                    pe.matmul(psh[b][:, 0:m * P], wx[:, :], c.x1t[:, cols], start=True, stop=False)
                    pe.matmul(psh[b][:, 0:m * P], wa[:, :], c.vals[:, cols], start=False, stop=True).then_inc(s_pre, 1)

                def second(g, b, m):
                    pe.wait_ge(s_hid, g + 1)
                    wait_count(pe, s_res, g - 1)
                    bias_rows(pe, pso[b], one, b2, m)
                    for k in range(m):
                        ins = pe.matmul(pso[b][:, k * F:(k + 1) * F], hid[:, b, k * P:(k + 1) * P], w2[:, :],
                                        start=False, stop=(k == m - 1))
                    ins.then_inc(s_o, 1)
                each_batch(pe, lambda g, b: at_batches(g, b, ((1, first), (0, second))), lead=1)

            @block.scalar
            def _(act):
                act.wait_ge(s_w, 80)

                def hidden(g, b):
                    n = batch_size(g) * P
                    act.wait_ge(s_pre, g + 1)
                    wait_count(act, s_o, g - 1)
                    act.activation(hid[:, b, 0:n], psh[b][:, 0:n], ACT.Silu, bias=b1[:, 0:1]).then_inc(s_hid, 1)
                each_batch(act, hidden)

            @block.vector
            def _(dve):
                def add(g, b):
                    m = batch_size(g)
                    dve.wait_ge(s_x[b], batch_count(g, b))
                    dve.wait_ge(s_o, g + 1)
                    dve.tensor_tensor(c.work[:, bass.ds(g * BW * F, m * F)], pso[b][:, 0:m * F],
                                      xr[:, b, 0:m, :].rearrange("p w f -> p (w f)"), ALU.add).then_inc(s_res, 1)
                each_batch(dve, add)


def clear_semaphores(c, sems):
    nc = c.nc
    with nc.Block() as block:
        @block.gpsimd
        def _(pool):
            for s in sems:
                pool.sem_clear(s)


def program(nc, a, out):
    with ExitStack() as stack:
        c = Ctx()
        c.nc, c.stack = nc, stack
        dram = lambda n, s: nc.dram_tensor(n, s, F32, kind="Internal").ap()
        c.k_dram = dram("k_rows_dram", [NP, F])
        c.b_dram = dram("b_rows_dram", [NP, F])
        c.x1_dram = dram("x1_rows_dram", [NP, F])
        c.rec_dram = dram("records_dram", [P, NT * R])
        c.rec_rows = c.rec_dram.rearrange("p (t r) -> (p t) r", r=R)
        c.row_dram = dram("contributions_dram", [P, NTD * CW])
        c.row_rows = c.row_dram.rearrange("p (t r) -> (p t) r", r=CW)
        c.pe_regs = [nc.tensor.alloc_register(f"pe_window{k}") for k in range(2 * G)]
        c.more_pe_regs = [nc.tensor.alloc_register(f"pe_window_b{k}") for k in range(2 * G)]
        c.dve_regs = [nc.vector.alloc_register(f"dve_window{k}") for k in range(2 * G)]
        sb = lambda st, n, s, d: st.enter_context(nc.sbuf_tensor(n, s, d))
        with Epoch() as c.sems:
            constants(c)
            c.work = sb(stack, "work", [P, NP], F32)
            c.vals = sb(stack, "vals", [P, NP], F32)
            c.tab = sb(stack, "tab", [P, 3, NP], BF16)
            with ExitStack() as st:
                e = Ctx()
                e.ids = {s: sb(st, "ids_" + s, [P, ET], I32) for s in SIDES}
                e.hi = {s: sb(st, "win_of_" + s, [P, ET], F32) for s in SIDES}
                e.run = {s: sb(st, "run_" + s, [P, 2, NW], F32) for s in SIDES}
                e.rec = sb(st, "record", [P, ET, R], F32)
                c.rfill = sb(st, "rfill", [P, RF, R], F32)
                c.fill = sb(st, "cfill", [P, CF, CW], F32)
                with ExitStack() as st2:
                    e.tmpi = sb(st2, "tmp_int", [P, 2, ET], I32)
                    e.attr = sb(st2, "attr_in", [P, ET * 2], F32)
                    e.mask = sb(st2, "mask_in", [P, ET * H], F32)
                    load_edges(c, a, e)
                count_windows(c, e)
                place_and_project(c, e, a)
            c.rec = sb(stack, "records", [P, NT, R], F32)
            with ExitStack() as st:
                c.sc = sb(st, "scores", [P, NT * H], F32)
                load_records(c)
                score(c)
                exps(c)
                normalise_values(c)
                split_table(c, "values")
                weigh(c)
            clear_semaphores(c, c.sems.taken)
        with ExitStack() as c.sems:
            collect(c)
            c.x1t = sb(stack, "x1t", [P, NP], F32)
            add_projected(c, a)
            normalise_table(c, "norm1", c.x1_dram, P)
            edge_inputs(c, a)
            split_table(c, "sources")
            edges(c, a)
            node_mlp(c, a)
            normalise_table(c, "norm2", out, LAST)


def kernel(**inputs):
    import numpy as np
    import concourse.bacc as bacc
    from concourse.bass_utils import run_bass_kernel_spmd

    given = {k.split("gnn_")[-1]: np.asarray(v) for k, v in inputs.items()}
    given["xT"] = given["x"].T
    for w in ("Wq", "Wk", "Wv", "Wo"):
        given[w + "T"] = given.pop(w).T
    nc = bacc.Bacc("TRN2", target_bir_lowering=False, num_devices=1)
    arrays, a = {}, {}
    for name, v in given.items():
        v = np.ascontiguousarray(v)
        arrays[f"in_{name}_dram"] = v
        a[name] = nc.dram_tensor(f"in_{name}_dram", v.shape, mybir.dt.from_np(v.dtype), kind="ExternalInput").ap()
    out = nc.dram_tensor("out_dram", (N, F), F32, kind="ExternalOutput").ap()
    program(nc, a, out)
    r = run_bass_kernel_spmd(nc, [arrays], core_ids=[0])
    return r.results[0]["out_dram"]
```
